# Optimizing a Trainium2 kernel written in Bass

```python
import numpy as np
import jax
import jax.numpy as jnp

def _softmax(x, axis=-1):
    return jax.nn.softmax(x, axis=axis)

def _gelu(x):
    return jax.nn.gelu(x, approximate=True)

def _silu(x):
    return jax.nn.silu(x)

def _sigmoid(x):
    return jax.nn.sigmoid(x)

def _layernorm(x, axis=-1, eps=1e-05):
    m = jnp.mean(x, axis=axis, keepdims=True)
    v = jnp.var(x, axis=axis, keepdims=True)
    return (x - m) / jnp.sqrt(v + eps)

def _scatter_add(tgt, idx, src, axis=0):
    return tgt.at[idx].add(src)

def _segment_sum(src, seg, n):
    return jax.ops.segment_sum(src, seg, n)
kernel_name = 'mk_xattn_ffn_d1_seqx_r2_444e0b'

def setup_inputs(seed: int=0):
    np.random.seed(seed)
    _w = jnp.asarray

    def _rec_inputs():
        import jax
        import jax.numpy as jnp
        _rk = jax.random.key(seed)
        x = -0.0003929 + 0.9999 * jax.random.normal(jax.random.fold_in(_rk, 1), (4, 2048, 512), jnp.float32)
        _lenS = 2048 - jax.random.randint(jax.random.fold_in(_rk, 7), (4,), 0, max(1, 2048 // 4) + 1, jnp.int32)
        _lenS2 = 77 - jax.random.randint(jax.random.fold_in(_rk, 8), (4,), 0, max(1, 77 // 4) + 1, jnp.int32)
        _ctx_512P = jax.random.normal(jax.random.fold_in(_rk, 11), (4, 16, 256), jnp.float32)
        _ctx_512c = jax.random.dirichlet(jax.random.fold_in(_rk, 511), 0.3 * jnp.ones((16,), jnp.float32), (4, 77))
        _ctx_512t = jnp.einsum('bsk,bkd->bsd', _ctx_512c, _ctx_512P)
        _ctx_512t = _ctx_512t * jax.lax.rsqrt(jnp.mean(jnp.square(_ctx_512t)) + 1e-12) * 0.953939
        ctx_512 = -1.39393e-06 + 0.999914 * (_ctx_512t + 0.3 * jax.random.normal(jax.random.fold_in(_rk, 611), (4, 77, 256), jnp.float32))
        return (x, ctx_512)
    x, ctx_512 = _rec_inputs()

    def _L0_xattn_setup():
        import jax, jax.numpy as jnp
        import numpy as np
        HEADS = 16
        D_MODEL = 512
        IMG_MODEL = 256
        D_K = D_MODEL // HEADS
        key = jax.random.key(seed)
        ks = jax.random.split(key, 12)
        B, LQ, LKV = (8, 1024, 512)
        s_dm = 1.0 / np.sqrt(D_MODEL)
        s_im = 1.0 / np.sqrt(IMG_MODEL)
        return {'q': jax.random.normal(ks[0], (B, LQ, D_MODEL), jnp.float32), 'k': jax.random.normal(ks[1], (B, LKV, IMG_MODEL), jnp.float32), 'v': jax.random.normal(ks[2], (B, LKV, IMG_MODEL), jnp.float32), 'Wq': jax.random.normal(ks[3], (D_MODEL, D_MODEL), jnp.float32) * s_dm, 'bq': jnp.zeros((D_MODEL,), jnp.float32), 'Wk': jax.random.normal(ks[4], (IMG_MODEL, D_MODEL), jnp.float32) * s_im, 'bk': jnp.zeros((D_MODEL,), jnp.float32), 'Wv': jax.random.normal(ks[5], (IMG_MODEL, D_MODEL), jnp.float32) * s_im, 'bv': jnp.zeros((D_MODEL,), jnp.float32), 'Wo': jax.random.normal(ks[6], (D_MODEL, D_MODEL), jnp.float32) * s_dm, 'bo': jnp.zeros((D_MODEL,), jnp.float32)}
    _L0_xattn_all = _L0_xattn_setup()
    _L0_xattn_in = {k: v for k, v in _L0_xattn_all.items() if k in ('Wq', 'bq', 'Wk', 'bk', 'Wv', 'bv', 'Wo', 'bo')}
    del _L0_xattn_all

    def _L0_ffn_setup():
        import jax, jax.numpy as jnp
        import numpy as np
        B, S, H, E = (2, 4096, 512, 8)
        SCALE = 0.5
        key = jax.random.key(seed)
        k1, k2 = jax.random.split(key)
        x = jax.random.normal(k1, (B, S, H), dtype=jnp.float32)
        gate_w = jax.random.normal(k2, (E, H), dtype=jnp.float32) * 0.02
        coeff = SCALE * (1.0 + 0.05 * jnp.arange(E, dtype=jnp.float32))
        expert_w = coeff[:, None, None] * jnp.eye(H, dtype=jnp.float32)
        return {'x': x, 'gate_w': gate_w, 'expert_w': expert_w}
    _L0_ffn_all = _L0_ffn_setup()
    _L0_ffn_in = {k: v for k, v in _L0_ffn_all.items() if k in ('gate_w', 'expert_w')}
    del _L0_ffn_all
    return {'x': x, 'ctx_512': ctx_512, 'L0_xattn_Wq': _L0_xattn_in['Wq'], 'L0_xattn_bq': _L0_xattn_in['bq'], 'L0_xattn_Wk': _L0_xattn_in['Wk'], 'L0_xattn_bk': _L0_xattn_in['bk'], 'L0_xattn_Wv': _L0_xattn_in['Wv'], 'L0_xattn_bv': _L0_xattn_in['bv'], 'L0_xattn_Wo': _L0_xattn_in['Wo'], 'L0_xattn_bo': _L0_xattn_in['bo'], 'L0_ffn_gate_w': _L0_ffn_in['gate_w'], 'L0_ffn_expert_w': _L0_ffn_in['expert_w']}

def reference(x, ctx_512, L0_xattn_Wq, L0_xattn_bq, L0_xattn_Wk, L0_xattn_bk, L0_xattn_Wv, L0_xattn_bv, L0_xattn_Wo, L0_xattn_bo, L0_ffn_gate_w, L0_ffn_expert_w):
    import jax
    import jax.numpy as jnp

    def _L0_xattn_ref(q, k, v, Wq, bq, Wk, bk, Wv, bv, Wo, bo):
        import jax, jax.numpy as jnp
        import numpy as np
        HEADS = 16
        D_MODEL = 512
        IMG_MODEL = 256
        D_K = D_MODEL // HEADS
        B, LQ, _ = q.shape
        LKV = k.shape[1]
        qh = (q @ Wq + bq).reshape(B, LQ, HEADS, D_K).transpose(0, 2, 1, 3)
        kh = (k @ Wk + bk).reshape(B, LKV, HEADS, D_K).transpose(0, 2, 1, 3)
        vh = (v @ Wv + bv).reshape(B, LKV, HEADS, D_K).transpose(0, 2, 1, 3)
        scale = 1.0 / np.sqrt(D_K)
        scores = jnp.einsum('bhqd,bhkd->bhqk', qh, kh) * scale
        attn = jax.nn.softmax(scores, axis=-1)
        out = jnp.einsum('bhqk,bhkd->bhqd', attn, vh)
        concat = out.transpose(0, 2, 1, 3).reshape(B, LQ, D_MODEL)
        return concat @ Wo + bo

    def _L0_ffn_ref(x, gate_w, expert_w):
        import jax, jax.numpy as jnp
        import numpy as np
        B, S, H, E = (2, 4096, 512, 8)
        SCALE = 0.5
        scores = jnp.einsum('bsh,eh->bse', x, gate_w)
        chosen = jnp.argmax(scores, axis=-1)
        onehot = jax.nn.one_hot(chosen, gate_w.shape[0], dtype=x.dtype)
        expert_out = jnp.einsum('bsh,efh->bsef', x, expert_w)
        return x + jnp.einsum('bsef,bse->bsf', expert_out, onehot)
    x = x + _L0_xattn_ref(_layernorm(x, axis=-1), ctx_512, ctx_512, L0_xattn_Wq, L0_xattn_bq, L0_xattn_Wk, L0_xattn_bk, L0_xattn_Wv, L0_xattn_bv, L0_xattn_Wo, L0_xattn_bo)
    x = x + _L0_ffn_ref(_layernorm(x, axis=-1), L0_ffn_gate_w, L0_ffn_expert_w)
    return x

_drawn_inputs = setup_inputs


def setup_inputs(seed=0):
    import zlib

    import numpy as np

    out = dict(_drawn_inputs(seed))
    spreads = {'L0_xattn_bq': (0.0, 0.389),
     'L0_xattn_bk': (0.0, 0.8),
     'L0_xattn_bv': (0.0, 0.1),
     'L0_xattn_bo': (0.0, 0.1)}
    factors = {'L0_ffn_gate_w': 2.778}
    for name, (base, spread) in spreads.items():
        noise = np.random.default_rng([zlib.crc32(name.encode()), seed]).standard_normal(out[name].shape)
        drawn = base * np.exp(spread * noise) if base else spread * noise
        out[name] = jnp.asarray(drawn.astype(out[name].dtype))
    for name, factor in factors.items():
        out[name] = (out[name] * factor).astype(out[name].dtype)
    return out
```

```python
from contextlib import ExitStack

import concourse.bass as bass

from concourse import mybir

F32, F32R, F16, BF16, I32 = (mybir.dt.float32, mybir.dt.float32r, mybir.dt.float16,
                             mybir.dt.bfloat16, mybir.dt.int32)
ALU = mybir.AluOpType
ACT = mybir.ActivationFunctionType
X = mybir.AxisListType.X

P = 128
B, LQ, DM = 4, 2048, 512
LK, DC = 77, 256
H = 16
DK = DM // H
E = 8
EPS = 1e-5
KT = DM // P
CT = DC // P
HG = P // DK
TPC = 4
CH = TPC * P
NCHUNK = B * LQ // CH
CPB = NCHUNK // B
NC = 3
PK = -(-HG * LK // NC)
KC = HG * LK
KCP = NC * PK
VC = DK + 1
NTOK = B * LQ
REGION = NTOK + P
ROW = DM + 3
C_RSTD, C_NMR, C_ID = DM, DM + 1, DM + 2
NTILE = NTOK // P + E
UNROLL = 8
SCALE = 1.0 / float(DK) ** 0.5
TOP = 16384.0

STEPS = [("T", t) for t in range(TPC)] + [("NM",)] + [("C", t) for t in range(TPC)] + [("S", 0), ("Q", 0)]
for _g in range(1, KT):
    STEPS += [("S", _g), ("M", _g - 1, 0), ("O", _g - 1), ("M", _g - 1, 1), ("Q", _g), ("M", _g - 1, 2),
              ("PV", _g - 1), ("M", _g - 1, 3)]
STEPS += [("O", KT - 1), ("M", KT - 1, 0), ("GC",), ("M", KT - 1, 1), ("PV", KT - 1), ("M", KT - 1, 2), ("GX",),
          ("M", KT - 1, 3), ("R",)]
FRONT, CORE, TAIL = {"T", "Q", "M", "GX"}, {"NM", "S", "PV"}, {"C", "O", "GC", "R"}
BANKED = {"T", "C", "NM", "Q", "M", "O", "GX", "GC", "R"}
SPLIT = {"T", "C", "Q"}
WB = 3
LAST = NCHUNK + 1


def steps_of(front, core, tail):
    return [s for s in STEPS if (s[0] in FRONT and front) or (s[0] in CORE and core) or (s[0] in TAIL and tail)]


class Chunk:

    def __init__(self, b, c):
        self.b, self.c = b, c

    def plus(self, k):
        return Chunk(self.b, self.c + k)

    @property
    def static(self):
        return isinstance(self.b, int)

    @property
    def n(self):
        return self.b * CPB + self.c

    @property
    def slot(self):
        return self.c % CPB

    @property
    def batch(self):
        return self.b + self.c // CPB

    def is_(self, k):
        return self.static and self.n == k

    def steps(self):
        i = self.n if self.static else 1
        return steps_of(i < NCHUNK - 1, 0 <= i < NCHUNK, i >= 1)

    def number(self, what, kinds):
        own = [s for s in self.steps() if s[0] in kinds]
        first, second, full = (len([s for s in steps_of(*p) if s[0] in kinds])
                               for p in ((True, False, False), (True, True, False), (True, True, True)))
        k = own.index(what)
        if self.is_(-1):
            return k
        if self.is_(0):
            return first + k
        if self.is_(NCHUNK):
            before = len([s for s in steps_of(False, True, True) if s[0] in kinds])
            return first + second + full * (NCHUNK - 2) + before + k
        return (self.n - 1) * full + (first + second + k)


def build(nc, x, ctx, Wq, bq, Wk, bk, Wv, bv, Wo, bo, gate_w, expert_w, out):
    es = ExitStack()
    sems = {}

    def sb(name, shape, dt=F32, stack=es):
        return stack.enter_context(nc.sbuf_tensor(name, shape, dt))

    def sem(name):
        if name not in sems:
            sems[name] = es.enter_context(nc.semaphore(name))
        return sems[name]

    def wait_alone(eng, name, value):
        eng.wait_ge(sem(name), value)
        eng.sem_inc(sem("waited_alone"))

    def steps(eng, name):
        n = [0]

        def do(ins):
            n[0] += 1
            ins.then_inc(sem(name), 1)
            eng.wait_ge(sem(name), n[0])
        return do

    rows = nc.dram_tensor("rows_by_expert", [E * REGION + P, ROW], F32)
    rows = rows.ap()
    out_rows = out.rearrange("b s d -> (b s) d")

    ident = sb("ident", [P, P])
    base = sb("base", [P, E])
    inv = sb("inv", [P, 8])
    scl = sb("scl", [P, 8])
    S_WQ, S_WO, S_G, S_V, S_WG, S_E = range(6)
    attention = ExitStack()

    def sa(name, shape, dt=F32):
        return sb(name, shape, dt, attention)

    wq = [sa(f"wq_{s}", [P, KT, DM], F16) for s in ("hi", "lo")]
    wo = [sa(f"wo_{s}", [P, KT, DM], F16) for s in ("hi", "lo")]
    gt = [sa(f"gate_{s}", [P, KT, E], F16) for s in ("hi", "lo")]
    wg = [sa(f"wogate_{s}", [P, KT, E], F16) for s in ("hi", "lo")]
    k_all = [sa(f"k_all_{s}", [P, B, KT, LK], F32R) for s in ("hi", "lo")]
    k_cur = [sa(f"k_cur_{s}", [P, KT, KCP], F32R) for s in ("hi", "lo")]
    v_all = [sa(f"v_all_{s}", [PK, B, KT, NC, 2 * VC], F16) for s in ("hi", "lo")]
    mask_k = sa("mask_k", [P, HG])
    sel = sa("sel", [P, KT, KCP], F32R)
    tri = sa("tri", [P, P], BF16)
    ones = sa("ones", [P, P], BF16)
    bo_rep = sa("bo_rep", [P, DM])
    bq_s = sa("bq_s", [P, KT])
    gate_c = sa("gate_c", [P, E])
    exp_scale = sa("exp_scale", [P, 1])
    inv_y = sa("inv_y", [P, 1])
    inv_gc = sa("inv_gc", [P, 1])
    pows = sa("pows", [P, 2, TPC])
    weight8 = sa("weight8", [P, E])
    token = sa("token", [P, TPC])
    xt = sa("xt", [P, CPB, TPC, DM])
    xv = x.rearrange("b (c t p) d -> (b c) p t d", t=TPC, p=P)

    with ExitStack() as st:
        def sp_(name, shape, dt=F32):
            return sb(name, shape, dt, st)
        wraw = {n: sp_("raw_" + n, [P, KT, DM]) for n in ("q", "o")}
        craw = {n: sp_("raw_" + n, [P, CT, DM]) for n in ("k", "v")}
        cx = sp_("cx", [LK, B, DC])
        cxT = sp_("cxT", [P, CT, B, KCP])
        bvec = sp_("bvec", [P, 3, KT])
        bv_rep = sp_("bv_rep", [P, DM])
        g8 = sp_("g8", [E, DM])
        gmean = sp_("gmean", [E, 1])
        gc8 = sp_("gc8", [E, DM])
        gT = sp_("gT", [P, KT, E])
        woT = sp_("woT", [P, KT, DM])
        wgf = sp_("wgf", [P, KT, E])
        kT = sp_("kT", [P, B, KT, LK])
        vf = sp_("vf", [PK, B, NC, DM])
        vs = [sp_(f"vs_{s}", [PK, B, NC, DM], F16) for s in ("hi", "lo")]
        mask_v = sp_("mask_v", [PK, NC, 2])
        self32 = sp_("sel32", [P, KT, KCP])
        bo_mat = sp_("bo_mat", [P, KT, P])
        mx = sp_("mx", [P, 8])
        onesf = sp_("onesf", [P, P])
        bank = [st.enter_context(nc.psum_tensor(f"prep{i}", [P, 512], F32)) for i in range(4)]
        blk = st.enter_context(nc.Block())

        @blk.sync
        def _(sp):
            def load(dst, src, name, n=1):
                sp.dma_start(dst, src).then_inc(sem(name), 16)
            load(cx[:], ctx.rearrange("b s d -> s b d"), "ld_cx")
            load(craw["k"][:], Wk.rearrange("(t p) n -> p t n", p=P), "ld_wk")
            load(craw["v"][:], Wv.rearrange("(t p) n -> p t n", p=P), "ld_wv")
            load(wraw["o"][:], Wo.rearrange("(t p) n -> p t n", p=P), "ld_wo")
            load(wraw["q"][:], Wq.rearrange("(t p) n -> p t n", p=P), "ld_wq")
            for c in range(CPB):
                load(xt[:, c, :, :], xv[c], f"x_in{c}")

        @blk.scalar
        def _(act):
            with nc.allow_non_contiguous_dma(reason="a few bias vectors by feature"):
                for n, v in enumerate((bq, bk, bo)):
                    act.dma_start(bvec[:, n, :], v.rearrange("(t p) -> p t", p=P)).then_inc(sem("ld_bias"), 16)
            act.dma_start(g8[:], gate_w).then_inc(sem("ld_bias"), 16)
            act.dma_start(bv_rep[:], bv.rearrange("(a n) -> a n", a=1).to_broadcast([P, DM])).then_inc(sem("ld_bias"), 16)
            act.dma_start(bo_rep[:], bo.rearrange("(a n) -> a n", a=1).to_broadcast([P, DM])).then_inc(sem("ld_bias"), 16)

        NBIAS = 6 * 16

        @blk.gpsimd
        def _(pool):
            do = steps(pool, "pool_prep")
            do(nc.gpsimd.memset(ident[:], 0.0))
            do(nc.gpsimd.memset(onesf[:], 1.0))
            do(nc.gpsimd.affine_select(out=ident[:], in_=ident[:], compare_op=ALU.not_equal, fill=1.0, base=0,
                                       pattern=[[-1, P]], channel_multiplier=1))
            do(nc.gpsimd.affine_select(out=onesf[:], in_=onesf[:], compare_op=ALU.is_gt, fill=0.0, base=0,
                                       pattern=[[1, P]], channel_multiplier=-1))
            do(nc.gpsimd.tensor_copy(tri[:], onesf[:]))
            do(nc.gpsimd.memset(ones[:], 1.0))
            do(nc.gpsimd.memset(mask_k[:], 1.0))
            do(nc.gpsimd.affine_select(out=mask_k[:], in_=mask_k[:], compare_op=ALU.is_ge, fill=0.0, base=0,
                                       pattern=[[-DK, HG]], channel_multiplier=1))
            do(nc.gpsimd.affine_select(out=mask_k[:], in_=mask_k[:], compare_op=ALU.is_ge, fill=0.0, base=DK - 1,
                                       pattern=[[DK, HG]], channel_multiplier=-1))
            do(nc.gpsimd.memset(mask_v[:], 1.0))
            do(nc.gpsimd.affine_select(out=mask_v[:], in_=mask_v[:], compare_op=ALU.is_ge, fill=0.0, base=0,
                                       pattern=[[PK - LK, NC], [-LK, 2]], channel_multiplier=1))
            do(nc.gpsimd.affine_select(out=mask_v[:], in_=mask_v[:], compare_op=ALU.is_ge, fill=0.0, base=LK - 1,
                                       pattern=[[LK - PK, NC], [LK, 2]], channel_multiplier=-1))
            do(nc.gpsimd.memset(self32[:], 0.0))
            do(nc.gpsimd.affine_select(out=self32[:, :, 0:KC].rearrange("p g (j s) -> p g j s", j=HG),
                                       in_=self32[:, :, 0:KC].rearrange("p g (j s) -> p g j s", j=HG),
                                       compare_op=ALU.not_equal, fill=1.0, base=0,
                                       pattern=[[-HG, KT], [-1, HG], [0, LK]], channel_multiplier=1))
            nc.gpsimd.memset(pows[:, 0, :], -0.5)
            nc.gpsimd.memset(pows[:, 1, :], 0.5)
            do(nc.gpsimd.iota(base[:], pattern=[[REGION, E]], base=0, channel_multiplier=0,
                              allow_small_or_imprecise_dtypes=True))
            do(nc.gpsimd.iota(weight8[:], pattern=[[-1, E]], base=E, channel_multiplier=0,
                              allow_small_or_imprecise_dtypes=True))
            do(nc.gpsimd.iota(token[:], pattern=[[P, TPC]], base=0, channel_multiplier=1,
                              allow_small_or_imprecise_dtypes=True))
            nc.gpsimd.memset(cxT[:, :, :, KC:KCP], 0.0).then_inc(sem("consts"), 1)
            for n, (c0, c1) in enumerate(((S_WQ, S_G + 1), (S_V, S_WG + 1))):
                pool.wait_ge(sem("mx_in"), n + 1)
                nc.gpsimd.partition_all_reduce(mx[:, c0:c1], mx[:, c0:c1], P, bass.bass_isa.ReduceOp.max)\
                    .then_inc(sem("mx_out"), 1)

        uses = [("cx", b, k) for b in range(B) for k in range(CT)]
        uses += [("g", 0, 0)] + [("k", g, 0) for g in range(KT)] + [("v", b, c) for b in range(B) for c in range(NC)]
        uses += [("wo", k, 0) for k in range(KT)] + [("wg", 0, 0)]

        @blk.tensor
        def _(pe):
            pe.wait_ge(sem("consts"), 1)
            for n, (kind, a, c) in enumerate(uses):
                if n >= 4:
                    pe.wait_ge(sem("prep_used"), n - 3)
                ps = bank[n % 4]
                if kind == "cx":
                    pe.wait_ge(sem("ld_cx"), 16)
                    last = nc.tensor.transpose(ps[:, 0:LK], cx[:, a, c * P:(c + 1) * P], ident[0:LK, 0:LK])
                elif kind == "k":
                    pe.wait_ge(sem("ld_wk"), 16)
                    pe.wait_ge(sem("prep_used"), uses.index(("cx", B - 1, CT - 1)) + 1)
                    for k in range(CT):
                        last = nc.tensor.matmul(ps[:, 0:B * LK], craw["k"][:, k, a * P:(a + 1) * P],
                                                cxT[:, k, :, 0:LK], start=k == 0, stop=k == CT - 1)
                elif kind == "v":
                    pe.wait_ge(sem("ld_wv"), 16)
                    for k in range(CT):
                        last = nc.tensor.matmul(ps[0:PK, :], cxT[:, k, a, c * PK:(c + 1) * PK],
                                                craw["v"][:, k, :], start=k == 0, stop=k == CT - 1)
                elif kind == "g":
                    pe.wait_ge(sem("gate_centred"), 1)
                    for k in range(KT):
                        last = nc.tensor.transpose(ps[:, k * E:(k + 1) * E], gc8[:, k * P:(k + 1) * P],
                                                   ident[0:E, 0:E])
                elif kind == "wo":
                    pe.wait_ge(sem("ld_wo"), 16)
                    for k in range(KT):
                        last = nc.tensor.transpose(ps[:, k * P:(k + 1) * P], wraw["o"][:, k, a * P:(a + 1) * P],
                                                   ident[:])
                elif kind == "wg":
                    pe.wait_ge(sem("prep_used"), n)
                    pe.wait_ge(sem("bo_ready"), 1)
                    for k in range(KT):
                        for o in range(KT):
                            last = nc.tensor.matmul(ps[:, k * E:(k + 1) * E], woT[:, o, k * P:(k + 1) * P],
                                                    gT[:, o, :], start=o == 0, stop=o == KT - 1)
                    for o in range(KT):
                        last = nc.tensor.matmul(ps[:, KT * E:(KT + 1) * E], bo_mat[:, o, :], gT[:, o, :],
                                                start=o == 0, stop=o == KT - 1)
                last.then_inc(sem("prep_filled"), 1)

        @blk.vector
        def _(dve):
            do = steps(dve, "dve_prep")

            def split(dst, src, s):
                do(nc.vector.tensor_scalar(dst[0], src, s, None, ALU.mult))
                nc.vector.scalar_tensor_tensor(out=dst[1], in0=src, scalar=s, in1=dst[0], op0=ALU.mult,
                                               op1=ALU.subtract)

            def scales(c0, c1):
                do(nc.vector.tensor_scalar(mx[:, c0:c1], mx[:, c0:c1], 1e-25, None, ALU.max))
                do(nc.vector.tensor_scalar(inv[:, c0:c1].bitcast(I32), mx[:, c0:c1].bitcast(I32), 0x7F800000, None,
                                           ALU.bitwise_and))
                do(nc.vector.tensor_scalar(inv[:, c0:c1], inv[:, c0:c1], 1.0 / TOP, None, ALU.mult))
                do(nc.vector.reciprocal(scl[:, c0:c1], inv[:, c0:c1]))

            dve.wait_ge(sem("ld_bias"), NBIAS)
            do(nc.vector.tensor_reduce(gmean[:], g8[:], X, ALU.add))
            do(nc.vector.tensor_scalar(gmean[:], gmean[:], 1.0 / DM, None, ALU.mult))
            nc.vector.tensor_scalar(gc8[:], g8[:], gmean[:, 0:1], None, ALU.subtract).then_inc(sem("gate_centred"), 1)
            dve.wait_ge(sem("consts"), 1)
            do(nc.vector.memset(mx[:], 0.0))
            for s in (0, 1):
                do(nc.vector.memset(v_all[s][:], 0.0))
                do(nc.vector.tensor_scalar(k_cur[s][:, :, KC:KCP], self32[:, :, KC:KCP], 0.0, None, ALU.mult))
            nc.vector.tensor_copy(sel[:], self32[:])
            nc.vector.tensor_copy(bo_mat[:], bvec[:, 2, :].unsqueeze(2).to_broadcast([P, KT, P]))\
                .then_inc(sem("bo_ready"), 1)
            for n, (kind, a, c) in enumerate(uses):
                dve.wait_ge(sem("prep_filled"), n + 1)
                ps = bank[n % 4]
                if kind == "cx":
                    last = nc.vector.tensor_copy(cxT[:, c, a, 0:KC].rearrange("p (j s) -> p j s", j=HG),
                                                 ps[:, 0:LK].unsqueeze(1).to_broadcast([P, HG, LK]))
                elif kind == "k":
                    last = nc.vector.tensor_scalar(kT[:, :, a, :], ps[:, 0:B * LK].rearrange("p (b s) -> p b s", b=B),
                                                   bvec[:, 1, a:a + 1], None, ALU.add)
                elif kind == "v":
                    last = nc.vector.tensor_tensor(vf[:, a, c, :], ps[0:PK, :], bv_rep[0:PK, :], ALU.add)
                elif kind == "g":
                    last = nc.vector.tensor_copy(gT[:].rearrange("p k e -> p (k e)"), ps[:, 0:KT * E])
                elif kind == "wo":
                    last = nc.vector.tensor_copy(woT[:, a, :], ps[:, :])
                elif kind == "wg":
                    nc.vector.tensor_copy(wgf[:].rearrange("p k e -> p (k e)"), ps[:, 0:KT * E])
                    last = nc.vector.tensor_copy(gate_c[:], ps[:, KT * E:(KT + 1) * E])
                last.then_inc(sem("prep_used"), 1)
            dve.wait_ge(sem("prep_used"), len(uses))
            AX2 = mybir.AxisListType.XY
            dve.wait_ge(sem("ld_wq"), 16)
            dve.wait_ge(sem("ld_wo"), 16)
            for col, src in ((S_WQ, wraw["q"]), (S_WO, wraw["o"]), (S_G, gT)):
                last = nc.vector.tensor_reduce(mx[:, col:col + 1], src[:], AX2, ALU.max, apply_absolute_value=True)
            last.then_inc(sem("mx_in"), 1)
            nc.vector.tensor_reduce(mx[0:PK, S_V:S_V + 1], vf[:], mybir.AxisListType.XYZ, ALU.max,
                                    apply_absolute_value=True)
            nc.vector.tensor_reduce(mx[:, S_WG:S_WG + 1], wgf[:], AX2, ALU.max, apply_absolute_value=True)\
                .then_inc(sem("mx_in"), 1)
            do(nc.vector.tensor_copy(k_all[0][:], kT[:]))
            nc.vector.tensor_tensor(k_all[1][:], kT[:], k_all[0][:].bitcast(F32), ALU.subtract)
            dve.wait_ge(sem("mx_out"), 2)
            scales(S_WQ, S_WG + 1)
            split([w[:] for w in wq], wraw["q"][:], scl[:, S_WQ:S_WQ + 1])
            split([w[:] for w in wo], wraw["o"][:], scl[:, S_WO:S_WO + 1])
            split([w[:] for w in gt], gT[:], scl[:, S_G:S_G + 1])
            split([w[:] for w in wg], wgf[:], scl[:, S_WG:S_WG + 1])
            split([v[:] for v in vs], vf[:], scl[0:PK, S_V:S_V + 1])
            do(nc.vector.tensor_scalar(bq_s[:], bvec[:, 0, :], scl[:, S_WQ:S_WQ + 1], None, ALU.mult))
            nc.vector.tensor_scalar(exp_scale[:], inv[:, S_WQ:S_WQ + 1], SCALE, None, ALU.mult)
            nc.vector.tensor_tensor(inv_y[:], inv[:, S_WO:S_WO + 1], inv[:, S_V:S_V + 1], ALU.mult)
            nc.vector.tensor_tensor(inv_gc[:], inv[:, S_WG:S_WG + 1], inv[:, S_V:S_V + 1], ALU.mult)
            for s in (0, 1):
                for b in range(B):
                    for c in range(NC):
                        for d in range(2):
                            src = vs[s][:, b, c, :].rearrange("p (g j k) -> p g j k", g=KT, j=HG)[:, :, c + d, :]
                            nc.vector.tensor_scalar(v_all[s][:, b, :, c, d * VC:d * VC + DK], src,
                                                    mask_v[:, c, d:d + 1], None, ALU.mult)
                        if s == 0:
                            den = v_all[s][:, b, :, c, :].rearrange("p g (d k) -> p g d k", d=2)[:, :, :, DK]
                            do(nc.vector.tensor_copy(den, mask_v[:, c, :].unsqueeze(1).to_broadcast([PK, KT, 2])))

    with ExitStack() as st:
        def sp_(name, shape, dt=F32):
            return sb(name, shape, dt, st)
        xn = sp_("xn", [P, TPC, DM])
        bst = sp_("bst", [P, TPC, 6])
        mv = sp_("mv", [P, TPC, 2])
        ve = sp_("ve", [P, TPC])
        rstd = sp_("rstd", [P, TPC])
        std = sp_("std", [P, 2, TPC])
        nmr = sp_("nmr", [P, TPC])
        xnT = [sp_(f"xnT_{s}", [P, KT, CH], F16) for s in ("hi", "lo")]
        q = [sp_(f"q_{s}", [P, KT, CH], F32R) for s in ("hi", "lo")]
        negmax = sp_("negmax", [P, TPC, P])
        nmT = sp_("nmT", [P, CH], F32R)
        pf = sp_("pf", [PK, 2, NC, CH])
        pp = [sp_(f"p_{s}", [PK, 2, NC, CH], F16) for s in ("hi", "lo")]
        den = sp_("den", [P, 2, 2, HG])
        cc = sp_("cc", [P, TPC, DM])
        cT = [sp_(f"cT_{s}", [P, KT, CH], F16) for s in ("hi", "lo")]
        pay = sp_("pay", [P, 2, TPC, ROW])
        bst2 = sp_("bst2", [P, TPC, 6])
        mv2 = sp_("mv2", [P, TPC, 2])
        ve2 = sp_("ve2", [P, TPC])
        gx = sp_("gx", [P, 2, TPC, E])
        lg = sp_("lg", [P, TPC, E])
        lmax = sp_("lmax", [P, TPC])
        oh = sp_("oh", [P, TPC, E], BF16)
        slotf = sp_("slotf", [P, TPC])
        slot = sp_("slot", [P, 2, TPC], I32)
        sbank = [st.enter_context(nc.psum_tensor(f"scoresT{c}", [P, 512], F32)) for c in range(NC)]
        obank = [st.enter_context(nc.psum_tensor(f"pv{c}", [P, 512], F32)) for c in range(2)]
        wbank = [st.enter_context(nc.psum_tensor(f"work{c}", [P, 512], F32)) for c in range(WB)]
        blk = st.enter_context(nc.Block())

        full = steps_of(True, True, True)
        assert len([st_ for st_ in full if st_[0] in BANKED]) % WB == 0

        def use(i, *what):
            return i.number(what, BANKED)

        def bank_of(i, *what):
            j = i if i.static else Chunk(0, 1)
            return wbank[j.number(what, BANKED) % WB]

        def iterations(eng, iteration):
            iteration(Chunk(0, -1))
            iteration(Chunk(0, 0))
            with eng.Fori(0, B - 1) as b:
                for c in range(CPB):
                    iteration(Chunk(b, c + 1))
            for c in range(CPB):
                iteration(Chunk(B - 1, c + 1))

        def has_ln(i):
            return not i.static or i.n + 2 < NCHUNK

        class OwnCount:

            def __init__(self, per):
                self.per, self.before, self.done = per, 0, 0

            def begin(self, i):
                if not i.static:
                    if i.c == 1:
                        self.before += self.done
                    else:
                        assert self.done == self.per, self.done
                    self.base = (i.n - 1) * self.per + self.before
                else:
                    self.before += self.done + (self.per * (CPB * (B - 1) - 1) if i.n == NCHUNK - 3 else 0)
                    self.base = self.before
                self.done = 0

            def value(self):
                return self.base + self.done

        @blk.sync
        def _(sp):
            with sp.Fori(0, B - 1) as b:
                for c in range(CPB):
                    m = Chunk(b, c)
                    sp.wait_ge(sem("work_used"), use(m.plus(1), "O", TPC - 1) + 1)
                    sp.dma_start(xt[:, m.slot, :, :],
                                 xv[bass.ds(m.plus(CPB).n, 1), :, :, :].rearrange("a p t d -> p (a t) d"))\
                        .then_inc(sem(f"x_in{c}"), 16)

        @blk.gpsimd
        def _(pool):
            own = OwnCount(4)

            def do(ins):
                own.done += 1
                ins.then_inc(sem("pool_step"), 1)
                wait_alone(pool, "pool_step", own.value())

            def ln(n):
                wait_alone(pool, "ln_stats", n.n + 1)
                nc.gpsimd.tensor_tensor(std[:, n.slot % 2, :], ve[:], pows[:, 1, :], ALU.pow)
                do(nc.gpsimd.tensor_tensor(rstd[:], ve[:], pows[:, 0, :], ALU.pow))
                do(nc.gpsimd.tensor_tensor(nmr[:], mv[:, :, 0], rstd[:], ALU.mult))
                if not n.is_(0):
                    wait_alone(pool, "work_filled", use(n.plus(-2), "T", TPC - 1) + 1)
                for t in range(TPC):
                    nc.gpsimd.tensor_scalar(xn[:, t, :], xt[:, n.slot, t, :], rstd[:, t:t + 1], nmr[:, t:t + 1],
                                            ALU.mult, ALU.subtract).then_inc(sem("xn_ready"), 1)

            def iteration(i):
                own.begin(i)
                if i.is_(-1):
                    ln(Chunk(0, 0))
                    ln(Chunk(0, 1))
                    return
                if has_ln(i):
                    ln(i.plus(2))
                if not i.is_(NCHUNK):
                    for t in range(TPC):
                        nc.gpsimd.tensor_tensor(xt[:, i.slot, t, :], xt[:, i.slot, t, :], bo_rep[:], ALU.add)\
                            .then_inc(sem("x_plus_bo"), 1)
                if i.is_(0):
                    return
                m = i.plus(-1)
                par = m.slot % 2
                wait_alone(pool, "ln2_stats", m.n + 1)
                do(nc.gpsimd.tensor_tensor(pay[:, par, :, C_RSTD], ve2[:], pows[:, 0, :], ALU.pow))
                do(nc.gpsimd.tensor_tensor(mv2[:, :, 1], mv2[:, :, 0], pay[:, par, :, C_RSTD], ALU.mult))
                nc.gpsimd.tensor_scalar(pay[:, par, :, C_NMR], mv2[:, :, 1], -1.0, None, ALU.mult)\
                    .then_inc(sem("pay_stats"), 1)
                wait_alone(pool, "slot_ready", m.n + 1)
                wait_alone(pool, "pay_stats", m.n + 2)
                for t in range(TPC):
                    nc.gpsimd.indirect_dma_start(
                        out=rows, out_offset=bass.IndirectOffsetOnAxis(ap=slot[:, par, t:t + 1], axis=0),
                        in_=pay[:, par, t, :], in_offset=None).then_inc(sem("scattered"), 16)
                pool.wait_ge(sem("scattered"), 16 * TPC * (m.n + 1))
                pool.sem_inc(sem("rows_left"))

            iterations(pool, iteration)

        @blk.tensor
        def _(pe):
            HL = ((0, 0), (1, 0), (0, 1))

            def product(dst, a, bm, first=True, final=True):
                for n, (ia, ib) in enumerate(HL):
                    ins = nc.tensor.matmul(dst, a[ia], bm[ib], start=first and n == 0, stop=final and n == 2)
                return ins

            def used(i, *what):
                pe.wait_ge(sem("work_used"), use(i, *what) + 1)

            def transposed(ps, src):
                for k in range(KT):
                    ins = nc.tensor.transpose(ps[:, k * P:(k + 1) * P], src[:, k * P:(k + 1) * P], ident[:])
                return ins

            def scores(i, g):
                if g == 0:
                    used(i, "NM")
                for c in range(NC):
                    pe.wait_ge(sem("exp_done"), NC * (KT * i.n + g) + c + 1)
                    cols = slice(c * PK, (c + 1) * PK)
                    product(sbank[c][0:PK, :], [k[:, g, cols] for k in k_cur], [v[:, g, :] for v in q], True, False)
                    nc.tensor.matmul(sbank[c][0:PK, :], sel[:, g, cols], nmT[:], start=False, stop=True)\
                        .then_inc(sem("scores_ready"), 1)

            def values(i, g):
                G = KT * i.n + g
                pe.wait_ge(sem("p_lo_ready"), NC * (G + 1))
                for h in range(2):
                    pe.wait_ge(sem("normalised"), 2 * G + h + 1)
                    for t in (2 * h, 2 * h + 1):
                        for c in range(NC):
                            col = (t % 2) * HG * VC + c * VC
                            for n, (ip, iv) in enumerate(HL):
                                vv = v_all[iv][:, bass.ds(i.batch, 1), g, c, :].rearrange("p a n -> p (a n)")
                                ins = nc.tensor.matmul(
                                    obank[h][:, col:col + 2 * VC], pp[ip][:, g % 2, c, t * P:(t + 1) * P], vv,
                                    start=(t % 2 == 0 and c == 0 and n == 0),
                                    stop=(t % 2 == 1 and c == NC - 1 and n == 2), skip_group_check=True)
                    ins.then_inc(sem("values_ready"), 1)

            def banked(i, kind, *at):
                k = use(i, kind, *at)
                if not (i.is_(-1) and k < WB):
                    pe.wait_ge(sem("work_used"), k - WB + 1)
                ps = bank_of(i, kind, *at)
                if kind == "T":
                    pe.wait_ge(sem("xn_ready"), i.plus(1).n * TPC + at[0] + 1)
                    return transposed(ps, xn[:, at[0], :])
                if kind == "C":
                    pe.wait_ge(sem("normalised"), 2 * KT * i.n + 2)
                    return transposed(ps, cc[:, at[0], :])
                if kind == "Q":
                    g, = at
                    if g == 0:
                        used(i, "T", TPC - 1)
                    for k in range(KT):
                        ins = product(ps[:, :], [w[:, k, g * P:(g + 1) * P] for w in wq], [v[:, k, :] for v in xnT],
                                      k == 0, k == KT - 1)
                    return ins
                if kind == "M":
                    g, t = at
                    if t == 0:
                        used(i, "Q", g)
                        pe.wait_ge(sem("k_built"), KT * i.plus(1).batch + g + 1)
                    return nc.tensor.matmul(ps[:, 0:KC], q[0][:, g, t * P:(t + 1) * P], k_cur[0][:, g, 0:KC],
                                            start=True, stop=True)
                if kind == "NM":
                    used(i.plus(-1), "M", KT - 1, TPC - 1)
                    for t in range(TPC):
                        ins = nc.tensor.transpose(ps[:, t * P:(t + 1) * P], negmax[:, t, :], ident[:])
                    return ins
                if kind in ("GX", "GC"):
                    a, w = (xnT, gt) if kind == "GX" else (cT, wg)
                    for t in range(TPC):
                        for k in range(KT):
                            ins = product(ps[:, t * E:(t + 1) * E], [v[:, k, t * P:(t + 1) * P] for v in a],
                                          [v[:, k, :] for v in w], k == 0, k == KT - 1)
                    return ins
                if kind == "O":
                    t, = at
                    used(i, "C", t)
                    for k in range(KT):
                        ins = product(ps[:, :], [v[:, k, t * P:(t + 1) * P] for v in cT], [w[:, k, :] for w in wo],
                                      k == 0, k == KT - 1)
                    return ins
                pe.wait_ge(sem("one_hot"), i.n)
                for t in range(TPC):
                    for s_ in range(t + 1):
                        nc.tensor.matmul(ps[:, t * E:(t + 1) * E], tri[:] if s_ == t else ones[:], oh[:, s_, :],
                                         start=s_ == 0, stop=s_ == t)
                for s_ in range(TPC):
                    ins = nc.tensor.matmul(ps[:, TPC * E:(TPC + 1) * E], ones[:], oh[:, s_, :],
                                           start=s_ == 0, stop=s_ == TPC - 1)
                return ins

            def iteration(i):
                for kind, *at in i.steps():
                    if kind == "S":
                        scores(i, *at)
                    elif kind == "PV":
                        values(i, *at)
                    else:
                        banked(i, kind, *at).then_inc(sem("work_filled"), 1)

            iterations(pe, iteration)

        @blk.scalar
        def _(act):
            act.nop().then_inc(sem("exp_done"), NC)

            def iteration(i):
                for kind, *at in i.steps():
                    if kind in SPLIT:
                        act.wait_ge(sem("work_filled"), use(i, kind, *at) + 1)
                        ps = bank_of(i, kind, *at)
                        if kind == "Q":
                            ins = nc.scalar.activation(q[0][:, at[0], :], ps[:, :], ACT.Identity,
                                                       bias=bq_s[:, at[0]:at[0] + 1])
                        else:
                            dst = (xnT if kind == "T" else cT)[0][:, :, at[0] * P:(at[0] + 1) * P]
                            ins = nc.scalar.activation(dst, ps[:, :].rearrange("p (k n) -> p k n", k=KT), ACT.Copy)
                        ins.then_inc(sem("hi_ready"), 1)
                    elif kind == "S":
                        g, = at
                        G = KT * i.n + g
                        act.wait_ge(sem("values_ready"), 2 * G + 2)
                        for k in range(NC):
                            act.wait_ge(sem("scores_ready"), NC * G + k + 1)
                            nc.scalar.activation(pf[:, g % 2, k, :], sbank[k][0:PK, :], ACT.Exp,
                                                 scale=exp_scale[0:PK, :])
                            nc.scalar.activation(pp[0][:, g % 2, k, :], sbank[k][0:PK, :], ACT.Exp,
                                                 scale=exp_scale[0:PK, :]).then_inc(sem("exp_done"), 1)

            iterations(act, iteration)

        @blk.vector
        def _(dve):
            own = OwnCount(21)

            def mark(ins):
                own.done += 1
                ins.then_inc(sem("dve_step"), 1)

            def do(ins):
                mark(ins)
                dve.wait_ge(sem("dve_step"), own.value())

            dve.nop().then_inc(sem("normalised"), 2)
            dve.nop().then_inc(sem("values_ready"), 4)
            dve.nop().then_inc(sem("rows_left"), 2)
            dve.nop().then_inc(sem("pay_stats"), 1)
            dve.memset(negmax[:], 0.0)

            def build_k(b, g):
                for s_ in (0, 1):
                    src = k_all[s_][:, bass.ds(b, 1), g, :].bitcast(F32).rearrange("p a s -> p (a s)")\
                        .unsqueeze(1).to_broadcast([P, HG, LK])
                    ins = nc.vector.tensor_tensor(
                        k_cur[s_][:, g, 0:KC].rearrange("p (j s) -> p j s", j=HG), src,
                        mask_k[:].unsqueeze(2).to_broadcast([P, HG, LK]), ALU.mult)
                ins.then_inc(sem("k_built"), 1)

            def ln_stats(n, t):
                if t == 0:
                    dve.wait_ge(sem(f"x_in{n.slot}"), 16 * (n.batch + 1))
                ins = nc.vector.bn_stats(bst[:, t, :], xt[:, n.slot, t, :])
                if t == TPC - 1:
                    mark(ins)

            def ln_end(n):
                wait_alone(dve, "dve_step", own.value())
                if not n.is_(0):
                    wait_alone(dve, "xn_ready", TPC * n.n)
                for t in range(TPC):
                    ins = nc.vector.bn_aggr(mv[:, t, :], bst[:, t, :])
                do(ins)
                nc.vector.tensor_scalar(ve[:], mv[:, :, 1], EPS, None, ALU.add).then_inc(sem("ln_stats"), 1)

            def ln(n):
                for t in range(TPC):
                    ln_stats(n, t)
                ln_end(n)

            def lo(i, kind, at):
                dve.wait_ge(sem("hi_ready"), i.number((kind, at), SPLIT) + 1)
                ps = bank_of(i, kind, at)
                if kind == "Q":
                    ins = nc.vector.scalar_tensor_tensor(out=q[1][:, at, :], in0=ps[:, :], scalar=bq_s[:, at:at + 1],
                                                         in1=q[0][:, at, :].bitcast(F32), op0=ALU.add,
                                                         op1=ALU.subtract)
                else:
                    dst = [v[:, :, at * P:(at + 1) * P] for v in (xnT if kind == "T" else cT)]
                    ins = nc.vector.tensor_tensor(dst[1], ps[:, :].rearrange("p (k n) -> p k n", k=KT), dst[0],
                                                  ALU.subtract)
                ins.then_inc(sem("work_used"), 1)

            def p_lo(i, g):
                for k in range(NC):
                    dve.wait_ge(sem("exp_done"), NC * (KT * i.n + g) + k + 1 + NC)
                    nc.vector.tensor_tensor(pp[1][:, g % 2, k, :], pf[:, g % 2, k, :], pp[0][:, g % 2, k, :],
                                            ALU.subtract).then_inc(sem("p_lo_ready"), 1)

            def normalise(i, g):
                for h in range(2):
                    dve.wait_ge(sem("values_ready"), 2 * (KT * i.n + g) + h + 1 + 4)
                    o = obank[h][:, 0:2 * HG * VC].rearrange("p (t j k) -> p t j k", t=2, j=HG)
                    do(nc.vector.reciprocal(den[:, h, :, :], o[:, :, :, DK]))
                    nc.vector.tensor_tensor(
                        cc[:, 2 * h:2 * h + 2, g * P:(g + 1) * P].rearrange("p t (j k) -> p t j k", j=HG),
                        o[:, :, :, 0:DK], den[:, h, :, :].unsqueeze(3).to_broadcast([P, 2, HG, DK]), ALU.mult)\
                        .then_inc(sem("normalised"), 1)

            def by_tile(ps):
                return ps[:, 0:TPC * E].rearrange("p (t e) -> p t e", t=TPC)

            def banked(i, kind, *at):
                dve.wait_ge(sem("work_filled"), use(i, kind, *at) + 1)
                ps = bank_of(i, kind, *at)
                if kind == "M":
                    g, t = at
                    return nc.vector.tensor_reduce(negmax[:, t, g * HG:(g + 1) * HG],
                                                   ps[:, 0:KC].rearrange("p (j s) -> p j s", j=HG), X, ALU.max,
                                                   negate=True)
                if kind == "NM":
                    return nc.vector.tensor_copy(nmT[:], ps[:, :])
                if kind == "GX":
                    par = i.plus(1).slot % 2
                    do(nc.vector.tensor_tensor(gx[:, par], by_tile(ps), std[:, par, :].unsqueeze(2)
                                               .to_broadcast([P, TPC, E]), ALU.mult))
                    return nc.vector.scalar_tensor_tensor(out=gx[:, par], in0=gx[:, par], scalar=inv[:, S_G:S_G + 1],
                                                          in1=gate_c[:].unsqueeze(1).to_broadcast([P, TPC, E]),
                                                          op0=ALU.mult, op1=ALU.add)
                m = i.plus(-1)
                par = m.slot % 2
                if kind == "O":
                    t, = at
                    if t == 0:
                        dve.wait_ge(sem("rows_left"), m.n + 1)
                    dve.wait_ge(sem("x_plus_bo"), TPC * m.n + t + 1)
                    return nc.vector.scalar_tensor_tensor(out=pay[:, par, t, 0:DM], in0=ps[:, :], scalar=inv_y[:],
                                                          in1=xt[:, m.slot, t, :], op0=ALU.mult, op1=ALU.add)
                if kind == "GC":
                    return nc.vector.scalar_tensor_tensor(out=lg[:], in0=by_tile(ps), scalar=inv_gc[:], in1=gx[:, par],
                                                          op0=ALU.mult, op1=ALU.add)
                do(nc.vector.tensor_tensor(lg[:], by_tile(ps), base[:].unsqueeze(1).to_broadcast([P, TPC, E]),
                                           ALU.add))
                return nc.vector.tensor_tensor(base[:], ps[:, TPC * E:(TPC + 1) * E], base[:], ALU.add)

            def one_hot(i):
                dve.wait_ge(sem("work_used"), use(i, "GC") + 1)
                do(nc.vector.tensor_reduce(lmax[:], lg[:], X, ALU.max))
                do(nc.vector.tensor_tensor(lg[:], lg[:], lmax[:].unsqueeze(2).to_broadcast([P, TPC, E]), ALU.is_ge))
                do(nc.vector.tensor_tensor(lg[:], lg[:], weight8[:].unsqueeze(1).to_broadcast([P, TPC, E]), ALU.mult))
                do(nc.vector.tensor_reduce(lmax[:], lg[:], X, ALU.max))
                nc.vector.tensor_tensor(oh[:], lg[:], lmax[:].unsqueeze(2).to_broadcast([P, TPC, E]), ALU.is_equal)\
                    .then_inc(sem("one_hot"), 1)
                wait_alone(dve, "pay_stats", i.n)
                for t in range(TPC):
                    ins = nc.vector.bn_aggr(mv2[:, t, :], bst2[:, t, :])
                do(ins)
                nc.vector.tensor_scalar(ve2[:], mv2[:, :, 1], EPS, None, ALU.add).then_inc(sem("ln2_stats"), 1)

            def slots(i):
                par = i.plus(-1).slot % 2
                dve.wait_ge(sem("work_used"), use(i, "R") + 1)
                do(nc.vector.tensor_tensor(lg[:], lg[:], oh[:], ALU.mult))
                do(nc.vector.tensor_reduce(slotf[:], lg[:], X, ALU.add))
                nc.vector.tensor_copy(slot[:, par, :], slotf[:])
                do(nc.vector.tensor_copy(pay[:, par, :, C_ID].bitcast(I32), token[:]))
                nc.vector.tensor_scalar(token[:], token[:], float(CH), None, ALU.add).then_inc(sem("slot_ready"), 1)

            def iteration(i):
                own.begin(i)
                if i.is_(-1):
                    ln(Chunk(0, 0))
                    for g in range(KT):
                        build_k(0, g)
                for kind, *at in i.steps():
                    if kind in SPLIT:
                        lo(i, kind, *at)
                        if has_ln(i) and not i.is_(-1) and kind == "Q" and at[0] < 2:
                            for t in (2 * at[0], 2 * at[0] + 1):
                                ln_stats(i.plus(2), t)
                            if at[0] == 1:
                                ln_end(i.plus(2))
                        if i.is_(-1) and (kind, *at) == ("T", TPC - 1):
                            ln(Chunk(0, 1))
                    elif kind == "S":
                        p_lo(i, *at)
                        if i.slot == CPB - 1 and not i.is_(NCHUNK - 1):
                            build_k(i.plus(1).batch, *at)
                    elif kind == "PV":
                        normalise(i, *at)
                    else:
                        banked(i, kind, *at).then_inc(sem("work_used"), 1)
                        if kind == "O":
                            dve.wait_ge(sem("work_used"), use(i, "O", *at) + 1)
                            mark_last = nc.vector.bn_stats(bst2[:, at[0], :], pay[:, i.plus(-1).slot % 2, at[0], 0:DM])
                            if at[0] == TPC - 1:
                                mark(mark_last)
                        if kind == "GC":
                            one_hot(i)
                        if kind == "R":
                            slots(i)

            iterations(dve, iteration)
    attention.close()

    e_w = [sb(f"e_{s}", [P, E, KT, DM], F16) for s in ("hi", "lo")]
    tab = sb("tab", [P, 2, NTILE], I32)
    with ExitStack() as st:
        def sp_(name, shape, dt=F32):
            return sb(name, shape, dt, st)
        er = sp_("er", [P, E, KT, DM])
        mxe = sp_("mxe", [P, E])
        mx = sp_("mx_e", [P, 1])
        zrow = sp_("zrow", [P, ROW])
        row_p = sp_("row_p", [P, 1])
        region = sp_("region", [P, E])
        ntf = sp_("ntf", [P, E])
        nti = sp_("nti", [P, E], I32)
        cum = sp_("cum", [P, E])
        jump = sp_("jump", [P, E])
        tile = sp_("tile", [P, NTILE])
        start = sp_("start", [P, NTILE])
        which = sp_("which", [P, NTILE])
        ge = sp_("ge", [P, NTILE])
        padf = sp_("padf", [P, E])
        pads = sp_("pads", [P, E], I32)
        NBK = 6
        bank = [st.enter_context(nc.psum_tensor(f"ex{i}", [P, 512], F32)) for i in range(NBK)]
        blk = st.enter_context(nc.Block())

        @blk.sync
        def _(sp):
            for e in range(E):
                sp.dma_start(er[:, e, :, :], expert_w[e].rearrange("(t p) h -> p t h", p=P))\
                    .then_inc(sem(f"e_in{e}"), 16)

        @blk.gpsimd
        def _(pool):
            do = steps(pool, "pool_experts")
            do(nc.gpsimd.iota(region[:], pattern=[[REGION, E]], base=0, channel_multiplier=0,
                              allow_small_or_imprecise_dtypes=True))
            do(nc.gpsimd.iota(row_p[:], pattern=[[0, 1]], base=0, channel_multiplier=1,
                              allow_small_or_imprecise_dtypes=True))
            do(nc.gpsimd.iota(tile[:], pattern=[[1, NTILE]], base=0, channel_multiplier=0,
                              allow_small_or_imprecise_dtypes=True))
            do(nc.gpsimd.memset(zrow[:], 0.0))
            do(nc.gpsimd.memset(zrow[:, C_ID:C_ID + 1].bitcast(I32), 1 << 20))
            pool.nop().then_inc(sem("e_consts"), 1)
            nc.gpsimd.dma_start(rows[E * REGION:E * REGION + P, :], zrow[:]).then_inc(sem("padded"), 16)
            pool.wait_ge(sem("pads_ready"), 1)
            for e in range(E):
                nc.gpsimd.indirect_dma_start(
                    out=rows, out_offset=bass.IndirectOffsetOnAxis(ap=pads[:, e:e + 1], axis=0),
                    in_=zrow[:], in_offset=None).then_inc(sem("padded"), 16)
            pool.wait_ge(sem("e_max"), 1)
            nc.gpsimd.partition_all_reduce(mx[:], mx[:], P, bass.bass_isa.ReduceOp.max).then_inc(sem("e_max_all"), 1)
            pool.wait_ge(sem("padded"), 16 * (E + 1))

        order = [(e, k) for e in range(E) for k in range(KT)]

        @blk.tensor
        def _(pe):
            for n, (e, k) in enumerate(order):
                pe.wait_ge(sem(f"e_in{e}"), 16)
                if n >= NBK:
                    pe.wait_ge(sem("e_lo"), n - NBK + 1)
                for f in range(KT):
                    ins = nc.tensor.transpose(bank[n % NBK][:, f * P:(f + 1) * P], er[:, e, f, k * P:(k + 1) * P],
                                              ident[:])
                ins.then_inc(sem("e_transposed"), 1)

        @blk.scalar
        def _(act):
            act.wait_ge(sem("e_scale"), 1)
            for n, (e, k) in enumerate(order):
                act.wait_ge(sem("e_transposed"), n + 1)
                nc.scalar.activation(e_w[0][:, e, k, :], bank[n % NBK][:, :], ACT.Identity,
                                     scale=scl[:, S_E:S_E + 1]).then_inc(sem("e_hi"), 1)

        @blk.vector
        def _(dve):
            do = steps(dve, "dve_experts")
            dve.wait_ge(sem("e_consts"), 1)
            do(nc.vector.tensor_scalar(padf[:], base[:], row_p[:], None, ALU.add))
            nc.vector.tensor_copy(pads[:], padf[:]).then_inc(sem("pads_ready"), 1)
            do(nc.vector.tensor_tensor(ntf[:], base[:], region[:], ALU.subtract))
            do(nc.vector.tensor_scalar(ntf[:], ntf[:], float(P - 1), None, ALU.add))
            do(nc.vector.tensor_copy(nti[:], ntf[:]))
            do(nc.vector.tensor_scalar(nti[:], nti[:], 7, None, ALU.logical_shift_right))
            do(nc.vector.tensor_copy(ntf[:], nti[:]))
            do(nc.vector.tensor_copy(cum[:], ntf[:]))
            for e in range(1, E):
                do(nc.vector.tensor_tensor(cum[:, e:e + 1], cum[:, e:e + 1], cum[:, e - 1:e], ALU.add))
            do(nc.vector.tensor_scalar(jump[:], ntf[:], -float(P), float(REGION), ALU.mult, ALU.add))
            do(nc.vector.tensor_scalar(start[:], tile[:], float(P), None, ALU.mult))
            do(nc.vector.memset(which[:], 0.0))
            for e in range(E):
                do(nc.vector.tensor_scalar(ge[:], tile[:], cum[:, e:e + 1], None, ALU.is_ge))
                do(nc.vector.tensor_tensor(which[:], which[:], ge[:], ALU.add))
                do(nc.vector.scalar_tensor_tensor(out=start[:], in0=ge[:], scalar=jump[:, e:e + 1], in1=start[:],
                                                  op0=ALU.mult, op1=ALU.add))
            do(nc.vector.tensor_scalar(start[:], start[:], float(E * REGION), None, ALU.min))
            do(nc.vector.tensor_scalar(which[:], which[:], float(E - 1), None, ALU.min))
            nc.vector.tensor_copy(tab[:, 0, :], start[:])
            do(nc.vector.tensor_copy(tab[:, 1, :], which[:]))
            for e in range(E):
                dve.wait_ge(sem(f"e_in{e}"), 16)
                ins = nc.vector.tensor_reduce(mxe[:, e:e + 1], er[:, e, :, :], mybir.AxisListType.XY, ALU.max,
                                              apply_absolute_value=True)
            do(ins)
            nc.vector.tensor_reduce(mx[:], mxe[:], X, ALU.max).then_inc(sem("e_max"), 1)
            dve.wait_ge(sem("e_max_all"), 1)
            c = slice(S_E, S_E + 1)
            do(nc.vector.tensor_scalar(mx[:], mx[:], 1e-25, None, ALU.max))
            do(nc.vector.tensor_scalar(inv[:, c].bitcast(I32), mx[:].bitcast(I32), 0x7F800000, None,
                                       ALU.bitwise_and))
            do(nc.vector.tensor_scalar(inv[:, c], inv[:, c], 1.0 / TOP, None, ALU.mult))
            nc.vector.reciprocal(scl[:, c], inv[:, c]).then_inc(sem("e_scale"), 1)
            dve.wait_ge(sem("e_scale"), 1)
            for n, (e, k) in enumerate(order):
                dve.wait_ge(sem("e_hi"), n + 1)
                nc.vector.scalar_tensor_tensor(out=e_w[1][:, e, k, :], in0=bank[n % NBK][:, :], scalar=scl[:, c],
                                               in1=e_w[0][:, e, k, :], op0=ALU.mult, op1=ALU.subtract)\
                    .then_inc(sem("e_lo"), 1)

    with ExitStack() as st:
        def sp_(name, shape, dt=F32):
            return sb(name, shape, dt, st)
        U = UNROLL
        row = sp_("row", [P, U, ROW])
        xn2 = sp_("xn2", [P, U, DM])
        x2T = [sp_(f"x2T_{s}", [P, 2, KT, P], F16) for s in ("hi", "lo")]
        res = sp_("res", [P, U, DM])
        tbank = [st.enter_context(nc.psum_tensor(f"mt{i}", [P, 512], F32)) for i in range(2)]
        obank2 = [st.enter_context(nc.psum_tensor(f"mo{i}", [P, 512], F32)) for i in range(2)]
        blk = st.enter_context(nc.Block())
        assert NTILE % U == 0

        def tiles(eng, body):
            with eng.Fori(0, NTILE // U - 1) as k:
                for u in range(U):
                    body(k * U + u, k, u)
            for u in range(U):
                body(NTILE - U + u, NTILE // U - 1, u)

        def has(t):
            return not isinstance(t, int) or t < NTILE

        @blk.sync
        def _(sp):
            def load(t, u):
                first = sp.value_load(tab[0:1, 0, bass.ds(t, 1)], min_val=0, max_val=E * REGION)
                sp.dma_start(row[:, u, :], rows[bass.ds(first, P), :]).then_inc(sem(f"row_in{u}"), 16)

            for u in range(U):
                load(u, u)
            with sp.Fori(1, NTILE // U) as k:
                for u in range(U):
                    sp.wait_ge(sem(f"out{u}"), 16 * k)
                    load(k * U + u, u)

        @blk.gpsimd
        def _(pool):
            def add(t, u):
                wait_alone(pool, "xn2_ready", t + 1)
                nc.gpsimd.tensor_tensor(row[:, u, 0:DM], row[:, u, 0:DM], xn2[:, u, :], ALU.add)\
                    .then_inc(sem("sum_ready"), 1)

            def body(t, k, u):
                if has(t + 1):
                    add(t + 1, (u + 1) % U)
                wait_alone(pool, "res_ready", t + 1 + 2)
                nc.gpsimd.indirect_dma_start(
                    out=out_rows, out_offset=bass.IndirectOffsetOnAxis(ap=row[:, u, C_ID:C_ID + 1].bitcast(I32), axis=0),
                    in_=res[:, u, :], in_offset=None, bounds_check=NTOK - 1, oob_is_err=False)\
                    .then_inc(sem(f"out{u}"), 16)

            add(0, 0)
            tiles(pool, body)
            for u in range(U):
                wait_alone(pool, f"out{u}", 16 * (NTILE // U))

        @blk.tensor
        def _(pe):
            HL = ((0, 0), (1, 0), (0, 1))

            def tr(t, u):
                pe.wait_ge(sem("xn2_ready"), t + 1)
                pe.wait_ge(sem("t_used"), t + 1)
                for k in range(KT):
                    ins = nc.tensor.transpose(tbank[u % 2][:, k * P:(k + 1) * P], xn2[:, u, k * P:(k + 1) * P],
                                              ident[:])
                ins.then_inc(sem("t_filled"), 1)

            def mm(t, u):
                e = pe.value_load(tab[0:1, 1, bass.ds(t, 1)], min_val=0, max_val=E - 1)
                pe.wait_ge(sem("t_used"), t + 1 + 2)
                pe.wait_ge(sem("res_ready"), t + 1)
                for k in range(KT):
                    for n, (ia, ib) in enumerate(HL):
                        w = e_w[ib][:, bass.ds(e, 1), k, :].rearrange("p a n -> p (a n)")
                        ins = nc.tensor.matmul(obank2[u % 2][:, :], x2T[ia][:, u % 2, k, :], w,
                                               start=k == 0 and n == 0, stop=k == KT - 1 and n == 2)
                ins.then_inc(sem("o_filled"), 1)

            def body(t, k, u):
                if has(t + 1):
                    tr(t + 1, (u + 1) % U)
                mm(t, u)

            tr(0, 0)
            tiles(pe, body)

        @blk.scalar
        def _(act):
            act.nop().then_inc(sem("o_filled"), 2)

            def body(t, k, u):
                act.wait_ge(sem("t_filled"), t + 1)
                act.wait_ge(sem("o_filled"), t + 1)
                nc.scalar.activation(x2T[0][:, u % 2, :, :], tbank[u % 2][:, :].rearrange("p (k n) -> p k n", k=KT),
                                     ACT.Copy).then_inc(sem("t_hi"), 1)

            tiles(act, body)

        @blk.vector
        def _(dve):
            dve.nop().then_inc(sem("t_used"), 2)
            dve.nop().then_inc(sem("res_ready"), 2)

            def norm(t, loads, u):
                dve.wait_ge(sem(f"row_in{u}"), 16 * loads)
                nc.vector.tensor_scalar(xn2[:, u, :], row[:, u, 0:DM], row[:, u, C_RSTD:C_RSTD + 1],
                                        row[:, u, C_NMR:C_NMR + 1], ALU.mult, ALU.add).then_inc(sem("xn2_ready"), 1)

            def lo(t, u):
                dve.wait_ge(sem("t_hi"), t + 1)
                nc.vector.tensor_tensor(x2T[1][:, u % 2, :, :], tbank[u % 2][:, :].rearrange("p (k n) -> p k n", k=KT),
                                        x2T[0][:, u % 2, :, :], ALU.subtract).then_inc(sem("t_used"), 1)

            def body(t, k, u):
                if has(t + 2):
                    norm(t + 2, k + (u + 2) // U + 1, (u + 2) % U)
                if has(t + 1):
                    lo(t + 1, (u + 1) % U)
                dve.wait_ge(sem("o_filled"), t + 1 + 2)
                dve.wait_ge(sem("sum_ready"), t + 1)
                nc.vector.scalar_tensor_tensor(out=res[:, u, :], in0=obank2[u % 2][:, :], scalar=inv[:, S_E:S_E + 1],
                                               in1=row[:, u, 0:DM], op0=ALU.mult, op1=ALU.add)\
                    .then_inc(sem("res_ready"), 1)

            norm(0, 1, 0)
            norm(1, 1, 1)
            lo(0, 0)
            tiles(dve, body)
    es.close()


_INS = ['x', 'ctx_512', 'L0_xattn_Wq', 'L0_xattn_bq', 'L0_xattn_Wk', 'L0_xattn_bk', 'L0_xattn_Wv', 'L0_xattn_bv',
        'L0_xattn_Wo', 'L0_xattn_bo', 'L0_ffn_gate_w', 'L0_ffn_expert_w']


def kernel(**inputs):
    import numpy as _np
    import concourse.bacc as _bacc
    from concourse.bass_utils import run_bass_kernel_spmd as _run

    nc = _bacc.Bacc("TRN2", target_bir_lowering=False, num_devices=1)
    arrays, args = {}, []
    for name in _INS:
        a = _np.ascontiguousarray(inputs[name])
        arrays[f"in_{name}"] = a
        args.append(nc.dram_tensor(f"in_{name}", a.shape, mybir.dt.from_np(a.dtype), kind="ExternalInput").ap())
    args.append(nc.dram_tensor("out_0", (B, LQ, DM), F32, kind="ExternalOutput").ap())
    build(nc, *args)
    r = _run(nc, [arrays], core_ids=[0])
    return _np.asarray(r.results[0]["out_0"])
```

```python
from contextlib import ExitStack

import concourse.bass as bass

from concourse import mybir

F32, F32R, F16, BF16, I32 = (mybir.dt.float32, mybir.dt.float32r, mybir.dt.float16,
                             mybir.dt.bfloat16, mybir.dt.int32)
ALU = mybir.AluOpType
ACT = mybir.ActivationFunctionType
X = mybir.AxisListType.X

P = 128
B, LQ, DM = 4, 2048, 512
LK, DC = 77, 256
H = 16
DK = DM // H
E = 8
EPS = 1e-5
KT = DM // P
CT = DC // P
HG = P // DK
TPC = 4
CH = TPC * P
NCHUNK = B * LQ // CH
CPB = NCHUNK // B
NC = 3
PK = -(-HG * LK // NC)
KC = HG * LK
KCP = NC * PK
VC = DK + 1
NTOK = B * LQ
REGION = NTOK + P
ROW = DM + 3
C_RSTD, C_NMR, C_ID = DM, DM + 1, DM + 2
NTILE = NTOK // P + E
UNROLL = 8
EPRE = 3
E_PASS = [*range(EPRE, E), *range(EPRE)]
SCALE = 1.0 / float(DK) ** 0.5
TOP = 16384.0

def order(text):
    names = [(w.rstrip("0123456789"), w) for w in text.split()]
    return [(kind, *(int(d) for d in w[len(kind):])) for kind, w in names]


STEPS = order("""
    T0 NM T1 C0 C1 S0 T2 T3 S1 C2 C3 Q0 Q1 O0 M00 M01 PV0 M02 S2 GC M03 Q2 PV1 R M10 S3 M11
    M12 Q3 M20 O1 M21 M13 PV2 M22 O2 M30 PV3 M23 M31 O3 M32 GX M33
""")
VECTOR = order("""
    T0 NM T1 C0 C1 L0 L1 P00 L2 T2 T3 C2 P01 C3 P02 P10 P11 Q0 K0 Q1 P12 L3 O0 V00 V01 B0 LE
    M00 P20 M01 M02 GC M03 K1 P21 H Q2 R V10 M10 P22 K2 P30 M11 M12 V11 SL P31 Q3 M20 P32 O1
    M21 B1 M13 M22 K3 V20 V21 O2 M30 M23 B2 V30 V31 M31 O3 M32 B3 GX M33 VE
""")
SCALAR = order("""
    T0 T1 C0 C1 S0 T2 T3 C2 C3 S1 Q0 Q1 S2 X0 Q2 S3 X1 Q3 X2 X3
""")
K_ORDER = [s[1] for s in VECTOR if s[0] == "K"]
FRONT, CORE, TAIL = {"T", "Q", "M", "GX"}, {"NM", "S", "PV", "P", "V", "K"}, {"C", "O", "GC", "R", "B", "H", "VE", "SL"}
NEXT = {"X", "L", "LE"}
BANKED = {"T", "C", "NM", "Q", "M", "O", "GX", "GC", "R"}
SPLIT = {"T", "C", "Q"}
WB = 3


def steps_of(front, core, tail, new=False, table=STEPS):
    return [s for s in table if (s[0] in FRONT and front) or (s[0] in CORE and core) or (s[0] in TAIL and tail)
            or (s[0] in NEXT and new)]


assert STEPS[-1] == ("M", KT - 1, TPC - 1)
for _kinds, _table in ((BANKED, VECTOR), (SPLIT, SCALAR)):
    assert [s for s in STEPS if s[0] in _kinds] == [s for s in _table if s[0] in _kinds]


class Chunk:

    def __init__(self, b, c):
        self.b, self.c = b, c

    def plus(self, k):
        return Chunk(self.b, self.c + k)

    @property
    def static(self):
        return isinstance(self.b, int)

    @property
    def n(self):
        return self.b * CPB + self.c

    @property
    def slot(self):
        return self.c % CPB

    @property
    def batch(self):
        return self.b + self.c // CPB

    def is_(self, k):
        return self.static and self.n == k

    def steps(self, table=STEPS):
        i = self.n if self.static else 1
        return steps_of(i < NCHUNK - 1, 0 <= i < NCHUNK, i >= 1, i < NCHUNK - 2, table)

    def number(self, what, kinds):
        own = [s for s in self.steps() if s[0] in kinds]
        first, second, full = (len([s for s in steps_of(*p) if s[0] in kinds])
                               for p in ((True, False, False), (True, True, False), (True, True, True)))
        k = own.index(what)
        if self.is_(-1):
            return k
        if self.is_(0):
            return first + k
        if self.is_(NCHUNK):
            before = len([s for s in steps_of(False, True, True) if s[0] in kinds])
            return first + second + full * (NCHUNK - 2) + before + k
        return (self.n - 1) * full + (first + second + k)


def build(nc, x, ctx, Wq, bq, Wk, bk, Wv, bv, Wo, bo, gate_w, expert_w, out):
    es = ExitStack()
    sems = {}

    def sb(name, shape, dt=F32, stack=es):
        return stack.enter_context(nc.sbuf_tensor(name, shape, dt))

    def sem(name):
        if name not in sems:
            sems[name] = es.enter_context(nc.semaphore(name))
        return sems[name]

    def wait_alone(eng, name, value):
        eng.wait_ge(sem(name), value)
        eng.sem_inc(sem("waited_alone"))

    def steps(eng, name):
        n = [0]

        def do(ins):
            n[0] += 1
            ins.then_inc(sem(name), 1)
            eng.wait_ge(sem(name), n[0])
        return do

    rows = nc.dram_tensor("rows_by_expert", [E * REGION + P, ROW], F32)
    rows = rows.ap()
    out_rows = out.rearrange("b s d -> (b s) d")

    ident = sb("ident", [P, P])
    base = sb("base", [P, E])
    inv = sb("inv", [P, 8])
    scl = sb("scl", [P, 8])
    S_WQ, S_WO, S_G, S_V, S_WG, S_E = range(6)
    er_pre = sb("er_pre", [P, EPRE, KT, DM])
    e_sum = sb("e_sum", [P, E])
    pows = sb("pows", [P, 2, TPC])
    pay = sb("pay", [P, 2, TPC, ROW])
    mv2 = sb("mv2", [P, TPC, 2])
    ve2 = sb("ve2", [P, TPC])
    slot = sb("slot", [P, 2, TPC], I32)
    attention = ExitStack()

    def sa(name, shape, dt=F32):
        return sb(name, shape, dt, attention)

    wq = [sa(f"wq_{s}", [P, KT, DM], F16) for s in ("hi", "lo")]
    wo = [sa(f"wo_{s}", [P, KT, DM], F16) for s in ("hi", "lo")]
    gt = [sa(f"gate_{s}", [P, KT, E], F16) for s in ("hi", "lo")]
    wg = [sa(f"wogate_{s}", [P, KT, E], F16) for s in ("hi", "lo")]
    k_all = [sa(f"k_all_{s}", [P, B, KT, LK], F32R) for s in ("hi", "lo")]
    k_cur = [sa(f"k_cur_{s}", [P, KT, KCP], F32R) for s in ("hi", "lo")]
    v_all = [sa(f"v_all_{s}", [PK, B, KT, NC, 2 * VC], F16) for s in ("hi", "lo")]
    mask_k = sa("mask_k", [P, HG])
    sel = sa("sel", [P, KT, KCP], F32R)
    tri = sa("tri", [P, P], BF16)
    ones = sa("ones", [P, P], BF16)
    bo_rep = sa("bo_rep", [P, DM])
    bq_s = sa("bq_s", [P, KT])
    gate_c = sa("gate_c", [P, E])
    exp_scale = sa("exp_scale", [P, 1])
    inv_y = sa("inv_y", [P, 1])
    inv_gc = sa("inv_gc", [P, 1])
    weight8 = sa("weight8", [P, E])
    token = sa("token", [P, TPC])
    xt = sa("xt", [P, CPB, TPC, DM])
    xn = sa("xn", [P, TPC, DM])
    bst = sa("bst", [P, TPC, 6])
    mv = sa("mv", [P, TPC, 2])
    ve = sa("ve", [P, TPC])
    rstd = sa("rstd", [P, TPC])
    std = sa("std", [P, 2, TPC])
    nmr = sa("nmr", [P, TPC])
    negmax = sa("negmax", [P, TPC, P])
    xv = x.rearrange("b (c t p) d -> (b c) p t d", t=TPC, p=P)

    def row_factors(m, pool, do):
        par = m.slot % 2
        wait_alone(pool, "ln2_stats", m.n + 1)
        do(nc.gpsimd.tensor_tensor(pay[:, par, :, C_RSTD], ve2[:], pows[:, 0, :], ALU.pow))
        do(nc.gpsimd.tensor_tensor(mv2[:, :, 1], mv2[:, :, 0], pay[:, par, :, C_RSTD], ALU.mult))
        nc.gpsimd.tensor_scalar(pay[:, par, :, C_NMR], mv2[:, :, 1], -1.0, None, ALU.mult)\
            .then_inc(sem("pay_stats"), 1)

    def scatter(m, pool):
        par = m.slot % 2
        wait_alone(pool, "slot_ready", m.n + 1)
        wait_alone(pool, "pay_stats", m.n + 2)
        for t in range(TPC):
            nc.gpsimd.indirect_dma_start(
                out=rows, out_offset=bass.IndirectOffsetOnAxis(ap=slot[:, par, t:t + 1], axis=0),
                in_=pay[:, par, t, :], in_offset=None).then_inc(sem("scattered"), 16)

    def build_k(b, g):
        for s_ in (0, 1):
            src = k_all[s_][:, bass.ds(b, 1), g, :].bitcast(F32).rearrange("p a s -> p (a s)")\
                .unsqueeze(1).to_broadcast([P, HG, LK])
            ins = nc.vector.tensor_tensor(
                k_cur[s_][:, g, 0:KC].rearrange("p (j s) -> p j s", j=HG), src,
                mask_k[:].unsqueeze(2).to_broadcast([P, HG, LK]), ALU.mult)
        ins.then_inc(sem("k_built"), 1)

    with ExitStack() as st:
        def sp_(name, shape, dt=F32):
            return sb(name, shape, dt, st)
        wraw = {n: sp_("raw_" + n, [P, KT, DM]) for n in ("q", "o")}
        craw = {n: sp_("raw_" + n, [P, CT, DM]) for n in ("k", "v")}
        cx = sp_("cx", [LK, B, DC])
        cxT = sp_("cxT", [P, CT, B, KCP])
        bvec = sp_("bvec", [P, 4, KT])
        BQ, BK, BO, BV = range(4)
        bmat = sp_("bmat", [P, 2, KT, P])
        g8 = sp_("g8", [E, DM])
        gmean = sp_("gmean", [E, 1])
        gc8 = sp_("gc8", [E, DM])
        gT = sp_("gT", [P, KT, E])
        woT = sp_("woT", [P, KT, DM])
        wgT = sp_("wgT", [E, DM])
        wgf = sp_("wgf", [P, KT, E])
        mask_v = sp_("mask_v", [PK, NC, 2])
        smask_v = sp_("smask_v", [PK, NC, 2])
        sel32 = sp_("sel32", [P, KT, KCP])
        mx = sp_("mx", [P, 8])
        M_CX, M_WV = 6, 7
        onesf = sp_("onesf", [P, P])
        NB = 8
        bank = [st.enter_context(nc.psum_tensor(f"prep{i}", [P, 512], F32)) for i in range(NB)]
        blk = st.enter_context(nc.Block())

        vs = [("v", b, c) for b in range(B) for c in range(NC)]
        uses = ([("cx", 0), ("cx", 1), ("g",)] + [("k", g) for g in range(KT)] + vs[:2]
                + [("wo", k) for k in range(KT)] + vs[2:5] + [("wgT",)] + vs[5:7] + [("wg",)] + vs[7:8] + [("bo",)]
                + vs[8:10] + [("gc",)] + vs[10:])
        by_act = [u for u in uses if u == ("cx", 1) or u[0] in ("k", "v", "wo", "wg")]
        by_dve = [u for u in uses if u != ("cx", 1) and u[0] != "wo"]

        def ready(eng, *u):
            if u in by_dve:
                eng.wait_ge(sem("prep_dve"), by_dve.index(u) + 1)
            else:
                eng.wait_ge(sem("prep_act"), by_act.index(u) + 1)

        def v_parts(c):
            return [(slice(d * VC, d * VC + DK), c + d) for d in range(2)]

        @blk.sync
        def _(sp):
            def load(dst, src, name):
                sp.dma_start(dst, src).then_inc(sem(name), 16)

            def by_feature(v):
                return v.rearrange("(t p) -> p t", p=P)

            load(cx[:], ctx.rearrange("b s d -> s b d"), "ld_cx")
            load(craw["k"][:], Wk.rearrange("(t p) n -> p t n", p=P), "ld_wk")
            load(craw["v"][:], Wv.rearrange("(t p) n -> p t n", p=P), "ld_wv")
            load(wraw["o"][:], Wo.rearrange("(t p) n -> p t n", p=P), "ld_wo")
            with nc.allow_non_contiguous_dma(reason="a few bias vectors by feature"):
                load(bvec[:, BV, :], by_feature(bv), "ld_bias")
                load(bvec[:, BO, :], by_feature(bo), "ld_bias")
                load(bvec[:, BQ, :], by_feature(bq), "ld_bias")
            load(wraw["q"][:], Wq.rearrange("(t p) n -> p t n", p=P), "ld_wq")
            load(bo_rep[:], bo.rearrange("(a n) -> a n", a=1).to_broadcast([P, DM]), "ld_bo_rep")
            for c in range(CPB):
                load(xt[:, c, :, :], xv[c], f"x_in{c}")
            for u in range(EPRE):
                load(er_pre[:, u, :, :], expert_w[E_PASS[u]].rearrange("(t p) h -> p t h", p=P), f"e_pre{u}")

        @blk.gpsimd
        def _(pool):
            do = steps(pool, "pool_prep")
            do(nc.gpsimd.memset(ident[:], 0.0))
            nc.gpsimd.affine_select(out=ident[:], in_=ident[:], compare_op=ALU.not_equal, fill=1.0, base=0,
                                    pattern=[[-1, P]], channel_multiplier=1).then_inc(sem("ident_ready"), 1)
            do(nc.gpsimd.memset(mask_v[:], 1.0))
            do(nc.gpsimd.affine_select(out=mask_v[:], in_=mask_v[:], compare_op=ALU.is_ge, fill=0.0, base=0,
                                       pattern=[[PK - LK, NC], [-LK, 2]], channel_multiplier=1))
            do(nc.gpsimd.affine_select(out=mask_v[:], in_=mask_v[:], compare_op=ALU.is_ge, fill=0.0, base=LK - 1,
                                       pattern=[[LK - PK, NC], [LK, 2]], channel_multiplier=-1))
            nc.gpsimd.memset(cxT[:, :, :, KC:KCP], 0.0).then_inc(sem("masks_ready"), 1)
            do(nc.gpsimd.memset(sel32[:], 0.0))
            nc.gpsimd.affine_select(out=sel32[:, :, 0:KC].rearrange("p g (j s) -> p g j s", j=HG),
                                    in_=sel32[:, :, 0:KC].rearrange("p g (j s) -> p g j s", j=HG),
                                    compare_op=ALU.not_equal, fill=1.0, base=0,
                                    pattern=[[-HG, KT], [-1, HG], [0, LK]], channel_multiplier=1)\
                .then_inc(sem("sel_ready"), 1)
            reductions = [(M_CX, M_WV + 1), (S_WO, S_G + 1), (S_WQ, S_WQ + 1)]

            def reduce_max():
                c0, c1 = reductions.pop(0)
                pool.wait_ge(sem("mx_in"), 3 - len(reductions))
                nc.gpsimd.partition_all_reduce(mx[:, c0:c1], mx[:, c0:c1], P, bass.bass_isa.ReduceOp.max)\
                    .then_inc(sem("mx_out"), 1)

            reduce_max()
            do(nc.gpsimd.memset(mask_k[:], 1.0))
            do(nc.gpsimd.affine_select(out=mask_k[:], in_=mask_k[:], compare_op=ALU.is_ge, fill=0.0, base=0,
                                       pattern=[[-DK, HG]], channel_multiplier=1))
            do(nc.gpsimd.affine_select(out=mask_k[:], in_=mask_k[:], compare_op=ALU.is_ge, fill=0.0, base=DK - 1,
                                       pattern=[[DK, HG]], channel_multiplier=-1))
            nc.gpsimd.memset(negmax[:], 0.0)
            pool.nop().then_inc(sem("mask_k_ready"), 1)
            dens = [v[:].rearrange("p b g c (d k) -> p (b g) c d k", d=2)[:, :, :, :, DK] for v in v_all]
            nc.gpsimd.tensor_copy(dens[0], mask_v[:].unsqueeze(1).to_broadcast([PK, B * KT, NC, 2]))
            nc.gpsimd.memset(dens[1], 0.0)
            do(nc.gpsimd.tensor_copy(sel[:], sel32[:]))
            reduce_max()
            do(nc.gpsimd.memset(onesf[:], 1.0))
            do(nc.gpsimd.affine_select(out=onesf[:], in_=onesf[:], compare_op=ALU.is_gt, fill=0.0, base=0,
                                       pattern=[[1, P]], channel_multiplier=-1))
            do(nc.gpsimd.tensor_copy(tri[:], onesf[:]))
            do(nc.gpsimd.memset(ones[:], 1.0))
            reduce_max()
            nc.gpsimd.memset(pows[:, 0, :], -0.5)
            do(nc.gpsimd.memset(pows[:, 1, :], 0.5))
            wait_alone(pool, "ln_stats", 1)
            nc.gpsimd.tensor_tensor(std[:, 0, :], ve[:], pows[:, 1, :], ALU.pow)
            do(nc.gpsimd.tensor_tensor(rstd[:], ve[:], pows[:, 0, :], ALU.pow))
            do(nc.gpsimd.tensor_tensor(nmr[:], mv[:, :, 0], rstd[:], ALU.mult))
            nc.gpsimd.tensor_scalar(nmr[:], nmr[:], -1.0, None, ALU.mult).then_inc(sem("factors_ready"), 1)
            do(nc.gpsimd.iota(base[:], pattern=[[REGION, E]], base=0, channel_multiplier=0,
                              allow_small_or_imprecise_dtypes=True))
            do(nc.gpsimd.iota(weight8[:], pattern=[[-1, E]], base=E, channel_multiplier=0,
                              allow_small_or_imprecise_dtypes=True))
            do(nc.gpsimd.iota(token[:], pattern=[[P, TPC]], base=0, channel_multiplier=1,
                              allow_small_or_imprecise_dtypes=True))

        @blk.tensor
        def _(pe):
            pe.wait_ge(sem("ident_ready"), 1)

            def sum_of(dst, pairs):
                for n, (a, b_) in enumerate(pairs):
                    ins = nc.tensor.matmul(dst, a, b_, start=n == 0, stop=n == len(pairs) - 1)
                return ins

            for n, (kind, *at) in enumerate(uses):
                if n >= NB:
                    ready(pe, *uses[n - NB])
                ps = bank[n % NB]
                if kind == "cx":
                    k, = at
                    pe.wait_ge(sem("ld_cx"), 16)
                    for b in range(B):
                        last = nc.tensor.transpose(ps[:, b * LK:(b + 1) * LK], cx[:, b, k * P:(k + 1) * P],
                                                   ident[0:LK, 0:LK])
                elif kind == "k":
                    g, = at
                    pe.wait_ge(sem("ld_wk"), 16)
                    ready(pe, "cx", 0)
                    ready(pe, "cx", 1)
                    last = sum_of(ps[:, 0:B * LK], [(craw["k"][:, k, g * P:(g + 1) * P], cxT[:, k, :, 0:LK])
                                                    for k in range(CT)])
                elif kind == "v":
                    b, c = at
                    pe.wait_ge(sem("ld_wv"), 16)
                    pe.wait_ge(sem("masks_ready"), 1)
                    last = sum_of(ps[0:PK, :], [(cxT[:, k, b, c * PK:(c + 1) * PK], craw["v"][:, k, :])
                                                for k in range(CT)])
                elif kind == "g":
                    pe.wait_ge(sem("gate_centred"), 1)
                    for k in range(KT):
                        last = nc.tensor.transpose(ps[:, k * E:(k + 1) * E], gc8[:, k * P:(k + 1) * P],
                                                   ident[0:E, 0:E])
                elif kind == "wo":
                    k, = at
                    pe.wait_ge(sem("ld_wo"), 16)
                    for f in range(KT):
                        last = nc.tensor.transpose(ps[:, f * P:(f + 1) * P], wraw["o"][:, f, k * P:(k + 1) * P],
                                                   ident[:])
                elif kind == "wgT":
                    ready(pe, "g")
                    ready(pe, "wo", KT - 1)
                    last = sum_of(ps[0:E, :], [(gT[:, k, :], woT[:, k, :]) for k in range(KT)])
                elif kind == "wg":
                    ready(pe, "wgT")
                    for k in range(KT):
                        last = nc.tensor.transpose(ps[:, k * E:(k + 1) * E], wgT[:, k * P:(k + 1) * P],
                                                   ident[0:E, 0:E])
                elif kind == "bo":
                    pe.wait_ge(sem("bmat_ready"), 1)
                    last = sum_of(ps[:, :], [(bmat[:, 1, k, :], wraw["o"][:, k, :]) for k in range(KT)])
                elif kind == "gc":
                    ready(pe, "wg")
                    last = sum_of(ps[:, 0:E], [(bmat[:, s, k, :], w[:, k, :]) for s, w in ((0, gT), (1, wgf))
                                               for k in range(KT)])
                last.then_inc(sem("prep_filled"), 1)

        @blk.scalar
        def _(act):
            act.dma_start(g8[:], gate_w).then_inc(sem("ld_gate"), 16)
            with nc.allow_non_contiguous_dma(reason="a bias vector by feature"):
                act.dma_start(bvec[:, BK, :], bk.rearrange("(t p) -> p t", p=P)).then_inc(sem("ld_bk"), 16)

            def scaled(dst, src, col):
                act.wait_ge(sem(f"scale{col}"), 1)
                return nc.scalar.activation(dst, src, ACT.Identity, scale=scl[:, col:col + 1])

            def filled(*u):
                act.wait_ge(sem("prep_filled"), uses.index(u) + 1)
                return bank[uses.index(u) % NB]

            for u in by_act:
                kind, *at = u
                ps = filled(*u)
                if kind == "cx":
                    last = nc.scalar.activation(
                        cxT[:, 1, :, 0:KC].rearrange("p b (j s) -> p b j s", j=HG),
                        ps[:, 0:B * LK].rearrange("p (b s) -> p b s", b=B).unsqueeze(2)
                        .to_broadcast([P, B, HG, LK]), ACT.Copy)
                elif kind == "k":
                    g, = at
                    act.wait_ge(sem("ld_bk"), 16)
                    last = nc.scalar.activation(k_all[0][:, :, g, :],
                                                ps[:, 0:B * LK].rearrange("p (b s) -> p b s", b=B), ACT.Identity,
                                                bias=bvec[:, BK, g:g + 1])
                elif kind == "v":
                    b, c = at
                    act.wait_ge(sem("smask_ready"), 1)
                    for d, (cols, j) in enumerate(v_parts(c)):
                        src = ps[0:PK, :].rearrange("p (g j k) -> p g j k", g=KT, j=HG)[:, :, j, :]
                        last = nc.scalar.activation(v_all[0][:, b, :, c, cols], src, ACT.Identity,
                                                    scale=smask_v[:, c, d:d + 1])
                elif kind == "wo":
                    last = nc.scalar.activation(woT[:, at[0], :], ps[:, :], ACT.Copy)
                elif kind == "wg":
                    nc.scalar.activation(wgf[:].rearrange("p k e -> p (k e)"), ps[:, 0:KT * E], ACT.Copy)
                    last = scaled(wg[0][:].rearrange("p k e -> p (k e)"), ps[:, 0:KT * E], S_WG)
                last.then_inc(sem("prep_act"), 1)
                if u == ("k", KT - 1):
                    act.wait_ge(sem("ld_bias"), 3 * 16)
                    nc.scalar.activation(bmat[:], bvec[:, BO:BV + 1, :].unsqueeze(3).to_broadcast([P, 2, KT, P]),
                                         ACT.Copy).then_inc(sem("bmat_ready"), 1)
                if u == vs[4]:
                    scaled(wo[0][:], wraw["o"][:], S_WO).then_inc(sem("wo_hi"), 1)
                if u == vs[6]:
                    scaled(wq[0][:], wraw["q"][:], S_WQ).then_inc(sem("wq_hi"), 1)
                if u == vs[-3]:
                    act.wait_ge(sem("factors_ready"), 1)
                    for t in range(TPC):
                        nc.scalar.activation(xn[:, t, :], xt[:, 0, t, :], ACT.Identity, scale=rstd[:, t:t + 1],
                                             bias=nmr[:, t:t + 1]).then_inc(sem("xn_ready"), 1)

        @blk.vector
        def _(dve):
            do = steps(dve, "dve_prep")
            XY = mybir.AxisListType.XY

            def scales(c):
                col = slice(c, c + 1)
                do(nc.vector.tensor_scalar(mx[:, col], mx[:, col], 1e-25, None, ALU.max))
                do(nc.vector.tensor_scalar(inv[:, col].bitcast(I32), mx[:, col].bitcast(I32), 0x7F800000, None,
                                           ALU.bitwise_and))
                do(nc.vector.tensor_scalar(inv[:, col], inv[:, col], 1.0 / TOP, None, ALU.mult))
                do(nc.vector.reciprocal(scl[:, col], inv[:, col]))
                dve.sem_inc(sem(f"scale{c}"))

            def bound(c, a, b, terms):
                do(nc.vector.tensor_tensor(mx[:, c:c + 1], mx[:, a:a + 1], mx[:, b:b + 1], ALU.mult))
                do(nc.vector.tensor_scalar(mx[:, c:c + 1], mx[:, c:c + 1], float(terms), None, ALU.mult))

            def absmax(col, src, rows=P):
                return nc.vector.tensor_reduce(mx[0:rows, col:col + 1], src, XY, ALU.max,
                                               apply_absolute_value=True)

            def lo(dst, src, scale, hi):
                return nc.vector.scalar_tensor_tensor(out=dst, in0=src, scalar=scale, in1=hi, op0=ALU.mult,
                                                      op1=ALU.subtract)

            do(nc.vector.memset(mx[:], 0.0))
            dve.wait_ge(sem("ld_gate"), 16)
            do(nc.vector.tensor_reduce(gmean[:], g8[:], X, ALU.add))
            do(nc.vector.tensor_scalar(gmean[:], gmean[:], 1.0 / DM, None, ALU.mult))
            nc.vector.tensor_scalar(gc8[:], g8[:], gmean[:, 0:1], None, ALU.subtract).then_inc(sem("gate_centred"), 1)

            def after_cx():
                dve.wait_ge(sem("ld_cx"), 16)
                absmax(M_CX, cx[:], LK)
                dve.wait_ge(sem("ld_wv"), 16)
                absmax(M_WV, craw["v"][:]).then_inc(sem("mx_in"), 1)

            def before_k():
                absmax(S_G, gT[:])

            def before_v():
                dve.wait_ge(sem("mx_out"), 1)
                bound(S_V, M_CX, M_WV, DC)
                scales(S_V)
                dve.wait_ge(sem("masks_ready"), 1)
                nc.vector.tensor_scalar(smask_v[:], mask_v[:], scl[0:PK, S_V:S_V + 1], None, ALU.mult)\
                    .then_inc(sem("smask_ready"), 1)
                dve.wait_ge(sem("smask_ready"), 1)
                dve.wait_ge(sem("ld_wo"), 16)
                absmax(S_WO, wraw["o"][:]).then_inc(sem("mx_in"), 1)

            def wq_max():
                dve.wait_ge(sem("ld_wq"), 16)
                absmax(S_WQ, wraw["q"][:]).then_inc(sem("mx_in"), 1)
                dve.wait_ge(sem("mx_out"), 2)
                scales(S_WO)
                scales(S_G)
                bound(S_WG, S_WO, S_G, DM)
                scales(S_WG)
                dve.wait_ge(sem("mx_out"), 3)
                scales(S_WQ)

            def wo_lo():
                dve.wait_ge(sem("wo_hi"), 1)
                lo(wo[1][:], wraw["o"][:], scl[:, S_WO:S_WO + 1], wo[0][:])

            def wq_lo():
                dve.wait_ge(sem("wq_hi"), 1)
                lo(wq[1][:], wraw["q"][:], scl[:, S_WQ:S_WQ + 1], wq[0][:])

            def gate_split():
                do(nc.vector.tensor_scalar(gt[0][:], gT[:], scl[:, S_G:S_G + 1], None, ALU.mult))
                lo(gt[1][:], gT[:], scl[:, S_G:S_G + 1], gt[0][:])
                nc.vector.tensor_scalar(bq_s[:], bvec[:, BQ, :], scl[:, S_WQ:S_WQ + 1], None, ALU.mult)
                nc.vector.tensor_scalar(exp_scale[:], inv[:, S_WQ:S_WQ + 1], SCALE, None, ALU.mult)
                nc.vector.tensor_tensor(inv_y[:], inv[:, S_WO:S_WO + 1], inv[:, S_V:S_V + 1], ALU.mult)
                nc.vector.tensor_tensor(inv_gc[:], inv[:, S_WG:S_WG + 1], inv[:, S_V:S_V + 1], ALU.mult)

            def k_pads():
                dve.wait_ge(sem("sel_ready"), 1)
                for s in (0, 1):
                    nc.vector.tensor_scalar(k_cur[s][:, :, KC:KCP], sel32[:, :, KC:KCP], 0.0, None, ALU.mult)

            def chunk_0():
                dve.wait_ge(sem("x_in0"), 16)
                for t in range(TPC):
                    last = nc.vector.bn_stats(bst[:, t, :], xt[:, 0, t, :])
                do(last)
                for t in range(TPC):
                    last = nc.vector.bn_aggr(mv[:, t, :], bst[:, t, :])
                do(last)
                nc.vector.tensor_scalar(ve[:], mv[:, :, 1], EPS, None, ALU.add).then_inc(sem("ln_stats"), 1)

            def keys_0():
                dve.wait_ge(sem("mask_k_ready"), 1)
                dve.wait_ge(sem("prep_dve"), by_dve.index(("k", KT - 1)) + 1)
                for g in K_ORDER:
                    build_k(0, g)

            jobs = {("cx", 0): after_cx, ("g",): before_k, ("k", KT - 1): before_v, vs[1]: wq_max, vs[4]: gate_split,
                    vs[6]: chunk_0,
                    vs[7]: wo_lo, vs[8]: wq_lo, vs[9]: k_pads, vs[10]: keys_0}
            for u in by_dve:
                kind, *at = u
                dve.wait_ge(sem("prep_filled"), uses.index(u) + 1)
                if u in by_act:
                    dve.wait_ge(sem("prep_act"), by_act.index(u) + 1)
                ps = bank[uses.index(u) % NB]
                if kind == "cx":
                    last = nc.vector.tensor_copy(
                        cxT[:, 0, :, 0:KC].rearrange("p b (j s) -> p b j s", j=HG),
                        ps[:, 0:B * LK].rearrange("p (b s) -> p b s", b=B).unsqueeze(2)
                        .to_broadcast([P, B, HG, LK]))
                elif kind == "g":
                    last = nc.vector.tensor_copy(gT[:].rearrange("p k e -> p (k e)"), ps[:, 0:KT * E])
                elif kind == "k":
                    g, = at
                    last = nc.vector.scalar_tensor_tensor(
                        out=k_all[1][:, :, g, :], in0=ps[:, 0:B * LK].rearrange("p (b s) -> p b s", b=B),
                        scalar=bvec[:, BK, g:g + 1], in1=k_all[0][:, :, g, :].bitcast(F32), op0=ALU.add,
                        op1=ALU.subtract)
                elif kind == "v":
                    b, c = at
                    for d, (cols, j) in enumerate(v_parts(c)):
                        src = ps[0:PK, :].rearrange("p (g j k) -> p g j k", g=KT, j=HG)[:, :, j, :]
                        last = lo(v_all[1][:, b, :, c, cols], src, smask_v[:, c, d:d + 1], v_all[0][:, b, :, c, cols])
                elif kind == "wgT":
                    last = nc.vector.tensor_copy(wgT[:], ps[0:E, :])
                elif kind == "wg":
                    last = lo(wg[1][:].rearrange("p k e -> p (k e)"), ps[:, 0:KT * E], scl[:, S_WG:S_WG + 1],
                              wg[0][:].rearrange("p k e -> p (k e)"))
                elif kind == "bo":
                    dve.wait_ge(sem("ld_bo_rep"), 16)
                    last = nc.vector.tensor_tensor(bo_rep[:], ps[:, :], bo_rep[:], ALU.add)
                elif kind == "gc":
                    last = nc.vector.tensor_copy(gate_c[:], ps[:, 0:E])
                last.then_inc(sem("prep_dve"), 1)
                if u in jobs:
                    if u == ("g",):
                        dve.wait_ge(sem("prep_dve"), by_dve.index(u) + 1)
                    jobs[u]()

    with ExitStack() as st:
        def sp_(name, shape, dt=F32):
            return sb(name, shape, dt, st)
        xnT = [sp_(f"xnT_{s}", [P, KT, CH], F16) for s in ("hi", "lo")]
        q = [sp_(f"q_{s}", [P, KT, CH], F32R) for s in ("hi", "lo")]
        nmT = sp_("nmT", [P, CH], F32R)
        pf = sp_("pf", [PK, 2, NC, CH])
        pp = [sp_(f"p_{s}", [PK, 2, NC, CH], F16) for s in ("hi", "lo")]
        den = sp_("den", [P, 2, 2, HG])
        cc = sp_("cc", [P, TPC, DM])
        cT = [sp_(f"cT_{s}", [P, KT, CH], F16) for s in ("hi", "lo")]
        bst2 = sp_("bst2", [P, TPC, 6])
        gx = sp_("gx", [P, CPB, TPC, E])
        lg = sp_("lg", [P, TPC, E])
        lmax = sp_("lmax", [P, TPC])
        oh = sp_("oh", [P, TPC, E], BF16)
        slotf = sp_("slotf", [P, TPC])
        sbank = [st.enter_context(nc.psum_tensor(f"scoresT{c}", [P, 512], F32)) for c in range(NC)]
        obank = [st.enter_context(nc.psum_tensor(f"pv{c}", [P, 512], F32)) for c in range(2)]
        wbank = [st.enter_context(nc.psum_tensor(f"work{c}", [P, 512], F32)) for c in range(WB)]
        blk = st.enter_context(nc.Block())

        full = steps_of(True, True, True)
        assert len([st_ for st_ in full if st_[0] in BANKED]) % WB == 0

        def use(i, *what):
            return i.number(what, BANKED)

        def bank_of(i, *what):
            j = i if i.static else Chunk(0, 1)
            return wbank[j.number(what, BANKED) % WB]

        def iterations(eng, iteration):
            iteration(Chunk(0, -1))
            iteration(Chunk(0, 0))
            with eng.Fori(0, B - 1) as b:
                for c in range(CPB):
                    iteration(Chunk(b, c + 1))
            for c in range(CPB):
                iteration(Chunk(B - 1, c + 1))

        def has_ln(i):
            return not i.static or i.n + 2 < NCHUNK

        class OwnCount:

            def __init__(self, per):
                self.per, self.before, self.done = per, 0, 0

            def begin(self, i):
                if not i.static:
                    if i.c == 1:
                        self.before += self.done
                    else:
                        assert self.done == self.per, self.done
                    self.base = (i.n - 1) * self.per + self.before
                else:
                    self.before += self.done + (self.per * (CPB * (B - 1) - 1) if i.n == NCHUNK - 3 else 0)
                    self.base = self.before
                self.done = 0

            def value(self):
                return self.base + self.done

        @blk.sync
        def _(sp):
            for n in range(EPRE, E):
                sp.wait_ge(sem("e_summed"), n - EPRE + 1)
                sp.dma_start(er_pre[:, n % EPRE, :, :], expert_w[E_PASS[n]].rearrange("(t p) h -> p t h", p=P))\
                    .then_inc(sem(f"e_pre{n % EPRE}"), 16)
            with sp.Fori(0, B - 1) as b:
                for c in range(CPB):
                    m = Chunk(b, c)
                    sp.wait_ge(sem("work_used"), use(m.plus(1), "O", TPC - 1) + 1)
                    sp.dma_start(xt[:, m.slot, :, :],
                                 xv[bass.ds(m.plus(CPB).n, 1), :, :, :].rearrange("a p t d -> p (a t) d"))\
                        .then_inc(sem(f"x_in{c}"), 16)

        @blk.gpsimd
        def _(pool):
            own = OwnCount(4)

            def do(ins):
                own.done += 1
                ins.then_inc(sem("pool_step"), 1)
                wait_alone(pool, "pool_step", own.value())

            def ln(n):
                wait_alone(pool, "ln_stats", n.n + 1)
                if not n.is_(0):
                    wait_alone(pool, "xn_ready", TPC * n.n)
                nc.gpsimd.tensor_tensor(std[:, n.slot % 2, :], ve[:], pows[:, 1, :], ALU.pow)
                do(nc.gpsimd.tensor_tensor(rstd[:], ve[:], pows[:, 0, :], ALU.pow))
                do(nc.gpsimd.tensor_tensor(nmr[:], mv[:, :, 0], rstd[:], ALU.mult))
                nc.gpsimd.tensor_scalar(nmr[:], nmr[:], -1.0, None, ALU.mult).then_inc(sem("factors_ready"), 1)

            def iteration(i):
                own.begin(i)
                if i.is_(-1):
                    ln(Chunk(0, 1))
                    return
                if has_ln(i):
                    ln(i.plus(2))
                if not i.is_(NCHUNK):
                    if not has_ln(i):
                        wait_alone(pool, "xn_ready", TPC * (i.n + 1))
                    for t in range(TPC):
                        nc.gpsimd.tensor_tensor(xt[:, i.slot, t, :], xt[:, i.slot, t, :], bo_rep[:], ALU.add)\
                            .then_inc(sem("x_plus_bo"), 1)
                if i.is_(0):
                    return
                m = i.plus(-1)
                if i.is_(NCHUNK):
                    return
                row_factors(m, pool, do)
                scatter(m, pool)
                pool.wait_ge(sem("scattered"), 16 * TPC * (m.n + 1))
                pool.sem_inc(sem("rows_left"))

            iterations(pool, iteration)

        @blk.tensor
        def _(pe):
            HL = ((0, 0), (1, 0), (0, 1))

            def product(dst, a, bm, first=True, final=True):
                for n, (ia, ib) in enumerate(HL):
                    ins = nc.tensor.matmul(dst, a[ia], bm[ib], start=first and n == 0, stop=final and n == 2)
                return ins

            def used(i, *what):
                pe.wait_ge(sem("work_used"), use(i, *what) + 1)

            def transposed(ps, src):
                for k in range(KT):
                    ins = nc.tensor.transpose(ps[:, k * P:(k + 1) * P], src[:, k * P:(k + 1) * P], ident[:])
                return ins

            def scores(i, g):
                if g == 0:
                    used(i, "NM")
                for c in range(NC):
                    pe.wait_ge(sem("exp_done"), NC * (KT * i.n + g) + c + 1)
                    cols = slice(c * PK, (c + 1) * PK)
                    product(sbank[c][0:PK, :], [k[:, g, cols] for k in k_cur], [v[:, g, :] for v in q], True, False)
                    nc.tensor.matmul(sbank[c][0:PK, :], sel[:, g, cols], nmT[:], start=False, stop=True)\
                        .then_inc(sem("scores_ready"), 1)

            def values(i, g):
                G = KT * i.n + g
                pe.wait_ge(sem("p_lo_ready"), NC * (G + 1))
                for h in range(2):
                    pe.wait_ge(sem("normalised"), 2 * G + h + 1)
                    for t in (2 * h, 2 * h + 1):
                        for c in range(NC):
                            col = (t % 2) * HG * VC + c * VC
                            for n, (ip, iv) in enumerate(HL):
                                vv = v_all[iv][:, bass.ds(i.batch, 1), g, c, :].rearrange("p a n -> p (a n)")
                                ins = nc.tensor.matmul(
                                    obank[h][:, col:col + 2 * VC], pp[ip][:, g % 2, c, t * P:(t + 1) * P], vv,
                                    start=(t % 2 == 0 and c == 0 and n == 0),
                                    stop=(t % 2 == 1 and c == NC - 1 and n == 2), skip_group_check=True)
                    ins.then_inc(sem("values_ready"), 1)

            def banked(i, kind, *at):
                k = use(i, kind, *at)
                if not (i.is_(-1) and k < WB):
                    pe.wait_ge(sem("work_used"), k - WB + 1)
                ps = bank_of(i, kind, *at)
                if kind == "T":
                    pe.wait_ge(sem("xn_ready"), i.plus(1).n * TPC + at[0] + 1)
                    return transposed(ps, xn[:, at[0], :])
                if kind == "C":
                    pe.wait_ge(sem("normalised"), 2 * KT * i.n + 2)
                    return transposed(ps, cc[:, at[0], :])
                if kind == "Q":
                    g, = at
                    if g == 0:
                        used(i, "T", TPC - 1)
                    for k in range(KT):
                        ins = product(ps[:, :], [w[:, k, g * P:(g + 1) * P] for w in wq], [v[:, k, :] for v in xnT],
                                      k == 0, k == KT - 1)
                    return ins
                if kind == "M":
                    g, t = at
                    if t == 0:
                        used(i, "Q", g)
                        pe.wait_ge(sem("k_built"), KT * i.plus(1).batch + K_ORDER.index(g) + 1)
                    return nc.tensor.matmul(ps[:, 0:KC], q[0][:, g, t * P:(t + 1) * P], k_cur[0][:, g, 0:KC],
                                            start=True, stop=True)
                if kind == "NM":
                    used(i.plus(-1), "M", KT - 1, TPC - 1)
                    for t in range(TPC):
                        ins = nc.tensor.transpose(ps[:, t * P:(t + 1) * P], negmax[:, t, :], ident[:])
                    return ins
                if kind in ("GX", "GC"):
                    a, w = (xnT, gt) if kind == "GX" else (cT, wg)
                    used(i, "T" if kind == "GX" else "C", TPC - 1)
                    for t in range(TPC):
                        for k in range(KT):
                            ins = product(ps[:, t * E:(t + 1) * E], [v[:, k, t * P:(t + 1) * P] for v in a],
                                          [v[:, k, :] for v in w], k == 0, k == KT - 1)
                    return ins
                if kind == "O":
                    t, = at
                    used(i, "C", t)
                    for k in range(KT):
                        ins = product(ps[:, :], [v[:, k, t * P:(t + 1) * P] for v in cT], [w[:, k, :] for w in wo],
                                      k == 0, k == KT - 1)
                    return ins
                pe.wait_ge(sem("one_hot"), i.n)
                for t in range(TPC):
                    for s_ in range(t + 1):
                        nc.tensor.matmul(ps[:, t * E:(t + 1) * E], tri[:] if s_ == t else ones[:], oh[:, s_, :],
                                         start=s_ == 0, stop=s_ == t)
                for s_ in range(TPC):
                    ins = nc.tensor.matmul(ps[:, TPC * E:(TPC + 1) * E], ones[:], oh[:, s_, :],
                                           start=s_ == 0, stop=s_ == TPC - 1)
                return ins

            def iteration(i):
                for kind, *at in i.steps():
                    if kind == "S":
                        scores(i, *at)
                    elif kind == "PV":
                        values(i, *at)
                    else:
                        banked(i, kind, *at).then_inc(sem("work_filled"), 1)

            iterations(pe, iteration)

        @blk.scalar
        def _(act):
            act.nop().then_inc(sem("exp_done"), NC)

            def normalised_x(n, t):
                if t == 0:
                    act.wait_ge(sem("factors_ready"), n.n + 1)
                nc.scalar.activation(xn[:, t, :], xt[:, n.slot, t, :], ACT.Identity, scale=rstd[:, t:t + 1],
                                     bias=nmr[:, t:t + 1]).then_inc(sem("xn_ready"), 1)

            def sum_expert(n):
                u = n % EPRE
                act.wait_ge(sem(f"e_pre{u}"), 16 * (n // EPRE + 1))
                if n:
                    act.wait_ge(sem("e_summed"), n)
                nc.scalar.activation(pay[:, 0, :, 0:DM], er_pre[:, u, :, :], ACT.Abs, accum_out=e_sum[:, n:n + 1])\
                    .then_inc(sem("e_summed"), 1)

            def iteration(i):
                for kind, *at in i.steps(SCALAR):
                    if kind == "X":
                        act.wait_ge(sem("work_filled"), use(i, "T", *at) + 1)
                        normalised_x(i.plus(2), *at)
                    elif kind in SPLIT:
                        act.wait_ge(sem("work_filled"), use(i, kind, *at) + 1)
                        ps = bank_of(i, kind, *at)
                        if kind == "Q":
                            ins = nc.scalar.activation(q[0][:, at[0], :], ps[:, :], ACT.Identity,
                                                       bias=bq_s[:, at[0]:at[0] + 1])
                        else:
                            dst = (xnT if kind == "T" else cT)[0][:, :, at[0] * P:(at[0] + 1) * P]
                            ins = nc.scalar.activation(dst, ps[:, :].rearrange("p (k n) -> p k n", k=KT), ACT.Copy)
                        ins.then_inc(sem("hi_ready"), 1)
                        if kind == "Q" and (i.is_(-1) or i.is_(0)):
                            sum_expert((i.n + 1) * KT + at[0])
                    elif kind == "S":
                        g, = at
                        G = KT * i.n + g
                        act.wait_ge(sem("values_ready"), 2 * G + 2)
                        for k in range(NC):
                            act.wait_ge(sem("scores_ready"), NC * G + k + 1)
                            nc.scalar.activation(pf[:, g % 2, k, :], sbank[k][0:PK, :], ACT.Exp,
                                                 scale=exp_scale[0:PK, :])
                            nc.scalar.activation(pp[0][:, g % 2, k, :], sbank[k][0:PK, :], ACT.Exp,
                                                 scale=exp_scale[0:PK, :]).then_inc(sem("exp_done"), 1)

            iterations(act, iteration)

        @blk.vector
        def _(dve):
            own = OwnCount(21)

            def mark(ins):
                own.done += 1
                ins.then_inc(sem("dve_step"), 1)

            def do(ins):
                mark(ins)
                dve.wait_ge(sem("dve_step"), own.value())

            dve.nop().then_inc(sem("normalised"), 2)
            dve.nop().then_inc(sem("values_ready"), 4)
            dve.nop().then_inc(sem("rows_left"), 2)
            dve.nop().then_inc(sem("pay_stats"), 1)

            def ln_stats(n, t):
                if t == 0:
                    dve.wait_ge(sem(f"x_in{n.slot}"), 16 * (n.batch + 1))
                ins = nc.vector.bn_stats(bst[:, t, :], xt[:, n.slot, t, :])
                if t == TPC - 1:
                    mark(ins)

            def ln_end(n):
                wait_alone(dve, "dve_step", own.value())
                if not n.is_(0):
                    wait_alone(dve, "factors_ready", n.n)
                for t in range(TPC):
                    ins = nc.vector.bn_aggr(mv[:, t, :], bst[:, t, :])
                do(ins)
                nc.vector.tensor_scalar(ve[:], mv[:, :, 1], EPS, None, ALU.add).then_inc(sem("ln_stats"), 1)

            def ln(n):
                for t in range(TPC):
                    ln_stats(n, t)
                ln_end(n)

            def lo(i, kind, at):
                dve.wait_ge(sem("hi_ready"), i.number((kind, at), SPLIT) + 1)
                ps = bank_of(i, kind, at)
                if kind == "Q":
                    ins = nc.vector.scalar_tensor_tensor(out=q[1][:, at, :], in0=ps[:, :], scalar=bq_s[:, at:at + 1],
                                                         in1=q[0][:, at, :].bitcast(F32), op0=ALU.add,
                                                         op1=ALU.subtract)
                else:
                    dst = [v[:, :, at * P:(at + 1) * P] for v in (xnT if kind == "T" else cT)]
                    ins = nc.vector.tensor_tensor(dst[1], ps[:, :].rearrange("p (k n) -> p k n", k=KT), dst[0],
                                                  ALU.subtract)
                ins.then_inc(sem("work_used"), 1)

            def p_lo(i, g, k):
                dve.wait_ge(sem("exp_done"), NC * (KT * i.n + g) + k + 1 + NC)
                nc.vector.tensor_tensor(pp[1][:, g % 2, k, :], pf[:, g % 2, k, :], pp[0][:, g % 2, k, :],
                                        ALU.subtract).then_inc(sem("p_lo_ready"), 1)

            def normalise(i, g, h):
                dve.wait_ge(sem("values_ready"), 2 * (KT * i.n + g) + h + 1 + 4)
                o = obank[h][:, 0:2 * HG * VC].rearrange("p (t j k) -> p t j k", t=2, j=HG)
                do(nc.vector.reciprocal(den[:, h, :, :], o[:, :, :, DK]))
                nc.vector.tensor_tensor(
                    cc[:, 2 * h:2 * h + 2, g * P:(g + 1) * P].rearrange("p t (j k) -> p t j k", j=HG),
                    o[:, :, :, 0:DK], den[:, h, :, :].unsqueeze(3).to_broadcast([P, 2, HG, DK]), ALU.mult)\
                    .then_inc(sem("normalised"), 1)

            def by_tile(ps):
                return ps[:, 0:TPC * E].rearrange("p (t e) -> p t e", t=TPC)

            def banked(i, kind, *at):
                dve.wait_ge(sem("work_filled"), use(i, kind, *at) + 1)
                ps = bank_of(i, kind, *at)
                if kind == "M":
                    g, t = at
                    return nc.vector.tensor_reduce(negmax[:, t, g * HG:(g + 1) * HG],
                                                   ps[:, 0:KC].rearrange("p (j s) -> p j s", j=HG), X, ALU.max,
                                                   negate=True)
                if kind == "NM":
                    return nc.vector.tensor_copy(nmT[:], ps[:, :])
                if kind == "GX":
                    n = i.plus(1).slot
                    do(nc.vector.tensor_tensor(gx[:, n], by_tile(ps), std[:, n % 2, :].unsqueeze(2)
                                               .to_broadcast([P, TPC, E]), ALU.mult))
                    return nc.vector.scalar_tensor_tensor(out=gx[:, n], in0=gx[:, n], scalar=inv[:, S_G:S_G + 1],
                                                          in1=gate_c[:].unsqueeze(1).to_broadcast([P, TPC, E]),
                                                          op0=ALU.mult, op1=ALU.add)
                m = i.plus(-1)
                par = m.slot % 2
                if kind == "O":
                    t, = at
                    if t == 0:
                        dve.wait_ge(sem("rows_left"), m.n + 1)
                    dve.wait_ge(sem("x_plus_bo"), TPC * m.n + t + 1)
                    return nc.vector.scalar_tensor_tensor(out=pay[:, par, t, 0:DM], in0=ps[:, :], scalar=inv_y[:],
                                                          in1=xt[:, m.slot, t, :], op0=ALU.mult, op1=ALU.add)
                if kind == "GC":
                    return nc.vector.scalar_tensor_tensor(out=lg[:], in0=by_tile(ps), scalar=inv_gc[:], in1=gx[:, m.slot],
                                                          op0=ALU.mult, op1=ALU.add)
                do(nc.vector.tensor_tensor(lg[:], by_tile(ps), base[:].unsqueeze(1).to_broadcast([P, TPC, E]),
                                           ALU.add))
                return nc.vector.tensor_tensor(base[:], ps[:, TPC * E:(TPC + 1) * E], base[:], ALU.add)

            def one_hot(i):
                dve.wait_ge(sem("work_used"), use(i, "GC") + 1)
                do(nc.vector.tensor_reduce(lmax[:], lg[:], X, ALU.max))
                do(nc.vector.tensor_tensor(lg[:], lg[:], lmax[:].unsqueeze(2).to_broadcast([P, TPC, E]), ALU.is_ge))
                do(nc.vector.tensor_tensor(lg[:], lg[:], weight8[:].unsqueeze(1).to_broadcast([P, TPC, E]), ALU.mult))
                do(nc.vector.tensor_reduce(lmax[:], lg[:], X, ALU.max))
                nc.vector.tensor_tensor(oh[:], lg[:], lmax[:].unsqueeze(2).to_broadcast([P, TPC, E]), ALU.is_equal)\
                    .then_inc(sem("one_hot"), 1)

            def ln2_stats(i, t):
                dve.wait_ge(sem("work_used"), use(i, "O", t) + 1)
                ins = nc.vector.bn_stats(bst2[:, t, :], pay[:, i.plus(-1).slot % 2, t, 0:DM])
                if t == TPC - 1:
                    mark(ins)

            def ln2_end(i):
                wait_alone(dve, "dve_step", own.value())
                wait_alone(dve, "pay_stats", i.n)
                for t in range(TPC):
                    ins = nc.vector.bn_aggr(mv2[:, t, :], bst2[:, t, :])
                do(ins)
                nc.vector.tensor_scalar(ve2[:], mv2[:, :, 1], EPS, None, ALU.add).then_inc(sem("ln2_stats"), 1)

            def slots(i):
                par = i.plus(-1).slot % 2
                dve.wait_ge(sem("work_used"), use(i, "R") + 1)
                do(nc.vector.tensor_tensor(lg[:], lg[:], oh[:], ALU.mult))
                do(nc.vector.tensor_reduce(slotf[:], lg[:], X, ALU.add))
                nc.vector.tensor_copy(slot[:, par, :], slotf[:])
                do(nc.vector.tensor_copy(pay[:, par, :, C_ID].bitcast(I32), token[:]))
                nc.vector.tensor_scalar(token[:], token[:], float(CH), None, ALU.add).then_inc(sem("slot_ready"), 1)

            own_parts = {
                "P": p_lo, "V": normalise, "B": ln2_stats, "VE": ln2_end, "H": one_hot, "SL": slots,
                "L": lambda i, t: ln_stats(i.plus(2), t), "LE": lambda i: ln_end(i.plus(2)),
            }

            def iteration(i):
                own.begin(i)
                if i.is_(-1):
                    ln(Chunk(0, 1))
                for kind, *at in i.steps(VECTOR):
                    if kind in SPLIT:
                        lo(i, kind, *at)
                    elif kind in BANKED:
                        banked(i, kind, *at).then_inc(sem("work_used"), 1)
                    elif kind == "K":
                        if i.slot == CPB - 1 and not i.is_(NCHUNK - 1):
                            build_k(i.plus(1).batch, *at)
                    elif kind in NEXT and i.is_(-1):
                        pass
                    else:
                        own_parts[kind](i, *at)

            iterations(dve, iteration)
    attention.close()

    e_w = [sb(f"e_{s}", [P, E, KT, DM], F16) for s in ("hi", "lo")]
    U = UNROLL
    row = sb("row", [P, U, ROW])
    tab = sb("tab", [P, 2, NTILE], I32)

    def load_rows(sp, t, u):
        first = sp.value_load(tab[0:1, 0, bass.ds(t, 1)], min_val=0, max_val=E * REGION)
        sp.dma_start(row[:, u, :], rows[bass.ds(first, P), :]).then_inc(sem(f"row_in{u}"), 16)

    with ExitStack() as st:
        def sp_(name, shape, dt=F32):
            return sb(name, shape, dt, st)
        er_rest = sp_("er_rest", [P, E - EPRE, KT, DM])
        mx = sp_("mx_e", [P, 1])
        zrow = sp_("zrow", [P, ROW])
        row_p = sp_("row_p", [P, 1])
        region = sp_("region", [P, E])
        ntf = sp_("ntf", [P, E])
        nti = sp_("nti", [P, E], I32)
        cum = sp_("cum", [P, E])
        jump = sp_("jump", [P, E])
        tile = sp_("tile", [P, NTILE])
        start = sp_("start", [P, NTILE])
        which = sp_("which", [P, NTILE])
        ge = sp_("ge", [P, NTILE, E])
        moved = sp_("moved", [P, NTILE, E])
        padf = sp_("padf", [P, E])
        pads = sp_("pads", [P, E], I32)
        NBK = 8
        bank = [st.enter_context(nc.psum_tensor(f"ex{i}", [P, 512], F32)) for i in range(NBK)]
        blk = st.enter_context(nc.Block())

        @blk.sync
        def _(sp):
            for e in range(EPRE, E):
                sp.dma_start(er_rest[:, e - EPRE, :, :], expert_w[e].rearrange("(t p) h -> p t h", p=P))\
                    .then_inc(sem(f"e_in{e}"), 16)
            sp.wait_ge(sem("table_ready"), 1)
            sp.wait_ge(sem("padded"), 16 * (E + 1))
            sp.wait_ge(sem("scattered"), 16 * TPC * NCHUNK)
            for u in range(U):
                load_rows(sp, u, u)

        @blk.gpsimd
        def _(pool):
            do = steps(pool, "pool_experts")
            do(nc.gpsimd.iota(region[:], pattern=[[REGION, E]], base=0, channel_multiplier=0,
                              allow_small_or_imprecise_dtypes=True))
            do(nc.gpsimd.iota(row_p[:], pattern=[[0, 1]], base=0, channel_multiplier=1,
                              allow_small_or_imprecise_dtypes=True))
            do(nc.gpsimd.iota(tile[:], pattern=[[1, NTILE]], base=0, channel_multiplier=0,
                              allow_small_or_imprecise_dtypes=True))
            do(nc.gpsimd.memset(zrow[:], 0.0))
            do(nc.gpsimd.memset(zrow[:, C_ID:C_ID + 1].bitcast(I32), 1 << 20))
            pool.nop().then_inc(sem("e_consts"), 1)
            last = Chunk(B - 1, CPB - 1)
            row_factors(last, pool, do)
            pool.wait_ge(sem("e_max"), 1)
            nc.gpsimd.partition_all_reduce(mx[:], mx[:], P, bass.bass_isa.ReduceOp.max).then_inc(sem("e_max_all"), 1)
            scatter(last, pool)
            nc.gpsimd.dma_start(rows[E * REGION:E * REGION + P, :], zrow[:]).then_inc(sem("padded"), 16)
            pool.wait_ge(sem("pads_ready"), 1)
            for e in range(E):
                nc.gpsimd.indirect_dma_start(
                    out=rows, out_offset=bass.IndirectOffsetOnAxis(ap=pads[:, e:e + 1], axis=0),
                    in_=zrow[:], in_offset=None).then_inc(sem("padded"), 16)
            pool.wait_ge(sem("padded"), 16 * (E + 1))
            pool.wait_ge(sem("scattered"), 16 * TPC * NCHUNK)

        order = [(e, k) for e in range(E) for k in range(KT)]

        @blk.tensor
        def _(pe):
            for n, (e, k) in enumerate(order):
                if e >= EPRE:
                    pe.wait_ge(sem(f"e_in{e}"), 16)
                    src = er_rest[:, e - EPRE, :, k * P:(k + 1) * P]
                else:
                    n_pass = E_PASS.index(e)
                    pe.wait_ge(sem(f"e_pre{n_pass % EPRE}"), 16 * (n_pass // EPRE + 1))
                    src = er_pre[:, n_pass % EPRE, :, k * P:(k + 1) * P]
                if n >= NBK:
                    pe.wait_ge(sem("e_lo"), n - NBK + 1)
                for f in range(KT):
                    ins = nc.tensor.transpose(bank[n % NBK][:, f * P:(f + 1) * P], src[:, f, :], ident[:])
                ins.then_inc(sem("e_transposed"), 1)

        @blk.scalar
        def _(act):
            act.wait_ge(sem("e_scale"), 1)
            for n, (e, k) in enumerate(order):
                act.wait_ge(sem("e_transposed"), n + 1)
                nc.scalar.activation(e_w[0][:, e, k, :], bank[n % NBK][:, :], ACT.Identity,
                                     scale=scl[:, S_E:S_E + 1]).then_inc(sem("e_hi"), 1)

        @blk.vector
        def _(dve):
            do = steps(dve, "dve_experts")
            nc.vector.tensor_reduce(mx[:], e_sum[:], X, ALU.max).then_inc(sem("e_max"), 1)
            dve.wait_ge(sem("e_consts"), 1)
            do(nc.vector.tensor_scalar(padf[:], base[:], row_p[:], None, ALU.add))
            nc.vector.tensor_copy(pads[:], padf[:]).then_inc(sem("pads_ready"), 1)
            dve.wait_ge(sem("e_max_all"), 1)
            c = slice(S_E, S_E + 1)
            do(nc.vector.tensor_scalar(mx[:], mx[:], 1e-25, None, ALU.max))
            do(nc.vector.tensor_scalar(inv[:, c].bitcast(I32), mx[:].bitcast(I32), 0x7F800000, None,
                                       ALU.bitwise_and))
            do(nc.vector.tensor_scalar(inv[:, c], inv[:, c], 1.0 / TOP, None, ALU.mult))
            nc.vector.reciprocal(scl[:, c], inv[:, c]).then_inc(sem("e_scale"), 1)
            do(nc.vector.tensor_tensor(ntf[:], base[:], region[:], ALU.subtract))
            do(nc.vector.tensor_scalar(ntf[:], ntf[:], float(P - 1), None, ALU.add))
            do(nc.vector.tensor_copy(nti[:], ntf[:]))
            do(nc.vector.tensor_scalar(nti[:], nti[:], 7, None, ALU.logical_shift_right))
            do(nc.vector.tensor_copy(ntf[:], nti[:]))
            do(nc.vector.tensor_scalar(jump[:], ntf[:], -float(P), float(REGION), ALU.mult, ALU.add))
            do(nc.vector.tensor_copy(cum[:], ntf[:]))
            for e in range(1, E):
                do(nc.vector.tensor_tensor(cum[:, e:e + 1], cum[:, e:e + 1], cum[:, e - 1:e], ALU.add))
            every = [P, NTILE, E]
            do(nc.vector.tensor_tensor(ge[:], tile[:].unsqueeze(2).to_broadcast(every),
                                       cum[:].unsqueeze(1).to_broadcast(every), ALU.is_ge))
            do(nc.vector.tensor_tensor(moved[:], ge[:], jump[:].unsqueeze(1).to_broadcast(every), ALU.mult))
            do(nc.vector.tensor_reduce(which[:], ge[:], X, ALU.add))
            do(nc.vector.tensor_reduce(start[:], moved[:], X, ALU.add))
            do(nc.vector.scalar_tensor_tensor(out=start[:], in0=tile[:], scalar=float(P), in1=start[:], op0=ALU.mult,
                                              op1=ALU.add))
            do(nc.vector.tensor_scalar(start[:], start[:], float(E * REGION), None, ALU.min))
            do(nc.vector.tensor_scalar(which[:], which[:], float(E - 1), None, ALU.min))
            nc.vector.tensor_copy(tab[:, 0, :], start[:])
            nc.vector.tensor_copy(tab[:, 1, :], which[:]).then_inc(sem("table_ready"), 1)
            for n, (e, k) in enumerate(order):
                dve.wait_ge(sem("e_hi"), n + 1)
                nc.vector.scalar_tensor_tensor(out=e_w[1][:, e, k, :], in0=bank[n % NBK][:, :], scalar=scl[:, c],
                                               in1=e_w[0][:, e, k, :], op0=ALU.mult, op1=ALU.subtract)\
                    .then_inc(sem("e_lo"), 1)

    with ExitStack() as st:
        def sp_(name, shape, dt=F32):
            return sb(name, shape, dt, st)
        xn2 = sp_("xn2", [P, U, DM])
        x2T = [sp_(f"x2T_{s}", [P, 2, KT, P], F16) for s in ("hi", "lo")]
        res = sp_("res", [P, U, DM])
        tbank = [st.enter_context(nc.psum_tensor(f"mt{i}", [P, 512], F32)) for i in range(2)]
        obank2 = [st.enter_context(nc.psum_tensor(f"mo{i}", [P, 512], F32)) for i in range(2)]
        blk = st.enter_context(nc.Block())
        assert NTILE % U == 0

        def tiles(eng, body):
            with eng.Fori(0, NTILE // U - 1) as k:
                for u in range(U):
                    body(k * U + u, k, u)
            for u in range(U):
                body(NTILE - U + u, NTILE // U - 1, u)

        def has(t):
            return not isinstance(t, int) or t < NTILE

        @blk.sync
        def _(sp):
            with sp.Fori(1, NTILE // U) as k:
                for u in range(U):
                    sp.wait_ge(sem(f"out{u}"), 16 * k)
                    load_rows(sp, k * U + u, u)

        @blk.gpsimd
        def _(pool):
            def add(t, u):
                wait_alone(pool, "xn2_ready", t + 1)
                nc.gpsimd.tensor_tensor(row[:, u, 0:DM], row[:, u, 0:DM], xn2[:, u, :], ALU.add)\
                    .then_inc(sem("sum_ready"), 1)

            def body(t, k, u):
                if has(t + 1):
                    add(t + 1, (u + 1) % U)
                wait_alone(pool, "res_ready", t + 1 + 2)
                nc.gpsimd.indirect_dma_start(
                    out=out_rows, out_offset=bass.IndirectOffsetOnAxis(ap=row[:, u, C_ID:C_ID + 1].bitcast(I32), axis=0),
                    in_=res[:, u, :], in_offset=None, bounds_check=NTOK - 1, oob_is_err=False)\
                    .then_inc(sem(f"out{u}"), 16)

            add(0, 0)
            tiles(pool, body)
            for u in range(U):
                wait_alone(pool, f"out{u}", 16 * (NTILE // U))

        @blk.tensor
        def _(pe):
            HL = ((0, 0), (1, 0), (0, 1))

            def tr(t, u):
                pe.wait_ge(sem("xn2_ready"), t + 1)
                pe.wait_ge(sem("t_used"), t + 1)
                for k in range(KT):
                    ins = nc.tensor.transpose(tbank[u % 2][:, k * P:(k + 1) * P], xn2[:, u, k * P:(k + 1) * P],
                                              ident[:])
                ins.then_inc(sem("t_filled"), 1)

            def mm(t, u):
                e = pe.value_load(tab[0:1, 1, bass.ds(t, 1)], min_val=0, max_val=E - 1)
                pe.wait_ge(sem("t_used"), t + 1 + 2)
                pe.wait_ge(sem("res_ready"), t + 1)
                for k in range(KT):
                    for n, (ia, ib) in enumerate(HL):
                        w = e_w[ib][:, bass.ds(e, 1), k, :].rearrange("p a n -> p (a n)")
                        ins = nc.tensor.matmul(obank2[u % 2][:, :], x2T[ia][:, u % 2, k, :], w,
                                               start=k == 0 and n == 0, stop=k == KT - 1 and n == 2)
                ins.then_inc(sem("o_filled"), 1)

            def body(t, k, u):
                if has(t + 1):
                    tr(t + 1, (u + 1) % U)
                mm(t, u)

            tr(0, 0)
            tiles(pe, body)

        @blk.scalar
        def _(act):
            act.nop().then_inc(sem("o_filled"), 2)

            def body(t, k, u):
                act.wait_ge(sem("t_filled"), t + 1)
                act.wait_ge(sem("o_filled"), t + 1)
                nc.scalar.activation(x2T[0][:, u % 2, :, :], tbank[u % 2][:, :].rearrange("p (k n) -> p k n", k=KT),
                                     ACT.Copy).then_inc(sem("t_hi"), 1)

            tiles(act, body)

        @blk.vector
        def _(dve):
            dve.nop().then_inc(sem("t_used"), 2)
            dve.nop().then_inc(sem("res_ready"), 2)

            def norm(t, loads, u):
                dve.wait_ge(sem(f"row_in{u}"), 16 * loads)
                nc.vector.tensor_scalar(xn2[:, u, :], row[:, u, 0:DM], row[:, u, C_RSTD:C_RSTD + 1],
                                        row[:, u, C_NMR:C_NMR + 1], ALU.mult, ALU.add).then_inc(sem("xn2_ready"), 1)

            def lo(t, u):
                dve.wait_ge(sem("t_hi"), t + 1)
                nc.vector.tensor_tensor(x2T[1][:, u % 2, :, :], tbank[u % 2][:, :].rearrange("p (k n) -> p k n", k=KT),
                                        x2T[0][:, u % 2, :, :], ALU.subtract).then_inc(sem("t_used"), 1)

            def body(t, k, u):
                if has(t + 2):
                    norm(t + 2, k + (u + 2) // U + 1, (u + 2) % U)
                if has(t + 1):
                    lo(t + 1, (u + 1) % U)
                dve.wait_ge(sem("o_filled"), t + 1 + 2)
                dve.wait_ge(sem("sum_ready"), t + 1)
                nc.vector.scalar_tensor_tensor(out=res[:, u, :], in0=obank2[u % 2][:, :], scalar=inv[:, S_E:S_E + 1],
                                               in1=row[:, u, 0:DM], op0=ALU.mult, op1=ALU.add)\
                    .then_inc(sem("res_ready"), 1)

            norm(0, 1, 0)
            norm(1, 1, 1)
            lo(0, 0)
            tiles(dve, body)
    es.close()


_INS = ['x', 'ctx_512', 'L0_xattn_Wq', 'L0_xattn_bq', 'L0_xattn_Wk', 'L0_xattn_bk', 'L0_xattn_Wv', 'L0_xattn_bv',
        'L0_xattn_Wo', 'L0_xattn_bo', 'L0_ffn_gate_w', 'L0_ffn_expert_w']


def kernel(**inputs):
    import numpy as _np
    import concourse.bacc as _bacc
    from concourse.bass_utils import run_bass_kernel_spmd as _run

    nc = _bacc.Bacc("TRN2", target_bir_lowering=False, num_devices=1)
    arrays, args = {}, []
    for name in _INS:
        a = _np.ascontiguousarray(inputs[name])
        arrays[f"in_{name}"] = a
        args.append(nc.dram_tensor(f"in_{name}", a.shape, mybir.dt.from_np(a.dtype), kind="ExternalInput").ap())
    args.append(nc.dram_tensor("out_0", (B, LQ, DM), F32, kind="ExternalOutput").ap())
    build(nc, *args)
    r = _run(nc, [arrays], core_ids=[0])
    return _np.asarray(r.results[0]["out_0"])
```

```python
from contextlib import ExitStack

import concourse.bass as bass

from concourse import mybir

F32, F32R, F16, BF16, I32 = (mybir.dt.float32, mybir.dt.float32r, mybir.dt.float16,
                             mybir.dt.bfloat16, mybir.dt.int32)
ALU = mybir.AluOpType
ACT = mybir.ActivationFunctionType
X = mybir.AxisListType.X

P = 128
B, LQ, DM = 4, 2048, 512
LK, DC = 77, 256
H = 16
DK = DM // H
E = 8
EPS = 1e-5
KT = DM // P
CT = DC // P
HG = P // DK
TPC = 4
CH = TPC * P
NCHUNK = B * LQ // CH
CPB = NCHUNK // B
P_DVE = 2
KR = 3 * DK + H
VR = 96
VC = DK + 1
NTOK = B * LQ
REGION = NTOK + P
ROW = DM + 3
C_RSTD, C_NMR, C_ID = DM, DM + 1, DM + 2
NTILE = NTOK // P + E
UNROLL = 8
EPRE = 1
SCALE = 1.0 / float(DK) ** 0.5
TOP = 16384.0

def order(text):
    names = [(w.rstrip("0123456789"), w) for w in text.split()]
    return [(kind, *(int(d) for d in w[len(kind):])) for kind, w in names]


STEPS = order("""
    NM T0 C0 C1 T1 T2 O0 T3 C2 S00 S01 O1 S02 S03 Q0 S10 S11 C3 O2 S12 M00 M01 S13 Q1 S20 PV0
    S21 M10 GC M11 M12 M13 S22 PV1 S23 M02 S30 Q2 S31 R M03 S32 GX M20 M21 S33 Q3 PV2 M22 M30
    M31 M32 O3 M23 PV3 M33
""")
VECTOR = order("""
    NM T0 C0 C1 T1 T2 K O0 T3 C2 B0 L0 L1 P00 L2 O1 B1 P01 Q0 C3 P10 O2 M00 P11 B2 L3 M01 Q1
    V00 M10 V01 P20 LE GC M11 P21 H M12 M13 M02 V10 Q2 R M03 GX SL M20 P30 V11 M21 Q3 M22 P31
    M30 M31 V20 V21 M32 O3 M23 B3 M33 V30 V31 VE
""")
SCALAR = order("""
    T0 C0 C1 T1 T2 T3 C2 S00 S01 S02 S03 S10 Q0 C3 S11 S12 S13 Q1 S20 S21 S22 S23 S30 Q2 S31
    X0 S32 X1 Q3 X2 S33 X3
""")
GPSIMD = order("""
    A0 P02 A1 P03 P12 P13 F A2 P22 P23 A3 P32 P33 G D
""")
FRONT, CORE, TAIL = {"T", "Q", "M", "GX"}, {"NM", "S", "PV", "P", "V", "K", "A"}, {"C", "O", "GC", "R", "B", "H", "VE", "SL", "G", "D"}
NEXT = {"X", "L", "LE", "F"}
BANKED = {"T", "C", "NM", "Q", "M", "O", "GX", "GC", "R"}
SPLIT = {"T", "C", "Q"}
WB, SB = 4, 2


def steps_of(front, core, tail, new=False, table=STEPS):
    return [s for s in table if (s[0] in FRONT and front) or (s[0] in CORE and core) or (s[0] in TAIL and tail)
            or (s[0] in NEXT and new)]


assert VECTOR.index(("GC",)) < VECTOR.index(("GX",))
assert STEPS[-1] == ("M", KT - 1, TPC - 1)
for _kinds, _table in ((BANKED, VECTOR), (SPLIT, SCALAR)):
    assert [s for s in STEPS if s[0] in _kinds] == [s for s in _table if s[0] in _kinds]


class Chunk:

    def __init__(self, b, c):
        self.b, self.c = b, c

    def plus(self, k):
        return Chunk(self.b, self.c + k)

    @property
    def static(self):
        return isinstance(self.b, int)

    @property
    def n(self):
        return self.b * CPB + self.c

    @property
    def slot(self):
        return self.c % CPB

    @property
    def batch(self):
        return self.b + self.c // CPB

    def is_(self, k):
        return self.static and self.n == k

    def steps(self, table=STEPS):
        i = self.n if self.static else 1
        return steps_of(i < NCHUNK - 1, 0 <= i < NCHUNK, i >= 1, i < NCHUNK - 2, table)

    def number(self, what, kinds):
        own = [s for s in self.steps() if s[0] in kinds]
        first, second, full = (len([s for s in steps_of(*p) if s[0] in kinds])
                               for p in ((True, False, False), (True, True, False), (True, True, True)))
        k = own.index(what)
        if self.is_(-1):
            return k
        if self.is_(0):
            return first + k
        if self.is_(NCHUNK):
            before = len([s for s in steps_of(False, True, True) if s[0] in kinds])
            return first + second + full * (NCHUNK - 2) + before + k
        return (self.n - 1) * full + (first + second + k)


def build(nc, x, ctx, Wq, bq, Wk, bk, Wv, bv, Wo, bo, gate_w, expert_w, out):
    es = ExitStack()
    sems = {}

    def sb(name, shape, dt=F32, stack=es):
        return stack.enter_context(nc.sbuf_tensor(name, shape, dt))

    def sem(name):
        if name not in sems:
            sems[name] = es.enter_context(nc.semaphore(name))
        return sems[name]

    def wait_alone(eng, name, value):
        eng.wait_ge(sem(name), value)
        eng.sem_inc(sem("waited_alone"))

    def steps(eng, name):
        n = [0]

        def do(ins):
            n[0] += 1
            ins.then_inc(sem(name), 1)
            eng.wait_ge(sem(name), n[0])
        return do

    rows = nc.dram_tensor("rows_by_expert", [E * REGION + P, ROW], F32)
    rows = rows.ap()
    k_st = nc.dram_tensor("key_stacks", [3 * DK, H, B + 1, LK], F32).ap()
    out_rows = out.rearrange("b s d -> (b s) d")

    ident = sb("ident", [P, P])
    base = sb("base", [P, E])
    inv = sb("inv", [P, 8])
    scl = sb("scl", [P, 8])
    S_WQ, S_WO, S_G, S_V, S_WG, S_E = range(6)
    er_pre = sb("er_pre", [P, EPRE, KT, DM])
    e_sum = sb("e_sum", [P, E])
    pows = sb("pows", [P, 2, TPC])
    pay = sb("pay", [P, 2, TPC, ROW])
    mv2 = sb("mv2", [P, TPC, 2])
    ve2 = sb("ve2", [P, TPC])
    slot = sb("slot", [P, 2, TPC], I32)
    attention = ExitStack()

    def sa(name, shape, dt=F32):
        return sb(name, shape, dt, attention)

    wq = [sa(f"wq_{s}", [P, KT, DM], F16) for s in ("hi", "lo")]
    wo = [sa(f"wo_{s}", [P, KT, DM], F16) for s in ("hi", "lo")]
    gt = [sa(f"gate_{s}", [P, KT, E], F16) for s in ("hi", "lo")]
    wg = [sa(f"wogate_{s}", [P, KT, E], F16) for s in ("hi", "lo")]
    k_next = sa("k_next", [P, H, LK], F32R)
    k_now = sa("k_now", [P, H, LK], F32R)
    k_cur = sa("k_cur", [P, KT, HG * LK], F32R)
    v_now = [sa(f"v_now_{s}", [VR, H, VC], F16) for s in ("hi", "lo")]
    v_all = [sa(f"v_all_{s}", [VR, B, H, VC], F16) for s in ("hi", "lo")]
    tri = sa("tri", [P, P], BF16)
    ones = sa("ones", [P, P], BF16)
    bo_rep = sa("bo_rep", [P, DM])
    bq_s = sa("bq_s", [P, KT])
    gate_c = sa("gate_c", [P, E])
    exp_scale = sa("exp_scale", [P, 1])
    inv_y = sa("inv_y", [P, 1])
    inv_gc = sa("inv_gc", [P, 1])
    weight8 = sa("weight8", [P, E])
    token = sa("token", [P, TPC])
    xt = sa("xt", [P, CPB, TPC, DM])
    xn = sa("xn", [P, TPC, DM])
    bst = sa("bst", [P, TPC, 6])
    mv = sa("mv", [P, TPC, 2])
    ve = sa("ve", [P, TPC])
    rstd = sa("rstd", [P, TPC])
    std = sa("std", [P, 2, TPC])
    nmr = sa("nmr", [P, TPC])
    xv = x.rearrange("b (c t p) d -> (b c) p t d", t=TPC, p=P)

    def row_factors(m, pool, do):
        par = m.slot % 2
        wait_alone(pool, "ln2_stats", m.n + 1)
        do(nc.gpsimd.tensor_tensor(pay[:, par, :, C_RSTD], ve2[:], pows[:, 0, :], ALU.pow))
        do(nc.gpsimd.tensor_tensor(mv2[:, :, 1], mv2[:, :, 0], pay[:, par, :, C_RSTD], ALU.mult))
        nc.gpsimd.tensor_scalar(pay[:, par, :, C_NMR], mv2[:, :, 1], -1.0, None, ALU.mult)\
            .then_inc(sem("pay_stats"), 1)

    def scatter(m, pool):
        par = m.slot % 2
        wait_alone(pool, "slot_ready", m.n + 1)
        wait_alone(pool, "pay_stats", m.n + 2)
        for t in range(TPC):
            nc.gpsimd.indirect_dma_start(
                out=rows, out_offset=bass.IndirectOffsetOnAxis(ap=slot[:, par, t:t + 1], axis=0),
                in_=pay[:, par, t, :], in_offset=None).then_inc(sem("scattered"), 16)

    def load_keys(sp, b):
        sp.dma_start(k_next[0:3 * DK, :, :].bitcast(F32), k_st[:, :, bass.ds(b, 1), :].rearrange("p h a s -> p h (a s)"))\
            .then_inc(sem("keys_in"), 16)

    def build_k(b):
        nc.vector.wait_ge(sem("keys_in"), 16 * (b + 1))
        for j in range(HG):
            src = k_next[0:DK, j:H:HG, :].bitcast(F32)
            ins = nc.vector.tensor_copy(k_cur[j * DK:(j + 1) * DK, :, j * LK:(j + 1) * LK], src)
        ins.then_inc(sem("k_built"), 1)

    def stack_k(tt, b):
        wait_alone(tt, "k_built", b + 1)
        tt.tensor_copy(k_now[0:3 * DK, :, :], k_next[0:3 * DK, :, :].bitcast(F32)).then_inc(sem("stack_built"), 1)

    def copy_v(b):
        for dst, src in zip(v_now, v_all):
            ins = nc.vector.tensor_copy(dst[:], src[:, bass.ds(b, 1), :, :].rearrange("p a h k -> p (a h) k"))
        ins.then_inc(sem("v_built"), 1)

    with ExitStack() as st:
        def sp_(name, shape, dt=F32):
            return sb(name, shape, dt, st)
        wraw = {n: sp_("raw_" + n, [P, KT, DM]) for n in ("q", "o")}
        craw = {n: sp_("raw_" + n, [P, CT, DM]) for n in ("k", "v")}
        cx = sp_("cx", [LK, B, DC])
        cxT = sp_("cxT", [P, CT, B, LK])
        k_nat = [sp_(f"k_nat_{s}", [P, KT, B, LK], F32R) for s in ("hi", "lo")]
        bvec = sp_("bvec", [P, 4, KT])
        BQ, BK, BO, BV = range(4)
        bmat = sp_("bmat", [P, 2, KT, P])
        g8 = sp_("g8", [E, DM])
        gmean = sp_("gmean", [E, 1])
        gc8 = sp_("gc8", [E, DM])
        gT = sp_("gT", [P, KT, E])
        woT = sp_("woT", [P, KT, DM])
        wgT = sp_("wgT", [E, DM])
        wgf = sp_("wgf", [P, KT, E])
        zeros = sp_("zeros", [P, HG * LK])
        sel32 = sp_("sel32", [P, H, LK])
        mx = sp_("mx", [P, 8])
        M_CX, M_WV = 6, 7
        onesf = sp_("onesf", [P, P])
        NB = 8
        bank = [st.enter_context(nc.psum_tensor(f"prep{i}", [P, 512], F32)) for i in range(NB)]
        blk = st.enter_context(nc.Block())

        vs = [("v", b) for b in range(B)]
        uses = ([("cx", 0), ("cx", 1), ("g",)] + [("k", g) for g in range(KT)] + vs[:1]
                + [("wo", k) for k in range(KT)] + vs[1:2] + [("wgT",)] + vs[2:3] + [("wg",), ("bo",)]
                + vs[3:] + [("gc",)])
        by_act = [u for u in uses if u == ("cx", 1) or u[0] in ("k", "v", "wo", "wg")]
        by_dve = [u for u in uses if u != ("cx", 1) and u[0] != "wo"]

        def ready(eng, *u):
            if u in by_dve:
                eng.wait_ge(sem("prep_dve"), by_dve.index(u) + 1)
            else:
                eng.wait_ge(sem("prep_act"), by_act.index(u) + 1)

        @blk.sync
        def _(sp):
            def load(dst, src, name):
                sp.dma_start(dst, src).then_inc(sem(name), 16)

            def by_feature(v):
                return v.rearrange("(t p) -> p t", p=P)

            load(cx[:], ctx.rearrange("b s d -> s b d"), "ld_cx")
            load(craw["k"][:], Wk.rearrange("(t p) n -> p t n", p=P), "ld_wk")
            load(craw["v"][:], Wv.rearrange("(t p) n -> p t n", p=P), "ld_wv")
            load(wraw["o"][:], Wo.rearrange("(t p) n -> p t n", p=P), "ld_wo")
            with nc.allow_non_contiguous_dma(reason="a few bias vectors by feature"):
                load(bvec[:, BV, :], by_feature(bv), "ld_bias")
                load(bvec[:, BO, :], by_feature(bo), "ld_bias")
                load(bvec[:, BQ, :], by_feature(bq), "ld_bias")
            load(wraw["q"][:], Wq.rearrange("(t p) n -> p t n", p=P), "ld_wq")
            load(bo_rep[:], bo.rearrange("(a n) -> a n", a=1).to_broadcast([P, DM]), "ld_bo_rep")
            load(xt[:, 0, :, :], xv[0], "x_in0")
            sp.wait_ge(sem("prep_dve"), by_dve.index(("k", KT - 1)) + 1)
            for part, half in ((0, 0), (1, 0), (2, 1)):
                for j in range(HG):
                    for b0, b1 in ((0, B), (B, B + 1)):
                        sp.dma_start(k_st[part * DK:(part + 1) * DK, j:H:HG, b0:b1, :],
                                     k_nat[half][j * DK:(j + 1) * DK, :, 0:b1 - b0, :].bitcast(F32))\
                            .then_inc(sem("k_stacked"), 16)
            load(xt[:, 1, :, :], xv[1], "x_in1")
            sp.wait_ge(sem("k_stacked"), 16 * 3 * HG * 2)
            load_keys(sp, 0)
            for c in range(2, 3):
                load(xt[:, c, :, :], xv[c], f"x_in{c}")
            for e in range(2):
                load(pay[:, e, :, 0:DM], expert_w[e].rearrange("(t p) h -> p t h", p=P), f"e_pre{e}")
            for e in range(EPRE):
                load(er_pre[:, e, :, :], expert_w[e].rearrange("(t p) h -> p t h", p=P), f"e_in{e}")

        @blk.gpsimd
        def _(pool):
            do = steps(pool, "pool_prep")
            do(nc.gpsimd.memset(ident[:], 0.0))
            nc.gpsimd.affine_select(out=ident[:], in_=ident[:], compare_op=ALU.not_equal, fill=1.0, base=0,
                                    pattern=[[-1, P]], channel_multiplier=1).then_inc(sem("ident_ready"), 1)
            nc.gpsimd.memset(zeros[:], 0.0)
            do(nc.gpsimd.memset(onesf[:], 1.0))
            do(nc.gpsimd.memset(sel32[:], 0.0))
            do(nc.gpsimd.affine_select(out=sel32[:], in_=sel32[:], compare_op=ALU.not_equal, fill=1.0, base=-3 * DK,
                                       pattern=[[-1, H], [0, LK]], channel_multiplier=1))
            pool.wait_ge(sem("v_zero"), 1)
            nc.gpsimd.memset(v_all[0][:, :, :, DK], 1.0).then_inc(sem("v_clear"), 1)
            reductions = [(M_CX, M_WV + 1), (S_WO, S_G + 1), (S_WQ, S_WQ + 1)]

            def reduce_max():
                c0, c1 = reductions.pop(0)
                pool.wait_ge(sem("mx_in"), 3 - len(reductions))
                nc.gpsimd.partition_all_reduce(mx[:, c0:c1], mx[:, c0:c1], P, bass.bass_isa.ReduceOp.max)\
                    .then_inc(sem("mx_out"), 1)

            reduce_max()
            reduce_max()
            reduce_max()
            pool.wait_ge(sem("mx_out"), 3)
            do(nc.gpsimd.tensor_copy(k_now[3 * DK:P, :, :], sel32[3 * DK:P, :, :]))
            for g in range(KT):
                nc.gpsimd.tensor_copy(k_cur[:, g, :], zeros[:]).then_inc(sem("k_cur_clear"), 1)
            do(nc.gpsimd.affine_select(out=onesf[:], in_=onesf[:], compare_op=ALU.is_gt, fill=0.0, base=0,
                                       pattern=[[1, P]], channel_multiplier=-1))
            do(nc.gpsimd.tensor_copy(tri[:], onesf[:]))
            do(nc.gpsimd.memset(ones[:], 1.0))
            nc.gpsimd.memset(pows[:, 0, :], -0.5)
            do(nc.gpsimd.memset(pows[:, 1, :], 0.5))
            wait_alone(pool, "ln_stats", 1)
            nc.gpsimd.tensor_tensor(std[:, 0, :], ve[:], pows[:, 1, :], ALU.pow)
            do(nc.gpsimd.tensor_tensor(rstd[:], ve[:], pows[:, 0, :], ALU.pow))
            do(nc.gpsimd.tensor_tensor(nmr[:], mv[:, :, 0], rstd[:], ALU.mult))
            nc.gpsimd.tensor_scalar(nmr[:], nmr[:], -1.0, None, ALU.mult).then_inc(sem("factors_ready"), 1)
            do(nc.gpsimd.iota(base[:], pattern=[[REGION, E]], base=0, channel_multiplier=0,
                              allow_small_or_imprecise_dtypes=True))
            do(nc.gpsimd.iota(weight8[:], pattern=[[-1, E]], base=E, channel_multiplier=0,
                              allow_small_or_imprecise_dtypes=True))
            do(nc.gpsimd.iota(token[:], pattern=[[P, TPC]], base=0, channel_multiplier=1,
                              allow_small_or_imprecise_dtypes=True))

        @blk.tensor
        def _(pe):
            pe.wait_ge(sem("ident_ready"), 1)

            def sum_of(dst, pairs):
                for n, (a, b_) in enumerate(pairs):
                    ins = nc.tensor.matmul(dst, a, b_, start=n == 0, stop=n == len(pairs) - 1)
                return ins

            for n, (kind, *at) in enumerate(uses):
                if n >= NB:
                    ready(pe, *uses[n - NB])
                ps = bank[n % NB]
                if kind == "cx":
                    k, = at
                    pe.wait_ge(sem("ld_cx"), 16)
                    for b in range(B):
                        last = nc.tensor.transpose(ps[:, b * LK:(b + 1) * LK], cx[:, b, k * P:(k + 1) * P],
                                                   ident[0:LK, 0:LK])
                elif kind == "k":
                    g, = at
                    pe.wait_ge(sem("ld_wk"), 16)
                    ready(pe, "cx", 0)
                    ready(pe, "cx", 1)
                    last = sum_of(ps[:, 0:B * LK], [(craw["k"][:, k, g * P:(g + 1) * P], cxT[:, k, :, :])
                                                    for k in range(CT)])
                elif kind == "v":
                    b, = at
                    pe.wait_ge(sem("ld_wv"), 16)
                    last = sum_of(ps[0:LK, :], [(cxT[:, k, b, :], craw["v"][:, k, :]) for k in range(CT)])
                elif kind == "g":
                    pe.wait_ge(sem("gate_centred"), 1)
                    for k in range(KT):
                        last = nc.tensor.transpose(ps[:, k * E:(k + 1) * E], gc8[:, k * P:(k + 1) * P],
                                                   ident[0:E, 0:E])
                elif kind == "wo":
                    k, = at
                    pe.wait_ge(sem("ld_wo"), 16)
                    for f in range(KT):
                        last = nc.tensor.transpose(ps[:, f * P:(f + 1) * P], wraw["o"][:, f, k * P:(k + 1) * P],
                                                   ident[:])
                elif kind == "wgT":
                    ready(pe, "g")
                    ready(pe, "wo", KT - 1)
                    last = sum_of(ps[0:E, :], [(gT[:, k, :], woT[:, k, :]) for k in range(KT)])
                elif kind == "wg":
                    ready(pe, "wgT")
                    for k in range(KT):
                        last = nc.tensor.transpose(ps[:, k * E:(k + 1) * E], wgT[:, k * P:(k + 1) * P],
                                                   ident[0:E, 0:E])
                elif kind == "bo":
                    pe.wait_ge(sem("bmat_ready"), 1)
                    last = sum_of(ps[:, :], [(bmat[:, 1, k, :], wraw["o"][:, k, :]) for k in range(KT)])
                elif kind == "gc":
                    ready(pe, "wg")
                    last = sum_of(ps[:, 0:E], [(bmat[:, s, k, :], w[:, k, :]) for s, w in ((0, gT), (1, wgf))
                                               for k in range(KT)])
                last.then_inc(sem("prep_filled"), 1)

        @blk.scalar
        def _(act):
            act.dma_start(g8[:], gate_w).then_inc(sem("ld_gate"), 16)
            with nc.allow_non_contiguous_dma(reason="a bias vector by feature"):
                act.dma_start(bvec[:, BK, :], bk.rearrange("(t p) -> p t", p=P)).then_inc(sem("ld_bk"), 16)

            def scaled(dst, src, col):
                act.wait_ge(sem(f"scale{col}"), 1)
                return nc.scalar.activation(dst, src, ACT.Identity, scale=scl[:, col:col + 1])

            def filled(*u):
                act.wait_ge(sem("prep_filled"), uses.index(u) + 1)
                return bank[uses.index(u) % NB]

            for u in by_act:
                kind, *at = u
                ps = filled(*u)
                if kind == "cx":
                    last = nc.scalar.activation(cxT[:, 1, :, :], ps[:, 0:B * LK].rearrange("p (b s) -> p b s", b=B),
                                                ACT.Copy)
                elif kind == "k":
                    g, = at
                    act.wait_ge(sem("ld_bk"), 16)
                    last = nc.scalar.activation(k_nat[0][:, g, :, :],
                                                ps[:, 0:B * LK].rearrange("p (b s) -> p b s", b=B), ACT.Identity,
                                                bias=bvec[:, BK, g:g + 1])
                elif kind == "v":
                    b, = at
                    act.wait_ge(sem("v_clear"), 1)
                    act.wait_ge(sem(f"scale{S_V}"), 1)
                    last = nc.scalar.activation(v_all[0][0:LK, b, :, 0:DK],
                                                ps[0:LK, :].rearrange("p (h k) -> p h k", h=H), ACT.Identity,
                                                scale=scl[0:LK, S_V:S_V + 1])
                elif kind == "wo":
                    last = nc.scalar.activation(woT[:, at[0], :], ps[:, :], ACT.Copy)
                elif kind == "wg":
                    nc.scalar.activation(wgf[:].rearrange("p k e -> p (k e)"), ps[:, 0:KT * E], ACT.Copy)
                    last = scaled(wg[0][:].rearrange("p k e -> p (k e)"), ps[:, 0:KT * E], S_WG)
                last.then_inc(sem("prep_act"), 1)
                if u == ("k", KT - 1):
                    act.wait_ge(sem("ld_bias"), 3 * 16)
                    nc.scalar.activation(bmat[:], bvec[:, BO:BV + 1, :].unsqueeze(3).to_broadcast([P, 2, KT, P]),
                                         ACT.Copy).then_inc(sem("bmat_ready"), 1)
                if u == vs[1]:
                    scaled(wo[0][:], wraw["o"][:], S_WO).then_inc(sem("wo_hi"), 1)
                if u == vs[2]:
                    scaled(wq[0][:], wraw["q"][:], S_WQ).then_inc(sem("wq_hi"), 1)
            act.wait_ge(sem("factors_ready"), 1)
            for t in range(TPC):
                nc.scalar.activation(xn[:, t, :], xt[:, 0, t, :], ACT.Identity, scale=rstd[:, t:t + 1],
                                     bias=nmr[:, t:t + 1]).then_inc(sem("xn_ready"), 1)

        @blk.vector
        def _(dve):
            do = steps(dve, "dve_prep")
            XY = mybir.AxisListType.XY

            def scales(c):
                col = slice(c, c + 1)
                do(nc.vector.tensor_scalar(mx[:, col], mx[:, col], 1e-25, None, ALU.max))
                do(nc.vector.tensor_scalar(inv[:, col].bitcast(I32), mx[:, col].bitcast(I32), 0x7F800000, None,
                                           ALU.bitwise_and))
                do(nc.vector.tensor_scalar(inv[:, col], inv[:, col], 1.0 / TOP, None, ALU.mult))
                do(nc.vector.reciprocal(scl[:, col], inv[:, col]))
                dve.sem_inc(sem(f"scale{c}"))

            def bound(c, a, b, terms):
                do(nc.vector.tensor_tensor(mx[:, c:c + 1], mx[:, a:a + 1], mx[:, b:b + 1], ALU.mult))
                do(nc.vector.tensor_scalar(mx[:, c:c + 1], mx[:, c:c + 1], float(terms), None, ALU.mult))

            def absmax(col, src, rows=P):
                return nc.vector.tensor_reduce(mx[0:rows, col:col + 1], src, XY, ALU.max,
                                               apply_absolute_value=True)

            def lo(dst, src, scale, hi):
                return nc.vector.scalar_tensor_tensor(out=dst, in0=src, scalar=scale, in1=hi, op0=ALU.mult,
                                                      op1=ALU.subtract)

            do(nc.vector.memset(mx[:], 0.0))
            nc.vector.memset(v_all[1][:], 0.0)
            nc.vector.memset(v_all[0][:], 0.0).then_inc(sem("v_zero"), 1)
            dve.wait_ge(sem("v_zero"), 1)
            dve.wait_ge(sem("ld_gate"), 16)
            do(nc.vector.tensor_reduce(gmean[:], g8[:], X, ALU.add))
            do(nc.vector.tensor_scalar(gmean[:], gmean[:], 1.0 / DM, None, ALU.mult))
            nc.vector.tensor_scalar(gc8[:], g8[:], gmean[:, 0:1], None, ALU.subtract).then_inc(sem("gate_centred"), 1)

            def after_cx():
                dve.wait_ge(sem("ld_cx"), 16)
                absmax(M_CX, cx[:], LK)
                dve.wait_ge(sem("ld_wv"), 16)
                absmax(M_WV, craw["v"][:]).then_inc(sem("mx_in"), 1)

            def before_k():
                absmax(S_G, gT[:])

            def before_v():
                dve.wait_ge(sem("mx_out"), 1)
                bound(S_V, M_CX, M_WV, DC)
                scales(S_V)
                dve.wait_ge(sem("ld_wo"), 16)
                absmax(S_WO, wraw["o"][:]).then_inc(sem("mx_in"), 1)

            def wq_max():
                dve.wait_ge(sem("ld_wq"), 16)
                absmax(S_WQ, wraw["q"][:]).then_inc(sem("mx_in"), 1)
                dve.wait_ge(sem("mx_out"), 2)
                scales(S_WO)
                scales(S_G)
                bound(S_WG, S_WO, S_G, DM)
                scales(S_WG)
                dve.wait_ge(sem("mx_out"), 3)
                scales(S_WQ)

            def wo_lo():
                dve.wait_ge(sem("wo_hi"), 1)
                lo(wo[1][:], wraw["o"][:], scl[:, S_WO:S_WO + 1], wo[0][:])

            def wq_lo():
                dve.wait_ge(sem("wq_hi"), 1)
                lo(wq[1][:], wraw["q"][:], scl[:, S_WQ:S_WQ + 1], wq[0][:])

            def gate_split():
                do(nc.vector.tensor_scalar(gt[0][:], gT[:], scl[:, S_G:S_G + 1], None, ALU.mult))
                lo(gt[1][:], gT[:], scl[:, S_G:S_G + 1], gt[0][:])
                nc.vector.tensor_scalar(bq_s[:], bvec[:, BQ, :], scl[:, S_WQ:S_WQ + 1], None, ALU.mult)
                nc.vector.tensor_scalar(exp_scale[:], inv[:, S_WQ:S_WQ + 1], SCALE, None, ALU.mult)
                nc.vector.tensor_tensor(inv_y[:], inv[:, S_WO:S_WO + 1], inv[:, S_V:S_V + 1], ALU.mult)
                nc.vector.tensor_tensor(inv_gc[:], inv[:, S_WG:S_WG + 1], inv[:, S_V:S_V + 1], ALU.mult)

            def chunk_0():
                dve.wait_ge(sem("x_in0"), 16)
                for t in range(TPC):
                    last = nc.vector.bn_stats(bst[:, t, :], xt[:, 0, t, :])
                do(last)
                for t in range(TPC):
                    last = nc.vector.bn_aggr(mv[:, t, :], bst[:, t, :])
                do(last)
                nc.vector.tensor_scalar(ve[:], mv[:, :, 1], EPS, None, ALU.add).then_inc(sem("ln_stats"), 1)

            jobs = {("cx", 0): after_cx, ("g",): before_k, ("k", KT - 1): before_v, vs[0]: wq_max, vs[1]: gate_split,
                    ("wgT",): chunk_0, ("bo",): wo_lo, vs[3]: wq_lo}
            for u in by_dve:
                kind, *at = u
                dve.wait_ge(sem("prep_filled"), uses.index(u) + 1)
                if u in by_act:
                    dve.wait_ge(sem("prep_act"), by_act.index(u) + 1)
                ps = bank[uses.index(u) % NB]
                if kind == "cx":
                    last = nc.vector.tensor_copy(cxT[:, 0, :, :], ps[:, 0:B * LK].rearrange("p (b s) -> p b s", b=B))
                elif kind == "g":
                    last = nc.vector.tensor_copy(gT[:].rearrange("p k e -> p (k e)"), ps[:, 0:KT * E])
                elif kind == "k":
                    g, = at
                    last = nc.vector.scalar_tensor_tensor(
                        out=k_nat[1][:, g, :, :], in0=ps[:, 0:B * LK].rearrange("p (b s) -> p b s", b=B),
                        scalar=bvec[:, BK, g:g + 1], in1=k_nat[0][:, g, :, :].bitcast(F32), op0=ALU.add,
                        op1=ALU.subtract)
                elif kind == "v":
                    b, = at
                    last = lo(v_all[1][0:LK, b, :, 0:DK], ps[0:LK, :].rearrange("p (h k) -> p h k", h=H),
                              scl[0:LK, S_V:S_V + 1], v_all[0][0:LK, b, :, 0:DK])
                elif kind == "wgT":
                    last = nc.vector.tensor_copy(wgT[:], ps[0:E, :])
                elif kind == "wg":
                    last = lo(wg[1][:].rearrange("p k e -> p (k e)"), ps[:, 0:KT * E], scl[:, S_WG:S_WG + 1],
                              wg[0][:].rearrange("p k e -> p (k e)"))
                elif kind == "bo":
                    dve.wait_ge(sem("ld_bo_rep"), 16)
                    last = nc.vector.tensor_tensor(bo_rep[:], ps[:, :], bo_rep[:], ALU.add)
                elif kind == "gc":
                    last = nc.vector.tensor_copy(gate_c[:], ps[:, 0:E])
                last.then_inc(sem("prep_dve"), 1)
                if u in jobs:
                    if u == ("g",):
                        dve.wait_ge(sem("prep_dve"), by_dve.index(u) + 1)
                    jobs[u]()
            dve.wait_ge(sem("k_cur_clear"), KT)
            build_k(0)
            stack_k(nc.vector, 0)
            dve.wait_ge(sem("prep_dve"), len(by_dve))
            copy_v(0)

    with ExitStack() as st:
        def sp_(name, shape, dt=F32):
            return sb(name, shape, dt, st)
        xnT = [sp_(f"xnT_{s}", [P, KT, CH], F16) for s in ("hi", "lo")]
        q = [sp_(f"q_{s}", [P, KT, CH], F32R) for s in ("hi", "lo")]
        q_st = sp_("q_st", [P, H, CH], F32R)
        negmax = sp_("negmax", [P, TPC, H])
        nmT = sp_("nmT", [H, CH], F32R)
        pf = sp_("pf", [LK, HG, CH])
        pp = [sp_(f"p_{s}", [VR, 2, HG, CH], F16) for s in ("hi", "lo")]
        den = sp_("den", [P, 2, 2, HG])
        cc = sp_("cc", [P, TPC, DM])
        cT = [sp_(f"cT_{s}", [P, KT, CH], F16) for s in ("hi", "lo")]
        bst2 = sp_("bst2", [P, TPC, 6])
        gx = sp_("gx", [P, 2, TPC, E])
        lg = sp_("lg", [P, TPC, E])
        lmax = sp_("lmax", [P, TPC])
        oh = sp_("oh", [P, TPC, E], BF16)
        slotf = sp_("slotf", [P, TPC])
        sbank = [st.enter_context(nc.psum_tensor(f"scoresT{c}", [P, 512], F32)) for c in range(SB)]
        obank = [st.enter_context(nc.psum_tensor(f"pv{c}", [P, 512], F32)) for c in range(2)]
        wbank = [st.enter_context(nc.psum_tensor(f"work{c}", [P, 512], F32)) for c in range(WB)]
        blk = st.enter_context(nc.Block())

        full = steps_of(True, True, True)
        assert len([st_ for st_ in full if st_[0] in BANKED]) % WB == 0

        def use(i, *what):
            return i.number(what, BANKED)

        def bank_of(i, *what):
            j = i if i.static else Chunk(0, 1)
            return wbank[j.number(what, BANKED) % WB]

        def iterations(eng, iteration):
            iteration(Chunk(0, -1))
            iteration(Chunk(0, 0))
            with eng.Fori(0, B - 1) as b:
                for c in range(CPB):
                    iteration(Chunk(b, c + 1))
            for c in range(CPB):
                iteration(Chunk(B - 1, c + 1))

        def has_ln(i):
            return not i.static or i.n + 2 < NCHUNK

        class OwnCount:

            def __init__(self, per):
                self.per, self.before, self.done = per, 0, 0

            def begin(self, i):
                if not i.static:
                    if i.c == 1:
                        self.before += self.done
                    else:
                        assert self.done == self.per, self.done
                    self.base = (i.n - 1) * self.per + self.before
                else:
                    self.before += self.done + (self.per * (CPB * (B - 1) - 1) if i.n == NCHUNK - 3 else 0)
                    self.base = self.before
                self.done = 0

            def value(self):
                return self.base + self.done

        def p_lo(tt, eng, i, g, j):
            wait_alone(eng, "exp_done", H * i.n + g * HG + j + 1 + SB)
            return tt.tensor_tensor(pp[1][0:LK, g % 2, j, :], pf[:, j, :], pp[0][0:LK, g % 2, j, :], ALU.subtract)

        @blk.sync
        def _(sp):
            def pass_expert(e):
                sp.wait_ge(sem("e_summed"), e - 1)
                sp.dma_start(pay[:, e % 2, :, 0:DM], expert_w[e].rearrange("(t p) h -> p t h", p=P))\
                    .then_inc(sem(f"e_pre{e % 2}"), 16)

            def iteration(i):
                if not i.is_(-1) and not i.is_(NCHUNK):
                    sp.wait_ge(sem("work_used"), use(i, "NM") + 1)
                    sp.dma_start(q_st[3 * DK:KR, :, :].bitcast(F32),
                                 nmT[:].bitcast(F32).unsqueeze(1).to_broadcast([H, H, CH])).then_inc(sem("max_stacked"), 16)
                if i.is_(0):
                    pass_expert(KT)
                    pass_expert(KT + 1)
                if not i.static or 1 <= i.n <= NCHUNK - 3:
                    n = i.plus(2)
                    wait_alone(sp, "work_used", use(i.plus(-1), "O", TPC - 1) + 1)
                    sp.dma_start(xt[:, n.slot, :, :],
                                 xv[bass.ds(n.n, 1), :, :, :].rearrange("a p t d -> p (a t) d"))\
                        .then_inc(sem(f"x_in{n.slot}"), 16)
                if i.slot == 0 and 0 <= (i.n if i.static else 1) < NCHUNK:
                    wait_alone(sp, "stack_built", i.batch + 1)
                    load_keys(sp, i.batch + 1)
                for kind, *at in i.steps():
                    if kind == "Q":
                        g, = at
                        if g % 2 or i.static:
                            sp.wait_ge(sem("work_used"), use(i, "Q", g) + 1)
                        for part, half in ((0, 0), (1, 1), (2, 0)) if g % 2 else ():
                            for j in range(HG):
                                sp.dma_start(
                                    q_st[part * DK:(part + 1) * DK, (g - 1) * HG + j:(g + 1) * HG:HG, :].bitcast(F32),
                                    q[half][j * DK:(j + 1) * DK, g - 1:g + 1, :].bitcast(F32))\
                                    .then_inc(sem(f"q_stacked{g // 2}"), 16)
                        if g < 2 and (i.is_(-1) or i.is_(0)):
                            pass_expert((i.n + 1) * KT + g + 2)

            iterations(sp, iteration)
            sp.wait_ge(sem("keys_in"), 16 * (B + 1))

        @blk.gpsimd
        def _(pool):
            own = OwnCount(4)

            def do(ins):
                own.done += 1
                ins.then_inc(sem("pool_step"), 1)
                wait_alone(pool, "pool_step", own.value())

            def ln(n):
                wait_alone(pool, "ln_stats", n.n + 1)
                if not n.is_(0):
                    wait_alone(pool, "xn_ready", TPC * n.n)
                nc.gpsimd.tensor_tensor(std[:, n.slot % 2, :], ve[:], pows[:, 1, :], ALU.pow)
                do(nc.gpsimd.tensor_tensor(rstd[:], ve[:], pows[:, 0, :], ALU.pow))
                do(nc.gpsimd.tensor_tensor(nmr[:], mv[:, :, 0], rstd[:], ALU.mult))
                nc.gpsimd.tensor_scalar(nmr[:], nmr[:], -1.0, None, ALU.mult).then_inc(sem("factors_ready"), 1)

            def x_plus_bo(i, t):
                if t == 0 and not i.is_(0):
                    wait_alone(pool, "xn_ready", TPC * (i.n + 1))
                nc.gpsimd.tensor_tensor(xt[:, i.slot, t, :], xt[:, i.slot, t, :], bo_rep[:], ALU.add)\
                    .then_inc(sem("x_plus_bo"), 1)

            def rows_out(i):
                m = i.plus(-1)
                scatter(m, pool)
                pool.wait_ge(sem("scattered"), 16 * TPC * (m.n + 1))
                pool.sem_inc(sem("rows_left"))

            def iteration(i):
                own.begin(i)
                for kind, *at in i.steps(GPSIMD):
                    if kind == "F":
                        ln(i.plus(2))
                    elif kind == "A":
                        x_plus_bo(i, *at)
                    elif kind == "P":
                        p_lo(nc.gpsimd, pool, i, *at).then_inc(sem("p_lo_pool"), 1)
                        if at == [KT - 1, HG - 1] and i.slot == CPB - 1 and not i.is_(NCHUNK - 1):
                            stack_k(nc.gpsimd, i.plus(1).batch)
                    elif i.is_(NCHUNK):
                        pass
                    elif kind == "G":
                        row_factors(i.plus(-1), pool, do)
                    else:
                        rows_out(i)

            for p_ in pp:
                nc.gpsimd.memset(p_[:], 0.0).then_inc(sem("p_clear"), 1)
            iterations(pool, iteration)

        @blk.tensor
        def _(pe):
            HL = ((0, 0), (1, 0), (0, 1))

            def product(dst, a, bm, first=True, final=True):
                for n, (ia, ib) in enumerate(HL):
                    ins = nc.tensor.matmul(dst, a[ia], bm[ib], start=first and n == 0, stop=final and n == 2)
                return ins

            def used(i, *what):
                pe.wait_ge(sem("work_used"), use(i, *what) + 1)

            def transposed(ps, src):
                for k in range(KT):
                    ins = nc.tensor.transpose(ps[:, k * P:(k + 1) * P], src[:, k * P:(k + 1) * P], ident[:])
                return ins

            def scores(i, g, j):
                n = g * HG + j
                if n == 0:
                    pe.wait_ge(sem("max_stacked"), 16 * (i.n + 1))
                if j == 0 and g % 2 == 0:
                    pe.wait_ge(sem(f"q_stacked{g // 2}"), 16 * 3 * HG * (i.n + 1))
                pe.wait_ge(sem("exp_done"), H * i.n + n + 1)
                if n == 0:
                    pe.wait_ge(sem("stack_built"), i.batch + 1)
                nc.tensor.matmul(sbank[n % SB][0:LK, :], k_now[0:KR, n, :], q_st[0:KR, n, :], start=True, stop=True)\
                    .then_inc(sem("scores_ready"), 1)

            def values(i, g):
                G = KT * i.n + g
                if g == 0:
                    pe.wait_ge(sem("v_built"), i.batch + 1)
                pe.wait_ge(sem("p_lo_ready"), P_DVE * (G + 1) + HG)
                pe.wait_ge(sem("p_lo_pool"), (HG - P_DVE) * (G + 1) + HG)
                for h in range(2):
                    pe.wait_ge(sem("normalised"), 2 * G + h + 1)
                    for t in (2 * h, 2 * h + 1):
                        for j in range(HG):
                            col = ((t % 2) * HG + j) * VC
                            for n, (ip, iv) in enumerate(HL):
                                ins = nc.tensor.matmul(obank[h][:, col:col + VC],
                                                       pp[ip][:, g % 2, j, t * P:(t + 1) * P],
                                                       v_now[iv][:, g * HG + j, :],
                                                       start=n == 0, stop=n == 2)
                    ins.then_inc(sem("values_ready"), 1)

            def banked(i, kind, *at):
                k = use(i, kind, *at)
                if not (i.is_(-1) and k < WB):
                    pe.wait_ge(sem("work_used"), k - WB + 1)
                ps = bank_of(i, kind, *at)
                if kind == "T":
                    pe.wait_ge(sem("xn_ready"), i.plus(1).n * TPC + at[0] + 1)
                    return transposed(ps, xn[:, at[0], :])
                if kind == "C":
                    pe.wait_ge(sem("normalised"), 2 * KT * i.n + 2)
                    return transposed(ps, cc[:, at[0], :])
                if kind == "Q":
                    g, = at
                    if g == 0:
                        used(i, "T", TPC - 1)
                    for k in range(KT):
                        ins = product(ps[:, :], [w[:, k, g * P:(g + 1) * P] for w in wq], [v[:, k, :] for v in xnT],
                                      k == 0, k == KT - 1)
                    return ins
                if kind == "M":
                    g, t = at
                    if t == 0:
                        used(i, "Q", g)
                        pe.wait_ge(sem("k_built"), i.plus(1).batch + 1)
                    return nc.tensor.matmul(ps[:, 0:HG * LK], q[0][:, g, t * P:(t + 1) * P], k_cur[:, g, :],
                                            start=True, stop=True)
                if kind == "NM":
                    used(i.plus(-1), "M", KT - 1, TPC - 1)
                    for t in range(TPC):
                        ins = nc.tensor.transpose(ps[0:H, t * P:(t + 1) * P], negmax[:, t, :], ident[:])
                    return ins
                if kind in ("GX", "GC"):
                    a, w = (xnT, gt) if kind == "GX" else (cT, wg)
                    used(i, "T" if kind == "GX" else "C", TPC - 1)
                    for t in range(TPC):
                        for k in range(KT):
                            ins = product(ps[:, t * E:(t + 1) * E], [v[:, k, t * P:(t + 1) * P] for v in a],
                                          [v[:, k, :] for v in w], k == 0, k == KT - 1)
                    return ins
                if kind == "O":
                    t, = at
                    used(i, "C", t)
                    for k in range(KT):
                        ins = product(ps[:, :], [v[:, k, t * P:(t + 1) * P] for v in cT], [w[:, k, :] for w in wo],
                                      k == 0, k == KT - 1)
                    return ins
                pe.wait_ge(sem("one_hot"), i.n)
                for t in range(TPC):
                    for s_ in range(t + 1):
                        nc.tensor.matmul(ps[:, t * E:(t + 1) * E], tri[:] if s_ == t else ones[:], oh[:, s_, :],
                                         start=s_ == 0, stop=s_ == t)
                for s_ in range(TPC):
                    ins = nc.tensor.matmul(ps[:, TPC * E:(TPC + 1) * E], ones[:], oh[:, s_, :],
                                           start=s_ == 0, stop=s_ == TPC - 1)
                return ins

            def iteration(i):
                for kind, *at in i.steps():
                    if kind == "S":
                        scores(i, *at)
                    elif kind == "PV":
                        values(i, *at)
                    else:
                        banked(i, kind, *at).then_inc(sem("work_filled"), 1)

            iterations(pe, iteration)

        @blk.scalar
        def _(act):
            act.nop().then_inc(sem("exp_done"), SB)

            def normalised_x(n, t):
                if t == 0:
                    act.wait_ge(sem("factors_ready"), n.n + 1)
                nc.scalar.activation(xn[:, t, :], xt[:, n.slot, t, :], ACT.Identity, scale=rstd[:, t:t + 1],
                                     bias=nmr[:, t:t + 1]).then_inc(sem("xn_ready"), 1)

            def sum_expert(n):
                act.wait_ge(sem(f"e_pre{n % 2}"), 16 * (n // 2 + 1))
                w = pay[:, n % 2, :, 0:DM]
                nc.scalar.activation(w, w, ACT.Abs, accum_out=e_sum[:, n:n + 1]).then_inc(sem("e_summed"), 1)

            def iteration(i):
                for kind, *at in i.steps(SCALAR):
                    if kind == "X":
                        act.wait_ge(sem("work_filled"), use(i, "T", *at) + 1)
                        normalised_x(i.plus(2), *at)
                    elif kind in SPLIT:
                        act.wait_ge(sem("work_filled"), use(i, kind, *at) + 1)
                        ps = bank_of(i, kind, *at)
                        if kind == "Q":
                            ins = nc.scalar.activation(q[0][:, at[0], :], ps[:, :], ACT.Identity,
                                                       bias=bq_s[:, at[0]:at[0] + 1])
                        else:
                            dst = (xnT if kind == "T" else cT)[0][:, :, at[0] * P:(at[0] + 1) * P]
                            ins = nc.scalar.activation(dst, ps[:, :].rearrange("p (k n) -> p k n", k=KT), ACT.Copy)
                        ins.then_inc(sem("hi_ready"), 1)
                        if kind == "Q" and (i.is_(-1) or i.is_(0)):
                            sum_expert((i.n + 1) * KT + at[0])
                    elif kind == "S":
                        g, j = at
                        G = KT * i.n + g
                        if j == 0:
                            act.wait_ge(sem("values_ready"), 2 * G + 2)
                        if j < P_DVE:
                            act.wait_ge(sem("p_lo_ready"), P_DVE * (G - 1) + j + 1 + HG)
                        else:
                            act.wait_ge(sem("p_lo_pool"), (HG - P_DVE) * (G - 1) + j - P_DVE + 1 + HG)
                        n = g * HG + j
                        if i.is_(0) and n == 0:
                            act.wait_ge(sem("p_clear"), 2)
                        act.wait_ge(sem("scores_ready"), H * i.n + n + 1)
                        nc.scalar.activation(pf[:, j, :], sbank[n % SB][0:LK, :], ACT.Exp, scale=exp_scale[0:LK, :])
                        nc.scalar.activation(pp[0][0:LK, g % 2, j, :], sbank[n % SB][0:LK, :], ACT.Exp,
                                             scale=exp_scale[0:LK, :]).then_inc(sem("exp_done"), 1)

            iterations(act, iteration)

        @blk.vector
        def _(dve):
            own = OwnCount(21)

            def mark(ins):
                own.done += 1
                ins.then_inc(sem("dve_step"), 1)

            def do(ins):
                mark(ins)
                dve.wait_ge(sem("dve_step"), own.value())

            dve.nop().then_inc(sem("normalised"), 2)
            dve.nop().then_inc(sem("values_ready"), 4)
            dve.nop().then_inc(sem("rows_left"), 2)
            dve.nop().then_inc(sem("pay_stats"), 1)
            dve.nop().then_inc(sem("p_lo_ready"), HG)
            dve.nop().then_inc(sem("p_lo_pool"), HG)

            def ln_stats(n, t):
                if t == 0:
                    dve.wait_ge(sem(f"x_in{n.slot}"), 16 * (n.batch + 1))
                ins = nc.vector.bn_stats(bst[:, t, :], xt[:, n.slot, t, :])
                if t == TPC - 1:
                    mark(ins)

            def ln_end(n):
                wait_alone(dve, "dve_step", own.value())
                if not n.is_(0):
                    wait_alone(dve, "factors_ready", n.n)
                for t in range(TPC):
                    ins = nc.vector.bn_aggr(mv[:, t, :], bst[:, t, :])
                do(ins)
                nc.vector.tensor_scalar(ve[:], mv[:, :, 1], EPS, None, ALU.add).then_inc(sem("ln_stats"), 1)

            def ln(n):
                for t in range(TPC):
                    ln_stats(n, t)
                ln_end(n)

            def lo(i, kind, at):
                dve.wait_ge(sem("hi_ready"), i.number((kind, at), SPLIT) + 1)
                ps = bank_of(i, kind, at)
                if kind == "Q":
                    ins = nc.vector.scalar_tensor_tensor(out=q[1][:, at, :], in0=ps[:, :], scalar=bq_s[:, at:at + 1],
                                                         in1=q[0][:, at, :].bitcast(F32), op0=ALU.add,
                                                         op1=ALU.subtract)
                else:
                    dst = [v[:, :, at * P:(at + 1) * P] for v in (xnT if kind == "T" else cT)]
                    ins = nc.vector.tensor_tensor(dst[1], ps[:, :].rearrange("p (k n) -> p k n", k=KT), dst[0],
                                                  ALU.subtract)
                ins.then_inc(sem("work_used"), 1)

            def normalise(i, g, h):
                dve.wait_ge(sem("values_ready"), 2 * (KT * i.n + g) + h + 1 + 4)
                o = obank[h][:, 0:2 * HG * VC].rearrange("p (t j k) -> p t j k", t=2, j=HG)
                do(nc.vector.reciprocal(den[:, h, :, :], o[:, :, :, DK]))
                nc.vector.tensor_tensor(
                    cc[:, 2 * h:2 * h + 2, g * P:(g + 1) * P].rearrange("p t (j k) -> p t j k", j=HG),
                    o[:, :, :, 0:DK], den[:, h, :, :].unsqueeze(3).to_broadcast([P, 2, HG, DK]), ALU.mult)\
                    .then_inc(sem("normalised"), 1)

            def by_tile(ps):
                return ps[:, 0:TPC * E].rearrange("p (t e) -> p t e", t=TPC)

            def banked(i, kind, *at):
                dve.wait_ge(sem("work_filled"), use(i, kind, *at) + 1)
                ps = bank_of(i, kind, *at)
                if kind == "M":
                    g, t = at
                    return nc.vector.tensor_reduce(negmax[:, t, g * HG:(g + 1) * HG],
                                                   ps[:, 0:HG * LK].rearrange("p (j s) -> p j s", j=HG), X, ALU.max,
                                                   negate=True)
                if kind == "NM":
                    return nc.vector.tensor_copy(nmT[:], ps[0:H, :])
                if kind == "GX":
                    n = i.plus(1).slot
                    do(nc.vector.tensor_tensor(gx[:, n % 2], by_tile(ps), std[:, n % 2, :].unsqueeze(2)
                                               .to_broadcast([P, TPC, E]), ALU.mult))
                    return nc.vector.scalar_tensor_tensor(out=gx[:, n % 2], in0=gx[:, n % 2], scalar=inv[:, S_G:S_G + 1],
                                                          in1=gate_c[:].unsqueeze(1).to_broadcast([P, TPC, E]),
                                                          op0=ALU.mult, op1=ALU.add)
                m = i.plus(-1)
                par = m.slot % 2
                if kind == "O":
                    t, = at
                    if t == 0:
                        dve.wait_ge(sem("rows_left"), m.n + 1)
                    dve.wait_ge(sem("x_plus_bo"), TPC * m.n + t + 1)
                    return nc.vector.scalar_tensor_tensor(out=pay[:, par, t, 0:DM], in0=ps[:, :], scalar=inv_y[:],
                                                          in1=xt[:, m.slot, t, :], op0=ALU.mult, op1=ALU.add)
                if kind == "GC":
                    return nc.vector.scalar_tensor_tensor(out=lg[:], in0=by_tile(ps), scalar=inv_gc[:], in1=gx[:, m.slot % 2],
                                                          op0=ALU.mult, op1=ALU.add)
                do(nc.vector.tensor_tensor(lg[:], by_tile(ps), base[:].unsqueeze(1).to_broadcast([P, TPC, E]),
                                           ALU.add))
                return nc.vector.tensor_tensor(base[:], ps[:, TPC * E:(TPC + 1) * E], base[:], ALU.add)

            def one_hot(i):
                dve.wait_ge(sem("work_used"), use(i, "GC") + 1)
                do(nc.vector.tensor_reduce(lmax[:], lg[:], X, ALU.max))
                do(nc.vector.tensor_tensor(lg[:], lg[:], lmax[:].unsqueeze(2).to_broadcast([P, TPC, E]), ALU.is_ge))
                do(nc.vector.tensor_tensor(lg[:], lg[:], weight8[:].unsqueeze(1).to_broadcast([P, TPC, E]), ALU.mult))
                do(nc.vector.tensor_reduce(lmax[:], lg[:], X, ALU.max))
                nc.vector.tensor_tensor(oh[:], lg[:], lmax[:].unsqueeze(2).to_broadcast([P, TPC, E]), ALU.is_equal)\
                    .then_inc(sem("one_hot"), 1)

            def ln2_stats(i, t):
                dve.wait_ge(sem("work_used"), use(i, "O", t) + 1)
                ins = nc.vector.bn_stats(bst2[:, t, :], pay[:, i.plus(-1).slot % 2, t, 0:DM])
                if t == TPC - 1:
                    mark(ins)

            def ln2_end(i):
                wait_alone(dve, "dve_step", own.value())
                wait_alone(dve, "pay_stats", i.n)
                for t in range(TPC):
                    ins = nc.vector.bn_aggr(mv2[:, t, :], bst2[:, t, :])
                do(ins)
                nc.vector.tensor_scalar(ve2[:], mv2[:, :, 1], EPS, None, ALU.add).then_inc(sem("ln2_stats"), 1)

            def slots(i):
                par = i.plus(-1).slot % 2
                dve.wait_ge(sem("work_used"), use(i, "R") + 1)
                do(nc.vector.tensor_tensor(lg[:], lg[:], oh[:], ALU.mult))
                do(nc.vector.tensor_reduce(slotf[:], lg[:], X, ALU.add))
                nc.vector.tensor_copy(slot[:, par, :], slotf[:])
                do(nc.vector.tensor_copy(pay[:, par, :, C_ID].bitcast(I32), token[:]))
                nc.vector.tensor_scalar(token[:], token[:], float(CH), None, ALU.add).then_inc(sem("slot_ready"), 1)

            own_parts = {
                "P": lambda i, g, j: p_lo(nc.vector, dve, i, g, j).then_inc(sem("p_lo_ready"), 1), "V": normalise, "B": ln2_stats, "VE": ln2_end, "H": one_hot, "SL": slots,
                "L": lambda i, t: ln_stats(i.plus(2), t), "LE": lambda i: ln_end(i.plus(2)),
            }

            def iteration(i):
                own.begin(i)
                if i.is_(-1):
                    ln(Chunk(0, 1))
                for kind, *at in i.steps(VECTOR):
                    if kind in SPLIT:
                        lo(i, kind, *at)
                    elif kind in BANKED:
                        banked(i, kind, *at).then_inc(sem("work_used"), 1)
                    elif kind == "K":
                        if i.slot == CPB - 1 and not i.is_(NCHUNK - 1):
                            dve.wait_ge(sem("work_used"), use(i.plus(-1), "M", KT - 1, TPC - 1) + 1)
                            build_k(i.plus(1).batch)
                    elif kind in NEXT and i.is_(-1):
                        pass
                    else:
                        own_parts[kind](i, *at)
                        if (kind, *at) == ("V", KT - 1, 1) and i.slot == CPB - 1 and not i.is_(NCHUNK - 1):
                            copy_v(i.plus(1).batch)

            iterations(dve, iteration)
    attention.close()

    e_w = [sb(f"e_{s}", [P, E, KT, DM], F16) for s in ("hi", "lo")]
    U = UNROLL
    row = sb("row", [P, U, ROW])
    tab = sb("tab", [P, 2, NTILE], I32)

    def load_rows(sp, t, u):
        first = sp.value_load(tab[0:1, 0, bass.ds(t, 1)], min_val=0, max_val=E * REGION)
        sp.dma_start(row[:, u, :], rows[bass.ds(first, P), :]).then_inc(sem(f"row_in{u}"), 16)

    with ExitStack() as st:
        def sp_(name, shape, dt=F32):
            return sb(name, shape, dt, st)
        er = sp_("er", [P, E - EPRE, KT, DM])
        mx = sp_("mx_e", [P, 1])
        zrow = sp_("zrow", [P, ROW])
        row_p = sp_("row_p", [P, 1])
        region = sp_("region", [P, E])
        ntf = sp_("ntf", [P, E])
        nti = sp_("nti", [P, E], I32)
        cum = sp_("cum", [P, E])
        jump = sp_("jump", [P, E])
        tile = sp_("tile", [P, NTILE])
        start = sp_("start", [P, NTILE])
        which = sp_("which", [P, NTILE])
        ge = sp_("ge", [P, NTILE, E])
        moved = sp_("moved", [P, NTILE, E])
        padf = sp_("padf", [P, E])
        pads = sp_("pads", [P, E], I32)
        NBK = 8
        bank = [st.enter_context(nc.psum_tensor(f"ex{i}", [P, 512], F32)) for i in range(NBK)]
        blk = st.enter_context(nc.Block())

        @blk.sync
        def _(sp):
            for e in range(EPRE, E):
                if e >= EPRE + 3:
                    sp.wait_ge(sem("e_transposed"), KT * (e - 3))
                sp.dma_start(er[:, e - EPRE, :, :], expert_w[e].rearrange("(t p) h -> p t h", p=P))\
                    .then_inc(sem(f"e_in{e}"), 16)
            sp.wait_ge(sem("table_ready"), 1)
            sp.wait_ge(sem("padded"), 16 * (E + 1))
            sp.wait_ge(sem("scattered"), 16 * TPC * NCHUNK)
            for u in range(U):
                load_rows(sp, u, u)

        @blk.gpsimd
        def _(pool):
            do = steps(pool, "pool_experts")
            do(nc.gpsimd.iota(region[:], pattern=[[REGION, E]], base=0, channel_multiplier=0,
                              allow_small_or_imprecise_dtypes=True))
            do(nc.gpsimd.iota(row_p[:], pattern=[[0, 1]], base=0, channel_multiplier=1,
                              allow_small_or_imprecise_dtypes=True))
            do(nc.gpsimd.iota(tile[:], pattern=[[1, NTILE]], base=0, channel_multiplier=0,
                              allow_small_or_imprecise_dtypes=True))
            do(nc.gpsimd.memset(zrow[:], 0.0))
            do(nc.gpsimd.memset(zrow[:, C_ID:C_ID + 1].bitcast(I32), 1 << 20))
            pool.nop().then_inc(sem("e_consts"), 1)
            last = Chunk(B - 1, CPB - 1)
            row_factors(last, pool, do)
            pool.wait_ge(sem("e_max"), 1)
            nc.gpsimd.partition_all_reduce(mx[:], mx[:], P, bass.bass_isa.ReduceOp.max).then_inc(sem("e_max_all"), 1)
            scatter(last, pool)
            nc.gpsimd.dma_start(rows[E * REGION:E * REGION + P, :], zrow[:]).then_inc(sem("padded"), 16)
            pool.wait_ge(sem("pads_ready"), 1)
            for e in range(E):
                nc.gpsimd.indirect_dma_start(
                    out=rows, out_offset=bass.IndirectOffsetOnAxis(ap=pads[:, e:e + 1], axis=0),
                    in_=zrow[:], in_offset=None).then_inc(sem("padded"), 16)
            pool.wait_ge(sem("padded"), 16 * (E + 1))
            pool.wait_ge(sem("scattered"), 16 * TPC * NCHUNK)

        order = [(e, k) for e in range(E) for k in range(KT)]

        @blk.tensor
        def _(pe):
            for n, (e, k) in enumerate(order):
                pe.wait_ge(sem(f"e_in{e}"), 16)
                src = (er_pre[:, e] if e < EPRE else er[:, e - EPRE])[:, :, k * P:(k + 1) * P]
                if n >= NBK:
                    pe.wait_ge(sem("e_lo"), n - NBK + 1)
                for f in range(KT):
                    ins = nc.tensor.transpose(bank[n % NBK][:, f * P:(f + 1) * P], src[:, f, :], ident[:])
                ins.then_inc(sem("e_transposed"), 1)

        @blk.scalar
        def _(act):
            act.wait_ge(sem("e_scale"), 1)
            for n, (e, k) in enumerate(order):
                act.wait_ge(sem("e_transposed"), n + 1)
                nc.scalar.activation(e_w[0][:, e, k, :], bank[n % NBK][:, :], ACT.Identity,
                                     scale=scl[:, S_E:S_E + 1]).then_inc(sem("e_hi"), 1)

        @blk.vector
        def _(dve):
            do = steps(dve, "dve_experts")
            nc.vector.tensor_reduce(mx[:], e_sum[:], X, ALU.max).then_inc(sem("e_max"), 1)
            dve.wait_ge(sem("e_consts"), 1)
            do(nc.vector.tensor_scalar(padf[:], base[:], row_p[:], None, ALU.add))
            nc.vector.tensor_copy(pads[:], padf[:]).then_inc(sem("pads_ready"), 1)
            dve.wait_ge(sem("e_max_all"), 1)
            c = slice(S_E, S_E + 1)
            do(nc.vector.tensor_scalar(mx[:], mx[:], 1e-25, None, ALU.max))
            do(nc.vector.tensor_scalar(inv[:, c].bitcast(I32), mx[:].bitcast(I32), 0x7F800000, None,
                                       ALU.bitwise_and))
            do(nc.vector.tensor_scalar(inv[:, c], inv[:, c], 1.0 / TOP, None, ALU.mult))
            nc.vector.reciprocal(scl[:, c], inv[:, c]).then_inc(sem("e_scale"), 1)
            do(nc.vector.tensor_tensor(ntf[:], base[:], region[:], ALU.subtract))
            do(nc.vector.tensor_scalar(ntf[:], ntf[:], float(P - 1), None, ALU.add))
            do(nc.vector.tensor_copy(nti[:], ntf[:]))
            do(nc.vector.tensor_scalar(nti[:], nti[:], 7, None, ALU.logical_shift_right))
            do(nc.vector.tensor_copy(ntf[:], nti[:]))
            do(nc.vector.tensor_scalar(jump[:], ntf[:], -float(P), float(REGION), ALU.mult, ALU.add))
            do(nc.vector.tensor_copy(cum[:], ntf[:]))
            for e in range(1, E):
                do(nc.vector.tensor_tensor(cum[:, e:e + 1], cum[:, e:e + 1], cum[:, e - 1:e], ALU.add))
            every = [P, NTILE, E]
            do(nc.vector.tensor_tensor(ge[:], tile[:].unsqueeze(2).to_broadcast(every),
                                       cum[:].unsqueeze(1).to_broadcast(every), ALU.is_ge))
            do(nc.vector.tensor_tensor(moved[:], ge[:], jump[:].unsqueeze(1).to_broadcast(every), ALU.mult))
            do(nc.vector.tensor_reduce(which[:], ge[:], X, ALU.add))
            do(nc.vector.tensor_reduce(start[:], moved[:], X, ALU.add))
            do(nc.vector.scalar_tensor_tensor(out=start[:], in0=tile[:], scalar=float(P), in1=start[:], op0=ALU.mult,
                                              op1=ALU.add))
            do(nc.vector.tensor_scalar(start[:], start[:], float(E * REGION), None, ALU.min))
            do(nc.vector.tensor_scalar(which[:], which[:], float(E - 1), None, ALU.min))
            nc.vector.tensor_copy(tab[:, 0, :], start[:])
            nc.vector.tensor_copy(tab[:, 1, :], which[:]).then_inc(sem("table_ready"), 1)
            for n, (e, k) in enumerate(order):
                dve.wait_ge(sem("e_hi"), n + 1)
                nc.vector.scalar_tensor_tensor(out=e_w[1][:, e, k, :], in0=bank[n % NBK][:, :], scalar=scl[:, c],
                                               in1=e_w[0][:, e, k, :], op0=ALU.mult, op1=ALU.subtract)\
                    .then_inc(sem("e_lo"), 1)

    with ExitStack() as st:
        def sp_(name, shape, dt=F32):
            return sb(name, shape, dt, st)
        xn2 = sp_("xn2", [P, U, DM])
        x2T = [sp_(f"x2T_{s}", [P, 2, KT, P], F16) for s in ("hi", "lo")]
        res = sp_("res", [P, U, DM])
        tbank = [st.enter_context(nc.psum_tensor(f"mt{i}", [P, 512], F32)) for i in range(2)]
        obank2 = [st.enter_context(nc.psum_tensor(f"mo{i}", [P, 512], F32)) for i in range(2)]
        blk = st.enter_context(nc.Block())
        assert NTILE % U == 0

        def tiles(eng, body):
            with eng.Fori(0, NTILE // U - 1) as k:
                for u in range(U):
                    body(k * U + u, k, u)
            for u in range(U):
                body(NTILE - U + u, NTILE // U - 1, u)

        def has(t):
            return not isinstance(t, int) or t < NTILE

        @blk.sync
        def _(sp):
            with sp.Fori(1, NTILE // U) as k:
                for u in range(U):
                    sp.wait_ge(sem(f"out{u}"), 16 * k)
                    load_rows(sp, k * U + u, u)

        @blk.gpsimd
        def _(pool):
            def add(t, u):
                wait_alone(pool, "xn2_ready", t + 1)
                nc.gpsimd.tensor_tensor(row[:, u, 0:DM], row[:, u, 0:DM], xn2[:, u, :], ALU.add)\
                    .then_inc(sem("sum_ready"), 1)

            def body(t, k, u):
                if has(t + 1):
                    add(t + 1, (u + 1) % U)
                wait_alone(pool, "res_ready", t + 1 + 2)
                nc.gpsimd.indirect_dma_start(
                    out=out_rows, out_offset=bass.IndirectOffsetOnAxis(ap=row[:, u, C_ID:C_ID + 1].bitcast(I32), axis=0),
                    in_=res[:, u, :], in_offset=None, bounds_check=NTOK - 1, oob_is_err=False)\
                    .then_inc(sem(f"out{u}"), 16)

            add(0, 0)
            tiles(pool, body)
            for u in range(U):
                wait_alone(pool, f"out{u}", 16 * (NTILE // U))

        @blk.tensor
        def _(pe):
            HL = ((0, 0), (1, 0), (0, 1))

            def tr(t, u):
                pe.wait_ge(sem("xn2_ready"), t + 1)
                pe.wait_ge(sem("t_used"), t + 1)
                for k in range(KT):
                    ins = nc.tensor.transpose(tbank[u % 2][:, k * P:(k + 1) * P], xn2[:, u, k * P:(k + 1) * P],
                                              ident[:])
                ins.then_inc(sem("t_filled"), 1)

            def mm(t, u):
                e = pe.value_load(tab[0:1, 1, bass.ds(t, 1)], min_val=0, max_val=E - 1)
                pe.wait_ge(sem("t_used"), t + 1 + 2)
                pe.wait_ge(sem("res_ready"), t + 1)
                for k in range(KT):
                    for n, (ia, ib) in enumerate(HL):
                        w = e_w[ib][:, bass.ds(e, 1), k, :].rearrange("p a n -> p (a n)")
                        ins = nc.tensor.matmul(obank2[u % 2][:, :], x2T[ia][:, u % 2, k, :], w,
                                               start=k == 0 and n == 0, stop=k == KT - 1 and n == 2)
                ins.then_inc(sem("o_filled"), 1)

            def body(t, k, u):
                if has(t + 1):
                    tr(t + 1, (u + 1) % U)
                mm(t, u)

            tr(0, 0)
            tiles(pe, body)

        @blk.scalar
        def _(act):
            act.nop().then_inc(sem("o_filled"), 2)

            def body(t, k, u):
                act.wait_ge(sem("t_filled"), t + 1)
                act.wait_ge(sem("o_filled"), t + 1)
                nc.scalar.activation(x2T[0][:, u % 2, :, :], tbank[u % 2][:, :].rearrange("p (k n) -> p k n", k=KT),
                                     ACT.Copy).then_inc(sem("t_hi"), 1)

            tiles(act, body)

        @blk.vector
        def _(dve):
            dve.nop().then_inc(sem("t_used"), 2)
            dve.nop().then_inc(sem("res_ready"), 2)

            def norm(t, loads, u):
                dve.wait_ge(sem(f"row_in{u}"), 16 * loads)
                nc.vector.tensor_scalar(xn2[:, u, :], row[:, u, 0:DM], row[:, u, C_RSTD:C_RSTD + 1],
                                        row[:, u, C_NMR:C_NMR + 1], ALU.mult, ALU.add).then_inc(sem("xn2_ready"), 1)

            def lo(t, u):
                dve.wait_ge(sem("t_hi"), t + 1)
                nc.vector.tensor_tensor(x2T[1][:, u % 2, :, :], tbank[u % 2][:, :].rearrange("p (k n) -> p k n", k=KT),
                                        x2T[0][:, u % 2, :, :], ALU.subtract).then_inc(sem("t_used"), 1)

            def body(t, k, u):
                if has(t + 2):
                    norm(t + 2, k + (u + 2) // U + 1, (u + 2) % U)
                if has(t + 1):
                    lo(t + 1, (u + 1) % U)
                dve.wait_ge(sem("o_filled"), t + 1 + 2)
                dve.wait_ge(sem("sum_ready"), t + 1)
                nc.vector.scalar_tensor_tensor(out=res[:, u, :], in0=obank2[u % 2][:, :], scalar=inv[:, S_E:S_E + 1],
                                               in1=row[:, u, 0:DM], op0=ALU.mult, op1=ALU.add)\
                    .then_inc(sem("res_ready"), 1)

            norm(0, 1, 0)
            norm(1, 1, 1)
            lo(0, 0)
            tiles(dve, body)
    es.close()


_INS = ['x', 'ctx_512', 'L0_xattn_Wq', 'L0_xattn_bq', 'L0_xattn_Wk', 'L0_xattn_bk', 'L0_xattn_Wv', 'L0_xattn_bv',
        'L0_xattn_Wo', 'L0_xattn_bo', 'L0_ffn_gate_w', 'L0_ffn_expert_w']


def kernel(**inputs):
    import numpy as _np
    import concourse.bacc as _bacc
    from concourse.bass_utils import run_bass_kernel_spmd as _run

    nc = _bacc.Bacc("TRN2", target_bir_lowering=False, num_devices=1)
    arrays, args = {}, []
    for name in _INS:
        a = _np.ascontiguousarray(inputs[name])
        arrays[f"in_{name}"] = a
        args.append(nc.dram_tensor(f"in_{name}", a.shape, mybir.dt.from_np(a.dtype), kind="ExternalInput").ap())
    args.append(nc.dram_tensor("out_0", (B, LQ, DM), F32, kind="ExternalOutput").ap())
    build(nc, *args)
    r = _run(nc, [arrays], core_ids=[0])
    return _np.asarray(r.results[0]["out_0"])
```
